# Optimizing a Trainium2 kernel written in Bass

```python
import numpy as np
import jax
import jax.numpy as jnp

def _softmax(x, axis=-1):
    return jax.nn.softmax(x, axis=axis)

def _gelu(x):
    return jax.nn.gelu(x, approximate=True)

def _silu(x):
    return jax.nn.silu(x)

def _sigmoid(x):
    return jax.nn.sigmoid(x)

def _layernorm(x, axis=-1, eps=1e-05):
    m = jnp.mean(x, axis=axis, keepdims=True)
    v = jnp.var(x, axis=axis, keepdims=True)
    return (x - m) / jnp.sqrt(v + eps)

def _scatter_add(tgt, idx, src, axis=0):
    return tgt.at[idx].add(src)

def _segment_sum(src, seg, n):
    return jax.ops.segment_sum(src, seg, n)
kernel_name = 'mk_decoder_preln_d1_seqx_r4_2e1123'

def setup_inputs(seed: int=0):
    np.random.seed(seed)
    _w = jnp.asarray

    def _rec_inputs():
        import jax
        import jax.numpy as jnp
        _rk = jax.random.key(seed)
        x = 7.22e-05 + 1 * jax.random.normal(jax.random.fold_in(_rk, 1), (32, 112, 256), jnp.float32)
        _lenS = 112 - jax.random.randint(jax.random.fold_in(_rk, 7), (32,), 0, max(1, 112 // 4) + 1, jnp.int32)
        _lenS2 = 375 - jax.random.randint(jax.random.fold_in(_rk, 8), (32,), 0, max(1, 375 // 4) + 1, jnp.int32)
        _ctx_1024P = jax.random.normal(jax.random.fold_in(_rk, 11), (32, 16, 256), jnp.float32)
        _ctx_1024c = jax.random.dirichlet(jax.random.fold_in(_rk, 511), 0.3 * jnp.ones((16,), jnp.float32), (32, 375))
        _ctx_1024t = jnp.einsum('bsk,bkd->bsd', _ctx_1024c, _ctx_1024P)
        _ctx_1024t = _ctx_1024t * jax.lax.rsqrt(jnp.mean(jnp.square(_ctx_1024t)) + 1e-12) * 0.953939
        ctx_1024 = 4.13588e-05 + 0.999923 * (_ctx_1024t + 0.3 * jax.random.normal(jax.random.fold_in(_rk, 611), (32, 375, 256), jnp.float32))
        _validS = jnp.arange(112)[None, :] < _lenS[:, None]
        _validS2 = jnp.arange(375)[None, :] < _lenS2[:, None]
        _causal = jnp.tril(jnp.ones((112, 112), dtype=bool))
        mask_BxSxS2_ik1 = jnp.where(jnp.broadcast_to(_validS2[:, None, :], (32, 112, 375)), 1, 0).astype(jnp.int32)
        return (x, ctx_1024, mask_BxSxS2_ik1)
    x, ctx_1024, mask_BxSxS2_ik1 = _rec_inputs()

    def _L0_attn_setup():
        import jax, jax.numpy as jnp
        import numpy as np
        B, T, D = (4, 512, 256)
        HID = 2 * D
        EPS = 1e-06

        def _rmsnorm(x, w):
            return x * jax.lax.rsqrt(jnp.mean(x * x, axis=-1, keepdims=True) + EPS) * w

        def _ema_scan(v, alpha):

            def step(prev, v_t):
                cur = alpha * v_t + (1.0 - alpha) * prev
                return (cur, cur)
            v_tm = jnp.swapaxes(v, 0, 1)
            _, out = jax.lax.scan(step, jnp.zeros(v.shape[::2], v.dtype), v_tm)
            return jnp.swapaxes(out, 0, 1)

        def _delta_scan(q, k, v, beta):

            def step(S, inp):
                q_t, k_t, v_t, b_t = inp
                Sk = jnp.einsum('bij,bj->bi', S, k_t)
                S = S + b_t[:, None, None] * (v_t - Sk)[:, :, None] * k_t[:, None, :]
                o_t = jnp.einsum('bij,bj->bi', S, q_t)
                return (S, o_t)
            tm = lambda a: jnp.swapaxes(a, 0, 1)
            S0 = jnp.zeros((q.shape[0], q.shape[2], q.shape[2]), q.dtype)
            _, out = jax.lax.scan(step, S0, (tm(q), tm(k), tm(v), tm(beta)))
            return jnp.swapaxes(out, 0, 1)
        key = jax.random.key(seed)
        ks = jax.random.split(key, 12)
        s = 0.02
        return {'x': jax.random.normal(ks[0], (B, T, D), jnp.float32), 'norm1_w': jnp.ones((D,), jnp.float32), 'Wq': jax.random.normal(ks[1], (D, D), jnp.float32) * s, 'Wk': jax.random.normal(ks[2], (D, D), jnp.float32) * s, 'Wv': jax.random.normal(ks[3], (D, D), jnp.float32) * s, 'beta_w': jax.random.normal(ks[4], (D, 1), jnp.float32) * s, 'beta_b': jnp.zeros((1,), jnp.float32), 'Wo': jax.random.normal(ks[5], (D, D), jnp.float32) * s, 'alpha_logit': jnp.full((D,), float(np.log(0.1 / 0.9)), jnp.float32), 'norm2_w': jnp.ones((D,), jnp.float32), 'w_gate': jax.random.normal(ks[6], (D, HID), jnp.float32) * s, 'w_up': jax.random.normal(ks[7], (D, HID), jnp.float32) * s, 'w_down': jax.random.normal(ks[8], (HID, D), jnp.float32) * s}
    _L0_attn_all = _L0_attn_setup()
    _L0_attn_in = {k: v for k, v in _L0_attn_all.items() if k in ('norm1_w', 'Wq', 'Wk', 'Wv', 'beta_w', 'beta_b', 'Wo', 'alpha_logit', 'norm2_w', 'w_gate', 'w_up', 'w_down')}
    del _L0_attn_all

    def _L0_xattn_setup():
        import jax, jax.numpy as jnp
        import numpy as np
        N_HEADS = 16
        D_MODEL = 256
        HEAD_D = D_MODEL // N_HEADS
        key = jax.random.key(seed)
        ks = jax.random.split(key, 8)
        B, S, D = (4, 512, D_MODEL)
        scale = 1.0 / np.sqrt(D)
        return {'query': jax.random.normal(ks[0], (B, S, D), jnp.float32), 'key': jax.random.normal(ks[1], (B, S, D), jnp.float32), 'value': jax.random.normal(ks[2], (B, S, D), jnp.float32), 'mask': jax.random.randint(ks[3], (B, S, S), 0, 2, jnp.int32), 'wq': jax.random.normal(ks[4], (D, D), jnp.float32) * scale, 'wk': jax.random.normal(ks[5], (D, D), jnp.float32) * scale, 'wv': jax.random.normal(ks[6], (D, D), jnp.float32) * scale, 'w_out': jax.random.normal(ks[7], (D, D), jnp.float32) * scale}
    _L0_xattn_all = _L0_xattn_setup()
    _L0_xattn_in = {k: v for k, v in _L0_xattn_all.items() if k in ('wq', 'wk', 'wv', 'w_out')}
    del _L0_xattn_all

    def _L0_ffn_setup():
        import jax, jax.numpy as jnp
        import numpy as np
        DIM = 256
        MOE_INTER = 256
        SHARED_INTER = 256
        N_EXPERTS = 6
        TOP_K = 2
        ROUTE_SCALE = 1.0
        B, S = (8, 1024)
        STD = 0.02 / np.sqrt(DIM)
        STD_I = 0.02 / np.sqrt(MOE_INTER)
        key = jax.random.key(seed)
        ks = jax.random.split(key, 10)
        inp = {'x': jax.random.normal(ks[0], (B, S, DIM), dtype=jnp.float32), 'gate_w': jax.random.normal(ks[1], (N_EXPERTS, DIM), dtype=jnp.float32) * STD, 'gate_b': jnp.zeros((N_EXPERTS,), dtype=jnp.float32), 'ew1': jax.random.normal(ks[2], (N_EXPERTS, MOE_INTER, DIM), dtype=jnp.float32) * STD, 'ew2': jax.random.normal(ks[3], (N_EXPERTS, DIM, MOE_INTER), dtype=jnp.float32) * STD_I, 'ew3': jax.random.normal(ks[4], (N_EXPERTS, MOE_INTER, DIM), dtype=jnp.float32) * STD, 'fc1': jax.random.normal(ks[5], (SHARED_INTER, DIM), dtype=jnp.float32) * STD, 'fc2': jax.random.normal(ks[6], (SHARED_INTER, DIM), dtype=jnp.float32) * STD, 'fc3': jax.random.normal(ks[7], (DIM, SHARED_INTER), dtype=jnp.float32) * STD_I}
        return inp
    _L0_ffn_all = _L0_ffn_setup()
    _L0_ffn_in = {k: v for k, v in _L0_ffn_all.items() if k in ('gate_w', 'gate_b', 'ew1', 'ew2', 'ew3', 'fc1', 'fc2', 'fc3')}
    del _L0_ffn_all
    return {'x': x, 'ctx_1024': ctx_1024, 'mask_BxSxS2_ik1': mask_BxSxS2_ik1, 'L0_attn_norm1_w': _L0_attn_in['norm1_w'], 'L0_attn_Wq': _L0_attn_in['Wq'], 'L0_attn_Wk': _L0_attn_in['Wk'], 'L0_attn_Wv': _L0_attn_in['Wv'], 'L0_attn_beta_w': _L0_attn_in['beta_w'], 'L0_attn_beta_b': _L0_attn_in['beta_b'], 'L0_attn_Wo': _L0_attn_in['Wo'], 'L0_attn_alpha_logit': _L0_attn_in['alpha_logit'], 'L0_attn_norm2_w': _L0_attn_in['norm2_w'], 'L0_attn_w_gate': _L0_attn_in['w_gate'], 'L0_attn_w_up': _L0_attn_in['w_up'], 'L0_attn_w_down': _L0_attn_in['w_down'], 'L0_xattn_wq': _L0_xattn_in['wq'], 'L0_xattn_wk': _L0_xattn_in['wk'], 'L0_xattn_wv': _L0_xattn_in['wv'], 'L0_xattn_w_out': _L0_xattn_in['w_out'], 'L0_ffn_gate_w': _L0_ffn_in['gate_w'], 'L0_ffn_gate_b': _L0_ffn_in['gate_b'], 'L0_ffn_ew1': _L0_ffn_in['ew1'], 'L0_ffn_ew2': _L0_ffn_in['ew2'], 'L0_ffn_ew3': _L0_ffn_in['ew3'], 'L0_ffn_fc1': _L0_ffn_in['fc1'], 'L0_ffn_fc2': _L0_ffn_in['fc2'], 'L0_ffn_fc3': _L0_ffn_in['fc3']}

def reference(x, ctx_1024, mask_BxSxS2_ik1, L0_attn_norm1_w, L0_attn_Wq, L0_attn_Wk, L0_attn_Wv, L0_attn_beta_w, L0_attn_beta_b, L0_attn_Wo, L0_attn_alpha_logit, L0_attn_norm2_w, L0_attn_w_gate, L0_attn_w_up, L0_attn_w_down, L0_xattn_wq, L0_xattn_wk, L0_xattn_wv, L0_xattn_w_out, L0_ffn_gate_w, L0_ffn_gate_b, L0_ffn_ew1, L0_ffn_ew2, L0_ffn_ew3, L0_ffn_fc1, L0_ffn_fc2, L0_ffn_fc3):
    import jax
    import jax.numpy as jnp

    def _L0_attn_ref(x, norm1_w, Wq, Wk, Wv, beta_w, beta_b, Wo, alpha_logit, norm2_w, w_gate, w_up, w_down):
        import jax, jax.numpy as jnp
        import numpy as np
        B, T, D = (4, 512, 256)
        HID = 2 * D
        EPS = 1e-06

        def _rmsnorm(x, w):
            return x * jax.lax.rsqrt(jnp.mean(x * x, axis=-1, keepdims=True) + EPS) * w

        def _ema_scan(v, alpha):

            def step(prev, v_t):
                cur = alpha * v_t + (1.0 - alpha) * prev
                return (cur, cur)
            v_tm = jnp.swapaxes(v, 0, 1)
            _, out = jax.lax.scan(step, jnp.zeros(v.shape[::2], v.dtype), v_tm)
            return jnp.swapaxes(out, 0, 1)

        def _delta_scan(q, k, v, beta):

            def step(S, inp):
                q_t, k_t, v_t, b_t = inp
                Sk = jnp.einsum('bij,bj->bi', S, k_t)
                S = S + b_t[:, None, None] * (v_t - Sk)[:, :, None] * k_t[:, None, :]
                o_t = jnp.einsum('bij,bj->bi', S, q_t)
                return (S, o_t)
            tm = lambda a: jnp.swapaxes(a, 0, 1)
            S0 = jnp.zeros((q.shape[0], q.shape[2], q.shape[2]), q.dtype)
            _, out = jax.lax.scan(step, S0, (tm(q), tm(k), tm(v), tm(beta)))
            return jnp.swapaxes(out, 0, 1)
        h = _rmsnorm(x, norm1_w)
        q = h @ Wq
        k = h @ Wk
        k = k / jnp.maximum(jnp.linalg.norm(k, axis=-1, keepdims=True), 1e-12)
        v = h @ Wv
        v = _ema_scan(v, jax.nn.sigmoid(alpha_logit))
        beta = jax.nn.sigmoid(h @ beta_w + beta_b)[..., 0]
        attn_out = _delta_scan(q, k, v, beta)
        x = x + attn_out @ Wo
        h2 = _rmsnorm(x, norm2_w)
        mlp = jax.nn.silu(h2 @ w_gate) * (h2 @ w_up) @ w_down
        return x + mlp

    def _L0_xattn_ref(query, key, value, mask, wq, wk, wv, w_out):
        import jax, jax.numpy as jnp
        import numpy as np
        N_HEADS = 16
        D_MODEL = 256
        HEAD_D = D_MODEL // N_HEADS
        B, Sq, D = query.shape
        H, hd = (N_HEADS, HEAD_D)

        def split(x):
            return x.reshape(B, -1, H, hd).transpose(0, 2, 1, 3)
        Q = split(jnp.einsum('bsd,ed->bse', query, wq))
        K = split(jnp.einsum('bsd,ed->bse', key, wk))
        V = split(jnp.einsum('bsd,ed->bse', value, wv))
        scores = jnp.einsum('bhqd,bhkd->bhqk', Q, K) / np.sqrt(hd)
        scores = jnp.where(mask[:, None, :, :] == 1, jnp.float32(-1000000000.0), scores)
        attn = jax.nn.softmax(scores, axis=-1)
        out = jnp.einsum('bhqk,bhkd->bhqd', attn, V)
        out = out.transpose(0, 2, 1, 3).reshape(B, Sq, D)
        return jnp.einsum('bsd,ed->bse', out, w_out)

    def _L0_ffn_ref(x, gate_w, gate_b, ew1, ew2, ew3, fc1, fc2, fc3):
        import jax, jax.numpy as jnp
        import numpy as np
        DIM = 256
        MOE_INTER = 256
        SHARED_INTER = 256
        N_EXPERTS = 6
        TOP_K = 2
        ROUTE_SCALE = 1.0
        B, S = (8, 1024)
        STD = 0.02 / np.sqrt(DIM)
        STD_I = 0.02 / np.sqrt(MOE_INTER)
        orig_shape = x.shape
        xt = x.reshape(-1, DIM)
        logits = xt @ gate_w.T + gate_b
        probs = jax.nn.sigmoid(logits)
        w, idx = jax.lax.top_k(probs, TOP_K)
        w = w / (jnp.sum(w, axis=-1, keepdims=True) + 1e-08)
        w = w * ROUTE_SCALE
        ge = jnp.sum(jax.nn.one_hot(idx, N_EXPERTS, dtype=w.dtype) * w[..., None], axis=1)
        y = jnp.zeros_like(xt)
        for e in range(N_EXPERTS):
            h = jax.nn.silu(xt @ ew1[e].T) * (xt @ ew3[e].T)
            y = y + ge[:, e:e + 1] * (h @ ew2[e].T)
        z = jax.nn.silu(xt @ fc1.T) * (xt @ fc2.T) @ fc3.T
        return (y + z).reshape(orig_shape)
    x = x + _L0_attn_ref(_layernorm(x, axis=-1), L0_attn_norm1_w, L0_attn_Wq, L0_attn_Wk, L0_attn_Wv, L0_attn_beta_w, L0_attn_beta_b, L0_attn_Wo, L0_attn_alpha_logit, L0_attn_norm2_w, L0_attn_w_gate, L0_attn_w_up, L0_attn_w_down)
    x = x + _L0_xattn_ref(_layernorm(x, axis=-1), ctx_1024, ctx_1024, mask_BxSxS2_ik1, L0_xattn_wq, L0_xattn_wk, L0_xattn_wv, L0_xattn_w_out)
    x = x + _L0_ffn_ref(_layernorm(x, axis=-1), L0_ffn_gate_w, L0_ffn_gate_b, L0_ffn_ew1, L0_ffn_ew2, L0_ffn_ew3, L0_ffn_fc1, L0_ffn_fc2, L0_ffn_fc3)
    return x

_drawn_inputs = setup_inputs


def setup_inputs(seed=0):
    import zlib

    import numpy as np

    out = dict(_drawn_inputs(seed))
    spreads = {'L0_attn_norm1_w': (1.0, 0.6),
     'L0_attn_alpha_logit': (-2.1972246170043945, 0.6),
     'L0_attn_norm2_w': (1.0, 0.6),
     'L0_ffn_gate_b': (0.0, 2.0)}
    factors = {'L0_attn_Wq': 4.162,
     'L0_attn_Wk': 4.144,
     'L0_attn_Wv': 4.146,
     'L0_attn_beta_w': 8.0,
     'L0_attn_Wo': 4.136,
     'L0_attn_w_gate': 4.294,
     'L0_attn_w_up': 4.248,
     'L0_attn_w_down': 4.251,
     'L0_ffn_gate_w': 64.0,
     'L0_ffn_ew1': 64.0,
     'L0_ffn_ew2': 64.0,
     'L0_ffn_ew3': 64.0,
     'L0_ffn_fc1': 64.0,
     'L0_ffn_fc2': 64.0,
     'L0_ffn_fc3': 64.0}
    for name, (base, spread) in spreads.items():
        noise = np.random.default_rng([zlib.crc32(name.encode()), seed]).standard_normal(out[name].shape)
        drawn = base * np.exp(spread * noise) if base else spread * noise
        out[name] = jnp.asarray(drawn.astype(out[name].dtype))
    for name, factor in factors.items():
        out[name] = (out[name] * factor).astype(out[name].dtype)
    return out
```

```python
from contextlib import ExitStack

import numpy as np

import concourse.bass as bass
from concourse import mybir

ALU = mybir.AluOpType
ACT = mybir.ActivationFunctionType
F32 = mybir.dt.float32
F32R = mybir.dt.float32r
BF16 = mybir.dt.bfloat16
I32 = mybir.dt.int32
AX = mybir.AxisListType.X

P = 128
B, T, D = 32, 112, 256
S2 = 375
HEADS, HD = 16, 16
FF = 512
NE, EW = 6, 256
GB = 4
G = B // GB
GT = GB * T
DC = D // P
FC = FF // P
KC = 3
KP = S2 // KC
S2E = S2 + 1
LEVELS = (2, 4, 8, 16, 32, 64)
BIG = float(2 ** 40)
ROWS = 3 * HD
HPB = 4
LN_EPS, RMS_EPS = 1e-5, 1e-6

M_SLNEG, M_SUNEG, M_LE, M_B1, M_BT = 0, 1, 2, 3, 4
N_MASKS = 5 + len(LEVELS)


def shape_constants():
    t = np.arange(T)
    row, col = t[:, None], t[None, :]
    masks = np.zeros((T, N_MASKS, T), np.float32)
    masks[:, M_SLNEG] = np.where(col < row, -1.0, 0.0)
    masks[:, M_SUNEG] = np.where(col > row, -1.0, 0.0)
    masks[:, M_LE] = row <= col
    for n, b in enumerate((1,) + LEVELS):
        quarter = (row // (2 * b) == col // (2 * b)) & (row % (2 * b) >= b) & (col % (2 * b) < b)
        if b == 1:
            masks[:, M_B1] = quarter
        masks[:, M_BT + n] = quarter.T
    keep = np.ones((P, GT), np.float32)
    keep[:, ::T] = 0.0
    return {"masks": masks, "ident": np.eye(P, dtype=np.float32), "keep": keep}


def decoder_layer(nc, io, out):
    with ExitStack() as ctx:
        def sb_in(scope):
            return lambda name, shape, dt=F32: scope.enter_context(nc.sbuf_tensor(name, shape, dt))

        def sem(name):
            return ctx.enter_context(nc.semaphore(name))

        sb = sb_in(ctx)
        bank = [ctx.enter_context(nc.psum_tensor(f"bank{i}", [P, 512], F32)) for i in range(8)]

        x = sb("x_res", [T, B, D])
        ident = sb("ident_sb", [P, P])
        pcol = sb("pcol", [P, 4, DC])
        alpha = sb("alpha", [P, 2, DC])
        betab = sb("betab", [T, 2])
        gateb = sb("gateb", [T, NE])
        half = sb("neg_half", [T, 2, GB])
        xwq = sb("xwq_sb", [P, DC, D])
        xwk = sb("xwk_sb", [P, DC, D])
        xwv = sb("xwv_sb", [P, DC, D])
        xwo = sb("xwo_sb", [P, DC, D])
        router = sb("router_sb", [P, DC, NE])
        e1 = sb("e1_sb", [P, NE + 1, DC, EW])
        e3 = sb("e3_sb", [P, NE + 1, DC, EW])
        e2 = sb("e2_sb", [P, NE + 1, DC, D])
        stats = sb("stats", [T, GB, 6])
        mv = sb("mv", [T, GB, 2])
        rs = sb("rs", [T, 2, GB])
        small = sb("small", [T, 6, GB])

        with ExitStack() as scope:
            w1 = sb_in(scope)
            masks = w1("masks_sb", [T, N_MASKS, T])
            keep = w1("keep_sb", [P, GT])
            decay = w1("decay", [P, DC, GT])
            wq = w1("wq_sb", [P, DC, D])
            wk = w1("wk_sb", [P, DC, D])
            wv = w1("wv_sb", [P, DC, D])
            wbeta = w1("wbeta_sb", [P, DC])
            wo = w1("wo_sb", [P, DC, D])
            wgate = w1("wgate_sb", [P, DC, FF])
            wup = w1("wup_sb", [P, DC, FF])
            wdown = w1("wdown_sb", [P, FC, D])
            xn = w1("xn", [T, GB, D])
            h = w1("h", [T, GB, D])
            hT = w1("hT", [P, DC, GT])
            qT = w1("qT", [P, DC, GT])
            va = w1("va", [P, DC, GT])
            vs = w1("vs", [P, DC, GT])
            kt = w1("kt", [T, GB, D])
            kT = w1("kT", [P, DC, GT])
            vt = w1("vt", [T, GB, D])
            neg = w1("neg", [T, GB, T])
            negT = w1("negT", [T, GB, T])
            cT = w1("cT", [T, len(LEVELS), GB, T])
            tri = w1("tri", [T, GB, T])
            triT = w1("triT", [T, GB, T])
            xq = w1("xq", [T, GB, T])
            aT = w1("aT", [T, GB, T])
            y = w1("y", [T, GB, D])
            oT = w1("oT", [P, DC, GT])
            x1 = w1("x1", [T, GB, D])
            sq = w1("sq", [T, D])
            sg = w1("sg", [P, 2, GT])
            hid = w1("hid", [P, FC, GT])
        with ExitStack() as scope:
            w2 = sb_in(scope)
            ctxT = w2("ctxT", [P, 2, DC, S2])
            maskq = w2("maskq", [T, 2, S2], I32)
            maskk = w2("maskk", [KP, 2, KC, T], I32)
            biasq = w2("biasq", [T, 2, S2])
            flagk = w2("flagk", [KP, 2, KC, T], BF16)
            negbig = w2("negbig", [KP, KP], BF16)
            h2 = w2("h2", [T, D])
            h2T = w2("h2T", [P, DC, T])
            qhi = w2("qhi", [P, DC, T], F32R)
            qlo = w2("qlo", [P, DC, T], F32R)
            khi = w2("khi", [P, DC, S2], F32R)
            klo = w2("klo", [P, DC, S2], F32R)
            qst = [w2(f"qst{i}", [ROWS + 1, HEADS, T], F32R) for i in range(2)]
            kst = [w2(f"kst{i}", [ROWS + 1, HEADS, S2E], F32R) for i in range(2)]
            vaug = [w2(f"vaug{i}", [KP, KC, HEADS, 2 * HD]) for i in range(2)]
            smax = w2("smax", [T, HEADS])
            junk = w2("junk", [T, 2, S2])
            negm = w2("negm", [HEADS, T], F32R)
            pr = [w2(f"pr{i}", [KP, 2 * HPB, T]) for i in range(2)]
            pv = w2("pv", [P, HPB * T])
            rden = w2("rden", [T, HEADS, 1])
            on = w2("on", [T, HEADS, HD])
            onT = w2("onT", [P, DC, T])
        with ExitStack() as scope:
            w3 = sb_in(scope)
            h3 = w3("h3", [T, GB, D])
            h3T = w3("h3T", [P, DC, GT])
            logit = w3("logit", [T, GB, NE])
            prob = w3("prob", [T, GB, NE])
            cmp1 = w3("cmp1", [T, GB, NE, NE])
            rank = w3("rank", [T, GB, NE])
            wsum = w3("wsum", [T, GB, 1])
            gate = w3("gate", [T, GB, NE])
            sg3 = w3("sg3", [P, 2, GT])
            hid3 = w3("hid3", [P, 2, DC, GT])

        apart = {nc.gpsimd.engine: sem("pool_waited"), nc.vector.engine: sem("dve_waited")}
        names = """x_in w_in1 w_in2 w_in3 c_in setup_pool setup_dve setup_act alpha_t alpha_d
            stat1 var1 rs1 xn1 h1 ht_ps1 ht_act1 ht_dve1 q_ps k_ps v_ps q_sb va_sb v_scan tanh_b ksq kscale_a kscale_b kscale_c kscale
            kt_sb kT_ps vt_ps kT_sb vt_sb gram_ps aq_ps negs cmask tri0a tri0 aT_sb
            xps xsb tps_t tps_tt tri_up triT_up y_ps y_sb oT_ps oT_a oT_d wo_ps x1_sb x1_sq rms_a rms x_plus h2_sb h2t_ps h2t_a h2t_d
            g_ps u_ps silu hid_sb down_ps x_mlp""".split()
        s = {n: sem(n) for n in names}
        s2 = {n: sem("c_" + n) for n in """ctx0 ctx1 ready flags stat rs h hT_ps hT_sb q_ps q_hi q_lo k_ps k_hi k_lo v_ps v_sb qst0 qst1 kst0 kst1
            max_ps smax mt_ps negm negm_in sc_ps exp pv_done pv_ps pv_sb ot_ps rden on onT_ps onT_sb wo_ps x_new""".split()}
        s3 = {n: sem("e_" + n) for n in """stat rs h ht_ps ht_a ht_d lg_ps logit ex den prob cmp rank sel wsum gate g_ps u_ps silu hid d_ps x_new x_out""".split()}
        block = ctx.enter_context(nc.Block())

        def cols(j, width=T):
            return slice(j * width, (j + 1) * width)

        def over_rows(mask):
            return masks[:, mask, :].unsqueeze(1).broadcast_to([T, GB, T])

        def wait_apart(eng, semaphore, value):
            eng.wait_ge(semaphore, value)
            eng.sem_inc(apart[eng.engine], 1)

        def loaded(pair):
            return pair * 48 + 48

        def stacked(pair):
            return pair * 96 + 96

        @block.sync
        def _(sp):
            for g in range(G):
                sp.dma_start(x[:, g * GB:(g + 1) * GB, :], io["x"][g * GB:(g + 1) * GB].rearrange("b t d -> t b d")).then_inc(s["x_in"], 16)
            for tile, name in ((wq, "L0_attn_Wq"), (wk, "L0_attn_Wk"), (wv, "L0_attn_Wv"), (wo, "L0_attn_Wo"),
                               (wgate, "L0_attn_w_gate"), (wup, "L0_attn_w_up"), (wdown, "L0_attn_w_down")):
                sp.dma_start(tile[:], io[name].rearrange("(c p) n -> p c n", p=P)).then_inc(s["w_in1"], 16)
            sp.dma_start(wbeta[:], io["L0_attn_beta_w"]).then_inc(s["w_in1"], 16)
            for tile, name in ((xwq, "xwq"), (xwk, "xwk"), (xwv, "xwv"), (xwo, "xwo")):
                sp.dma_start(tile[:], io[name].rearrange("(c p) n -> p c n", p=P)).then_inc(s["w_in2"], 16)
            for tile, name in ((e1, "e1"), (e3, "e3"), (e2, "e2")):
                for e in range(NE + 1):
                    sp.dma_start(tile[:, e], io[name][e].rearrange("(c p) n -> p c n", p=P)).then_inc(s["w_in3"], 16)
            sp.dma_start(router[:], io["router"].rearrange("(c p) n -> p c n", p=P)).then_inc(s["w_in3"], 16)
            sp.wait_ge(s["x_mlp"], G)

            def load_context(pair, par):
                b = pair * 2 + par
                ready = s2["ctx0"] if par == 0 else s2["ctx1"]
                sp.dma_start(ctxT[:, par], io["ctxT"][bass.ds(b, 1)].rearrange("a (c p) k -> p (a c) k", p=P)).then_inc(ready, 16)
                sp.dma_start(maskq[:, par, :], io["mask"][bass.ds(b, 1)].rearrange("a q k -> (a q) k")).then_inc(ready, 16)
                sp.dma_start(maskk[:, par], io["maskT"][bass.ds(b, 1)].rearrange("a (c p) q -> p (a c) q", p=KP)).then_inc(ready, 16)

            def spread_heads(pair, par):
                b = pair * 2 + par
                for tile, src, r, ready, done, n in ((qst, qhi, 0, "q_hi", "qst", T), (qst, qhi, 1, "q_hi", "qst", T), (qst, qlo, 2, "q_lo", "qst", T),
                                                  (kst, khi, 0, "k_hi", "kst", S2), (kst, klo, 1, "k_lo", "kst", S2), (kst, khi, 2, "k_hi", "kst", S2)):
                    sp.wait_ge(s2[ready], b + 1)
                    for m in range(DC):
                        dst = tile[par][r * HD:(r + 1) * HD, cols(m, HEADS // DC), 0:n]
                        sp.dma_start(dst.bitcast(F32), src[:, m].bitcast(F32)).then_inc(s2[f"{done}{par}"], 16)

            def spread_max(pair, par):
                b = pair * 2 + par
                sp.wait_ge(s2["negm"], b + 1)
                sp.dma_start(qst[par][ROWS:ROWS + 1].bitcast(F32), negm[:].bitcast(F32)).then_inc(s2["negm_in"], 16)

            load_context(0, 0)
            load_context(0, 1)
            sp.wait_ge(s2["ready"], 1)
            spread_heads(0, 0)
            with sp.Fori(0, B // 2 - 1) as pair:
                b = pair * 2
                for par in range(2):
                    spread_max(pair, par)
                    spread_heads(pair + par, 1 - par)
                    sp.wait_ge(s2["v_ps"], b + par + 1)
                    sp.wait_ge(s2["flags"], b + par + 1)
                    load_context(pair + 1, par)
            spread_max(B // 2 - 1, 0)
            spread_heads(B // 2 - 1, 1)
            spread_max(B // 2 - 1, 1)

            with sp.Fori(0, G) as g:
                sp.wait_ge(s3["x_new"], (g + 1) * (NE + 1))
                sp.dma_start(out[bass.ds(g * GB, GB)].rearrange("b t d -> t b d"), x[:, bass.ds(g * GB, GB), :]).then_inc(s3["x_out"], 16)
            sp.wait_ge(s3["x_out"], 16 * G)

        @block.gpsimd
        def _(pool):
            pool.dma_start(ident[:], io["ident"]).then_inc(s["c_in"], 16)
            pool.dma_start(masks[:], io["masks"]).then_inc(s["c_in"], 16)
            pool.dma_start(keep[:], io["keep"]).then_inc(s["c_in"], 16)
            for n, name in enumerate(("L0_attn_norm1_w", "L0_attn_norm2_w", "L0_attn_alpha_logit")):
                pool.dma_start(pcol[:, n, :], io[name]).then_inc(s["c_in"], 16)
            pool.dma_start(betab[:, 0:1], io["L0_attn_beta_b"].partition_broadcast(T)).then_inc(s["c_in"], 16)
            pool.dma_start(gateb[:], io["L0_ffn_gate_b"].partition_broadcast(T)).then_inc(s["c_in"], 16)
            nc.gpsimd.memset(half[:, 0, :], -0.5)
            nc.gpsimd.memset(half[:, 1, :], 0.5).then_inc(s["setup_pool"], 1)
            pool.wait_ge(s["setup_pool"], 1)

            with pool.Fori(0, G) as g:
                pool.wait_ge(s["var1"], g + 1)
                nc.gpsimd.tensor_tensor(rs[:], rs[:], half[:, 0:1, :].broadcast_to([T, 2, GB]), op=ALU.pow).then_inc(s["rs1"], 1)
                wait_apart(pool, s["tanh_b"], g + 1)
                nc.gpsimd.tensor_scalar(small[:, 0], small[:, 0], 0.5, 0.5, ALU.mult, ALU.add).then_inc(s["kscale_a"], 1)
                pool.wait_ge(s["kscale_a"], g + 1)
                nc.gpsimd.tensor_tensor(small[:, 1], small[:, 0], half[:, 1, :], op=ALU.pow)
                wait_apart(pool, s["ksq"], g + 1)
                nc.gpsimd.tensor_scalar(small[:, 2], small[:, 2], 1e-24, None, ALU.max).then_inc(s["kscale_b"], 1)
                pool.wait_ge(s["kscale_b"], g + 1)
                nc.gpsimd.tensor_tensor(small[:, 3], small[:, 2], half[:, 0, :], op=ALU.pow).then_inc(s["kscale_c"], 1)
                pool.wait_ge(s["kscale_c"], g + 1)
                nc.gpsimd.tensor_tensor(small[:, 4], small[:, 3], small[:, 1], op=ALU.mult).then_inc(s["kscale"], 1)
                pool.wait_ge(s["negs"], g + 1)
                for n in range(len(LEVELS)):
                    nc.gpsimd.tensor_tensor(cT[:, n], negT[:], over_rows(M_BT + 1 + n), op=ALU.mult).then_inc(s["cmask"], 1)
                wait_apart(pool, s["x1_sq"], g + 1)
                nc.gpsimd.tensor_scalar(small[:, 5], small[:, 5], 1.0 / D, RMS_EPS, ALU.mult, ALU.add).then_inc(s["rms_a"], 1)
                pool.wait_ge(s["rms_a"], g + 1)
                nc.gpsimd.tensor_tensor(small[:, 5], small[:, 5], half[:, 0, :], op=ALU.pow).then_inc(s["rms"], 1)
                nc.gpsimd.tensor_tensor(x[:, bass.ds(g * GB, GB), :], x[:, bass.ds(g * GB, GB), :], x1[:], op=ALU.add).then_inc(s["x_plus"], 1)

            pool.wait_ge(s["x_mlp"], G)
            for i in range(2):
                nc.gpsimd.memset(kst[i][:].bitcast(F32), 1.0)
                nc.gpsimd.memset(vaug[i][:], 1.0)
            nc.gpsimd.tensor_scalar(negbig[:], ident[0:KP, 0:KP], -BIG, None, ALU.mult).then_inc(s2["ready"], 1)

            def mask_bias(pair, par):
                b = pair * 2 + par
                ready = s2["ctx0"] if par == 0 else s2["ctx1"]
                wait_apart(pool, ready, loaded(pair))
                nc.gpsimd.tensor_scalar(biasq[:, par, :], maskq[:, par, :], 1.0, -BIG, ALU.is_equal, ALU.mult)
                nc.gpsimd.tensor_scalar(flagk[:, par], maskk[:, par], 1.0, None, ALU.is_equal).then_inc(s2["flags"], 1)

            def rsqrt(b):
                pool.wait_ge(s2["stat"], b + 1)
                nc.gpsimd.tensor_tensor(rs[:, 0, 0:1], rs[:, 0, 0:1], half[:, 0, 0:1], op=ALU.pow).then_inc(s2["rs"], 1)

            rsqrt(0)
            mask_bias(0, 0)
            with pool.Fori(0, B // 2 - 1) as pair:
                b = pair * 2
                for par in range(2):
                    pool.wait_ge(s2["smax"], HEADS * (b + par) + 1)
                    mask_bias(pair + par, 1 - par)
                    rsqrt(b + par + 1)
            pool.wait_ge(s2["smax"], HEADS * (B - 2) + 1)
            mask_bias(B // 2 - 1, 1)
            rsqrt(B - 1)

            with pool.Fori(0, G) as g:
                pool.wait_ge(s3["stat"], g + 1)
                nc.gpsimd.tensor_tensor(rs[:, 0, :], rs[:, 0, :], half[:, 0, :], op=ALU.pow).then_inc(s3["rs"], 1)

        @block.tensor
        def _(pe):
            def transpose_in(src, b0, b1, done, last=True):
                for c in range(DC):
                    for j in range(GB):
                        mm = pe.transpose(bank[b0 if c == 0 else b1][:, cols(j)], src[:, j, cols(c, P)], ident[0:T, 0:T])
                mm.then_inc(done, 1)

            pe.wait_ge(s["c_in"], 16 * 8)
            pe.wait_ge(s["setup_dve"], 1)
            with pe.Fori(0, G) as g:
                pe.wait_ge(s["h1"], g + 1)
                transpose_in(h, 0, 1, s["ht_ps1"])
                pe.wait_ge(s["ht_act1"], g + 1)
                pe.wait_ge(s["ht_dve1"], g + 1)
                for m in range(DC):
                    for c in range(DC):
                        mm = pe.matmul(bank[2 + m][:, 0:GT], wq[:, c, cols(m, P)], hT[:, c], start=c == 0, stop=c == DC - 1)
                mm.then_inc(s["q_ps"], 1)
                for j in range(GB):
                    for c in range(DC):
                        pe.matmul(bank[4 + j // 2][0:T, cols(j % 2, D)], hT[:, c, cols(j)], wk[:, c], start=c == 0, stop=c == DC - 1)
                for j in range(GB):
                    for c in range(DC):
                        mm = pe.matmul(bank[6][0:T, j:j + 1], hT[:, c, cols(j)], wbeta[:, c:c + 1], start=c == 0, stop=c == DC - 1)
                mm.then_inc(s["k_ps"], 1)
                for m in range(DC):
                    for c in range(DC):
                        mm = pe.matmul(bank[m][:, 0:GT], wv[:, c, cols(m, P)], hT[:, c], start=c == 0, stop=c == DC - 1)
                mm.then_inc(s["v_ps"], 1)
                pe.wait_ge(s["kt_sb"], g + 1)
                pe.wait_ge(s["q_sb"], g + 1)
                transpose_in(kt, 2, 3, s["kT_ps"])
                pe.wait_ge(s["v_scan"], g + 1)
                for j in range(GB):
                    for c in range(DC):
                        mm = pe.transpose(bank[j // 2][0:T, (j % 2) * D + c * P:(j % 2) * D + (c + 1) * P], vs[:, c, cols(j)], ident[:])
                mm.then_inc(s["vt_ps"], 1)
                pe.wait_ge(s["kT_sb"], g + 1)
                for j in range(GB):
                    for c in range(DC):
                        mm = pe.matmul(bank[4][0:T, cols(j)], kT[:, c, cols(j)], kT[:, c, cols(j)], start=c == 0, stop=c == DC - 1)
                mm.then_inc(s["gram_ps"], 1)
                for j in range(GB):
                    for c in range(DC):
                        mm = pe.matmul(bank[5][0:T, cols(j)], kT[:, c, cols(j)], qT[:, c, cols(j)], start=c == 0, stop=c == DC - 1)
                mm.then_inc(s["aq_ps"], 1)
                for n in range(len(LEVELS)):
                    for u in range(2):
                        it = 2 * n + u
                        pe.wait_ge(s["cmask"], len(LEVELS) * g + n + 1)
                        if n == 0:
                            pe.wait_ge(s["tri0"], g + 1)
                            pe.wait_ge(s["vt_sb"], g + 1)
                        else:
                            pe.wait_ge(s["tri_up"], 2 * (len(LEVELS) - 1) * g + it - 1)
                        for j in (2 * u, 2 * u + 1):
                            mm = pe.matmul(bank[6 + u][0:T, cols(j % 2)], cT[:, n, j], tri[:, j], start=True, stop=True)
                        mm.then_inc(s["xps"], 1)
                    for u in range(2):
                        it = 2 * n + u
                        pe.wait_ge(s["xsb"], 2 * len(LEVELS) * g + it + 1)
                        if n > 0:
                            pe.wait_ge(s["triT_up"], 2 * len(LEVELS) * g + it - 1)
                        if n < len(LEVELS) - 1:
                            for j in (2 * u, 2 * u + 1):
                                mm = pe.matmul(bank[u][0:T, cols(j % 2)], triT[:, j], xq[:, j], start=True, stop=True)
                            mm.then_inc(s["tps_t"], 1)
                        for j in (2 * u, 2 * u + 1):
                            mm = pe.matmul(bank[2 + u][0:T, cols(j % 2)], xq[:, j], triT[:, j], start=True, stop=True)
                        mm.then_inc(s["tps_tt"], 1)
                pe.wait_ge(s["triT_up"], 2 * len(LEVELS) * (g + 1))
                pe.wait_ge(s["aT_sb"], g + 1)
                for j in range(GB):
                    mm = pe.matmul(bank[4 + j // 2][0:T, cols(j % 2, D)], triT[:, j], vt[:, j], start=True, stop=True)
                mm.then_inc(s["y_ps"], 1)
                pe.wait_ge(s["y_sb"], g + 1)
                for c in range(DC):
                    for j in range(GB):
                        mm = pe.matmul(bank[6 + c][:, cols(j)], y[:, j, cols(c, P)], aT[:, j], start=True, stop=True)
                mm.then_inc(s["oT_ps"], 1)
                pe.wait_ge(s["oT_a"], g + 1)
                pe.wait_ge(s["oT_d"], g + 1)
                for j in range(GB):
                    for c in range(DC):
                        mm = pe.matmul(bank[j // 2][0:T, cols(j % 2, D)], oT[:, c, cols(j)], wo[:, c], start=c == 0, stop=c == DC - 1)
                mm.then_inc(s["wo_ps"], 1)
                pe.wait_ge(s["h2_sb"], g + 1)
                transpose_in(h, 2, 3, s["h2t_ps"])
                pe.wait_ge(s["h2t_a"], g + 1)
                pe.wait_ge(s["h2t_d"], g + 1)
                for m in range(FC):
                    if m >= 2:
                        pe.wait_ge(s["silu"], FC * g + m - 1)
                    for c in range(DC):
                        mm = pe.matmul(bank[4 + m % 2][:, 0:GT], wgate[:, c, cols(m, P)], hT[:, c], start=c == 0, stop=c == DC - 1)
                    mm.then_inc(s["g_ps"], 1)
                    if m >= 2:
                        pe.wait_ge(s["hid_sb"], FC * g + m - 1)
                    for c in range(DC):
                        mm = pe.matmul(bank[6 + m % 2][:, 0:GT], wup[:, c, cols(m, P)], hT[:, c], start=c == 0, stop=c == DC - 1)
                    mm.then_inc(s["u_ps"], 1)
                pe.wait_ge(s["hid_sb"], FC * (g + 1))
                for j in range(GB):
                    for c in range(FC):
                        mm = pe.matmul(bank[j // 2][0:T, cols(j % 2, D)], hid[:, c, cols(j)], wdown[:, c], start=c == 0, stop=c == FC - 1)
                mm.then_inc(s["down_ps"], 1)

            pe.wait_ge(s["w_in2"], 16 * 4)
            pe.nop().then_inc(s2["pv_done"], 2)

            def project(pair, par):
                b = pair * 2 + par
                ready = s2["ctx0"] if par == 0 else s2["ctx1"]
                pe.wait_ge(ready, loaded(pair))
                if not (isinstance(b, int) and b == 0):
                    pe.wait_ge(s2["smax"], b * HEADS)
                for m in range(DC):
                    for c in range(DC):
                        mm = pe.matmul(bank[4 + m][:, 0:S2], xwk[:, c, cols(m, P)], ctxT[:, par, c], start=c == 0, stop=c == DC - 1)
                mm.then_inc(s2["k_ps"], 1)
                pe.wait_ge(s2["h"], b + 1)
                for c in range(DC):
                    mm = pe.transpose(bank[7][:, cols(c)], h2[:, cols(c, P)], ident[0:T, 0:T])
                mm.then_inc(s2["hT_ps"], 1)
                pe.wait_ge(s2["hT_sb"], b + 1)
                for m in range(DC):
                    for c in range(DC):
                        mm = pe.matmul(bank[7][:, 2 * T + m * T:2 * T + (m + 1) * T], xwq[:, c, cols(m, P)], h2T[:, c], start=c == 0, stop=c == DC - 1)
                mm.then_inc(s2["q_ps"], 1)
                pe.wait_ge(s2["k_lo"], b + 1)
                for c3 in range(KC):
                    for c in range(DC):
                        mm = pe.matmul(bank[4 + c3 // 2][0:KP, cols(c3 % 2, D)], ctxT[:, par, c, cols(c3, KP)], xwv[:, c], start=c == 0, stop=c == DC - 1)
                mm.then_inc(s2["v_ps"], 1)

            def row_max(pair, par):
                b = pair * 2 + par
                pe.wait_ge(s2[f"qst{par}"], stacked(pair))
                pe.wait_ge(s2[f"kst{par}"], stacked(pair))
                pe.wait_ge(s2["v_sb"], b + 1)
                for hd in range(HEADS):
                    if hd >= 2:
                        pe.wait_ge(s2["smax"], HEADS * b + hd - 1)
                    pe.matmul(bank[4 + hd % 2][0:T, 0:S2E], qst[par][0:ROWS, hd], kst[par][0:ROWS, hd], start=True, stop=True).then_inc(s2["max_ps"], 1)
                pe.wait_ge(s2["smax"], HEADS * (b + 1))
                pe.wait_ge(s2["q_lo"], b + 1)
                pe.transpose(bank[7][0:HEADS, 0:T], smax[:], ident[0:T, 0:T]).then_inc(s2["mt_ps"], 1)

            def scores(pair, par, n):
                b = pair * 2 + par
                c3, hf = n // 2, n % 2
                if n == 0:
                    pe.wait_ge(s2["negm_in"], 16 * (b + 1))
                    pe.wait_ge(s2["flags"], b + 1)
                pe.wait_ge(s2["exp"], 6 * b + n + 1)
                for u in range(2):
                    bk = bank[2 * (n % 2) + u]
                    pe.matmul(bk[0:KP, 0:GT], negbig[:], flagk[:, par, c3, :].unsqueeze(1).broadcast_to([KP, HPB, T]), start=True, stop=False, skip_group_check=True)
                    for i in range(HPB):
                        hd = 8 * hf + HPB * u + i
                        mm = pe.matmul(bk[0:KP, cols(i)], kst[par][:, hd, cols(c3, KP)], qst[par][:, hd], start=False, stop=True, skip_group_check=True)
                mm.then_inc(s2["sc_ps"], 1)

            def weighted_values(pair, par, n):
                b = pair * 2 + par
                c3, hf = n // 2, n % 2
                pe.wait_ge(s2["exp"], 6 * b + n + 3)
                for i in range(2 * HPB):
                    hd = 8 * hf + i
                    row = 2 * HD * (hd % HPB)
                    mm = pe.matmul(bank[6][row:row + 2 * HD, cols(hd // HPB)], vaug[par][:, c3, hd], pr[n % 2][:, i],
                                   start=(c3 == 0 and hd < HPB), stop=(c3 == KC - 1), skip_group_check=True)
                mm.then_inc(s2["pv_done"], 1)

            def close_row(pair, par):
                b = pair * 2 + par
                pe.wait_ge(s2["pv_sb"], b + 1)
                for g4 in range(HPB):
                    mm = pe.transpose(bank[7][0:T, cols(g4, P)], pv[:, cols(g4)], ident[:])
                mm.then_inc(s2["ot_ps"], 1)
                pe.wait_ge(s2["on"], b + 1)
                for c in range(DC):
                    mm = pe.transpose(bank[7][:, cols(c)], on[:].rearrange("q h d -> q (h d)")[:, cols(c, P)], ident[0:T, 0:T])
                mm.then_inc(s2["onT_ps"], 1)
                pe.wait_ge(s2["onT_sb"], b + 1)
                for c in range(DC):
                    mm = pe.matmul(bank[7][0:T, 0:D], onT[:, c], xwo[:, c], start=c == 0, stop=c == DC - 1)
                mm.then_inc(s2["wo_ps"], 1)

            def attend(pair, par):
                b = pair * 2 + par
                row_max(pair, par)
                scores(pair, par, 0)
                for n in range(1, 6):
                    scores(pair, par, n)
                    weighted_values(pair, par, n - 1)
                weighted_values(pair, par, 5)
                close_row(pair, par)

            project(0, 0)
            with pe.Fori(0, B // 2 - 1) as pair:
                b = pair * 2
                for par in range(2):
                    attend(pair, par)
                    pe.wait_ge(s2["x_new"], b + par + 1)
                    project(pair + par, 1 - par)
            attend(B // 2 - 1, 0)
            pe.wait_ge(s2["x_new"], B - 1)
            project(B // 2 - 1, 1)
            attend(B // 2 - 1, 1)

            pe.wait_ge(s["w_in3"], 16 * (3 * (NE + 1) + 1))
            with pe.Fori(0, G) as g:
                pe.wait_ge(s3["h"], g + 1)
                transpose_in(h3, 0, 1, s3["ht_ps"])
                pe.wait_ge(s3["ht_a"], g + 1)
                pe.wait_ge(s3["ht_d"], g + 1)
                for j in range(GB):
                    for c in range(DC):
                        mm = pe.matmul(bank[2][0:T, cols(j, NE)], h3T[:, c, cols(j)], router[:, c], start=c == 0, stop=c == DC - 1)
                mm.then_inc(s3["lg_ps"], 1)

                def expand(e):
                    for m in range(DC):
                        it = DC * e + m
                        if it >= 2:
                            pe.wait_ge(s3["silu"], DC * (NE + 1) * g + it - 1)
                        for c in range(DC):
                            mm = pe.matmul(bank[4 + it % 2][:, 0:GT], e1[:, e, c, cols(m, P)], h3T[:, c], start=c == 0, stop=c == DC - 1)
                        mm.then_inc(s3["g_ps"], 1)
                        if it >= 2:
                            pe.wait_ge(s3["hid"], DC * (NE + 1) * g + it - 1)
                        for c in range(DC):
                            mm = pe.matmul(bank[6 + it % 2][:, 0:GT], e3[:, e, c, cols(m, P)], h3T[:, c], start=c == 0, stop=c == DC - 1)
                        mm.then_inc(s3["u_ps"], 1)

                def contract(e):
                    pe.wait_ge(s3["hid"], DC * (NE + 1) * g + DC * (e + 1))
                    if e == 0:
                        pe.wait_ge(s3["logit"], g + 1)
                    if e >= 2:
                        pe.wait_ge(s3["x_new"], (NE + 1) * g + e - 1)
                    for j in range(GB):
                        for c in range(DC):
                            mm = pe.matmul(bank[2 * (e % 2) + j // 2][0:T, cols(j % 2, D)], hid3[:, e % 2, c, cols(j)], e2[:, e, c], start=c == 0, stop=c == DC - 1)
                    mm.then_inc(s3["d_ps"], 1)

                expand(0)
                for e in range(1, NE + 1):
                    expand(e)
                    contract(e - 1)
                contract(NE)

        @block.scalar
        def _(act):
            act.wait_ge(s["c_in"], 16 * 8)
            nc.scalar.activation(pcol[:, 3, :], pcol[:, 2, :], ACT.Tanh, scale=0.5).then_inc(s["alpha_t"], 1)
            nc.scalar.mul(betab[:, 1:2], betab[:, 0:1], 0.5).then_inc(s["setup_act"], 1)
            act.wait_ge(s["setup_act"], 1)
            act.wait_ge(s["alpha_d"], 2)
            with act.Fori(0, G) as g:
                act.wait_ge(s["ht_ps1"], g + 1)
                nc.scalar.copy(hT[:, 0], bank[0][:, 0:GT]).then_inc(s["ht_act1"], 1)
                act.wait_ge(s["q_ps"], g + 1)
                for m in range(DC):
                    last = nc.scalar.copy(qT[:, m], bank[2 + m][:, 0:GT])
                last.then_inc(s["q_sb"], 1)
                act.wait_ge(s["k_ps"], g + 1)
                nc.scalar.activation(small[:, 0], bank[6][0:T, 0:GB], ACT.Tanh, bias=betab[:, 1:2], scale=0.5).then_inc(s["tanh_b"], 1)
                for j in range(GB):
                    last = nc.scalar.activation(kt[:, j], bank[4 + j // 2][0:T, cols(j % 2, D)], ACT.Square, accum_out=small[:, 2, j:j + 1])
                last.then_inc(s["ksq"], 1)
                act.wait_ge(s["v_ps"], g + 1)
                for m in range(DC):
                    last = nc.scalar.activation(va[:, m], bank[m][:, 0:GT], ACT.Copy, scale=alpha[:, 0, m:m + 1])
                last.then_inc(s["va_sb"], 1)
                act.wait_ge(s["kscale"], g + 1)
                act.wait_ge(s["ksq"], g + 1)
                for j in range(GB):
                    last = nc.scalar.activation(kt[:, j], bank[4 + j // 2][0:T, cols(j % 2, D)], ACT.Copy, scale=small[:, 4, j:j + 1])
                last.then_inc(s["kt_sb"], 1)
                act.wait_ge(s["kT_ps"], g + 1)
                for c in range(DC):
                    last = nc.scalar.copy(kT[:, c], bank[2 + c][:, 0:GT])
                last.then_inc(s["kT_sb"], 1)
                act.wait_ge(s["vt_ps"], g + 1)
                for j in range(GB):
                    last = nc.scalar.activation(vt[:, j], bank[j // 2][0:T, cols(j % 2, D)], ACT.Copy, scale=small[:, 1, j:j + 1])
                last.then_inc(s["vt_sb"], 1)
                for n in range(len(LEVELS)):
                    for u in range(2):
                        act.wait_ge(s["xps"], 2 * len(LEVELS) * g + 2 * n + u + 1)
                        nc.scalar.copy(xq[:, 2 * u:2 * u + 2], bank[6 + u][0:T, 0:2 * T]).then_inc(s["xsb"], 1)
                act.wait_ge(s["y_ps"], g + 1)
                for u in range(2):
                    last = nc.scalar.copy(y[:, 2 * u:2 * u + 2], bank[4 + u][0:T, 0:2 * D])
                last.then_inc(s["y_sb"], 1)
                act.wait_ge(s["oT_ps"], g + 1)
                nc.scalar.copy(oT[:, 0], bank[6][:, 0:GT]).then_inc(s["oT_a"], 1)
                act.wait_ge(s["x1_sb"], g + 1)
                for j in range(GB):
                    last = nc.scalar.activation(kt[:, j], x1[:, j], ACT.Square, accum_out=small[:, 5, j:j + 1])
                last.then_inc(s["x1_sq"], 1)
                act.wait_ge(s["h2t_ps"], g + 1)
                nc.scalar.copy(hT[:, 0], bank[2][:, 0:GT]).then_inc(s["h2t_a"], 1)
                for m in range(FC):
                    act.wait_ge(s["g_ps"], FC * g + m + 1)
                    if m >= 2:
                        act.wait_ge(s["hid_sb"], FC * g + m - 1)
                    nc.scalar.activation(sg[:, m % 2], bank[4 + m % 2][:, 0:GT], ACT.Silu).then_inc(s["silu"], 1)

            def split_projections(pair, par):
                b = pair * 2 + par
                act.wait_ge(s2["k_ps"], b + 1)
                if not (isinstance(b, int) and b == 0):
                    act.wait_ge(s2[f"kst{1 - par}"], stacked(pair - 1 + par))
                    act.wait_ge(s2[f"qst{1 - par}"], stacked(pair - 1 + par))
                for m in range(DC):
                    last = nc.scalar.copy(khi[:, m], bank[4 + m][:, 0:S2])
                last.then_inc(s2["k_hi"], 1)
                act.wait_ge(s2["hT_ps"], b + 1)
                nc.scalar.copy(h2T[:], bank[7][:, 0:2 * T]).then_inc(s2["hT_sb"], 1)
                act.wait_ge(s2["q_ps"], b + 1)
                nc.scalar.copy(qhi[:], bank[7][:, 2 * T:4 * T]).then_inc(s2["q_hi"], 1)
                act.wait_ge(s2["v_ps"], b + 1)
                for c3 in range(KC):
                    last = nc.scalar.copy(vaug[par][:, c3, :, 0:HD], bank[4 + c3 // 2][0:KP, cols(c3 % 2, D)].rearrange("k (h d) -> k h d", d=HD))
                last.then_inc(s2["v_sb"], 1)

            def softmax_row(pair, par):
                b = pair * 2 + par
                act.wait_ge(s2["mt_ps"], b + 1)
                nc.scalar.mul(negm[:], bank[7][0:HEADS, 0:T], -1.0).then_inc(s2["negm"], 1)
                for n in range(6):
                    act.wait_ge(s2["sc_ps"], 6 * b + n + 1)
                    act.wait_ge(s2["pv_done"], 6 * b + n + 1)
                    for u in range(2):
                        last = nc.scalar.activation(pr[n % 2][:, HPB * u:HPB * (u + 1)], bank[2 * (n % 2) + u][0:KP, 0:GT], ACT.Exp, scale=1.0 / HD ** 0.5)
                    last.then_inc(s2["exp"], 1)
                act.wait_ge(s2["pv_done"], 6 * b + 8)
                nc.scalar.copy(pv[:], bank[6][:, 0:GT]).then_inc(s2["pv_sb"], 1)
                act.wait_ge(s2["onT_ps"], b + 1)
                nc.scalar.copy(onT[:], bank[7][:, 0:2 * T]).then_inc(s2["onT_sb"], 1)

            act.wait_ge(s2["ready"], 1)
            act.nop().then_inc(s2["exp"], 2)
            act.wait_ge(s["x_mlp"], G)
            split_projections(0, 0)
            with act.Fori(0, B // 2 - 1) as pair:
                b = pair * 2
                for par in range(2):
                    softmax_row(pair, par)
                    split_projections(pair + par, 1 - par)
            softmax_row(B // 2 - 1, 0)
            split_projections(B // 2 - 1, 1)
            softmax_row(B // 2 - 1, 1)

            with act.Fori(0, G) as g:
                act.wait_ge(s3["ht_ps"], g + 1)
                nc.scalar.copy(h3T[:, 0], bank[0][:, 0:GT]).then_inc(s3["ht_a"], 1)
                act.wait_ge(s3["logit"], g + 1)
                nc.scalar.activation(prob[:], logit[:], ACT.Exp, scale=-1.0).then_inc(s3["ex"], 1)
                for it in range(DC * (NE + 1)):
                    act.wait_ge(s3["g_ps"], DC * (NE + 1) * g + it + 1)
                    if it >= 2:
                        act.wait_ge(s3["hid"], DC * (NE + 1) * g + it - 1)
                    nc.scalar.activation(sg3[:, it % 2], bank[4 + it % 2][:, 0:GT], ACT.Silu).then_inc(s3["silu"], 1)

        @block.vector
        def _(dve):
            dve.wait_ge(s["c_in"], 16 * 8)
            dve.wait_ge(s["w_in1"], 16 * 8)
            for c in range(DC):
                for w in (wq[:, c], wk[:, c], wv[:, c], wbeta[:, c:c + 1]):
                    nc.vector.tensor_scalar(w, w, pcol[:, 0, c:c + 1], None, ALU.mult)
                for w in (wgate[:, c], wup[:, c]):
                    last = nc.vector.tensor_scalar(w, w, pcol[:, 1, c:c + 1], None, ALU.mult)
            last.then_inc(s["setup_dve"], 1)
            dve.wait_ge(s["alpha_t"], 1)
            nc.vector.tensor_scalar(alpha[:, 0], pcol[:, 3], 0.5, 0.5, ALU.mult, ALU.add)
            nc.vector.tensor_scalar(alpha[:, 1], pcol[:, 3], -0.5, 0.5, ALU.mult, ALU.add).then_inc(s["alpha_d"], 1)
            dve.wait_ge(s["alpha_d"], 1)
            for c in range(DC):
                last = nc.vector.tensor_scalar(decay[:, c], keep[:], alpha[:, 1, c:c + 1], None, ALU.mult)
            last.then_inc(s["alpha_d"], 1)
            dve.wait_ge(s["alpha_d"], 2)
            dve.wait_ge(s["x_in"], 16 * G)

            def group_stats(g, done):
                for j in range(GB):
                    nc.vector.bn_stats(out=stats[:, j], in_=x[:, bass.ds(g * GB + j, 1), :].rearrange("t a d -> t (a d)")).then_inc(done, 1)
                wait_apart(dve, done, (GB + 1) * g + GB)
                for j in range(GB):
                    last = nc.vector.bn_aggr(out=mv[:, j], in_=stats[:, j])
                last.then_inc(done, 1)
                dve.wait_ge(done, (GB + 1) * (g + 1))

            with dve.Fori(0, G) as g:
                group_stats(g, s["stat1"])
                nc.vector.tensor_scalar(rs[:, 0, :], mv[:, :, 1], LN_EPS, None, ALU.add)
                nc.vector.tensor_scalar(rs[:, 1, :], mv[:, :, 1], 1.0 + RMS_EPS, LN_EPS * RMS_EPS, ALU.mult, ALU.add).then_inc(s["var1"], 1)
                dve.wait_ge(s["rs1"], g + 1)
                for j in range(GB):
                    row = x[:, bass.ds(g * GB + j, 1), :].rearrange("t a d -> t (a d)")
                    last = nc.vector.tensor_scalar(h[:, j], row, mv[:, j, 0:1], rs[:, 1, j:j + 1], ALU.subtract, ALU.mult)
                last.then_inc(s["h1"], 1)
                for j in range(GB):
                    row = x[:, bass.ds(g * GB + j, 1), :].rearrange("t a d -> t (a d)")
                    last = nc.vector.tensor_scalar(xn[:, j], row, mv[:, j, 0:1], rs[:, 0, j:j + 1], ALU.subtract, ALU.mult)
                last.then_inc(s["xn1"], 1)
                dve.wait_ge(s["ht_ps1"], g + 1)
                nc.vector.tensor_copy(hT[:, 1], bank[1][:, 0:GT]).then_inc(s["ht_dve1"], 1)
                dve.wait_ge(s["va_sb"], g + 1)
                for c in range(DC):
                    last = nc.vector.tensor_tensor_scan(vs[:, c], decay[:, c], va[:, c], 0.0, ALU.mult, ALU.add)
                last.then_inc(s["v_scan"], 1)
                dve.wait_ge(s["gram_ps"], g + 1)
                gram = bank[4][0:T, 0:GT].rearrange("s (j t) -> s j t", j=GB)
                nc.vector.tensor_tensor(negT[:], gram, over_rows(M_SUNEG), op=ALU.mult)
                nc.vector.tensor_tensor(neg[:], gram, over_rows(M_SLNEG), op=ALU.mult).then_inc(s["negs"], 1)
                dve.wait_ge(s["aq_ps"], g + 1)
                nc.vector.tensor_tensor(aT[:], bank[5][0:T, 0:GT].rearrange("s (j t) -> s j t", j=GB), over_rows(M_LE), op=ALU.mult).then_inc(s["aT_sb"], 1)
                dve.wait_ge(s["negs"], g + 1)
                nc.vector.tensor_tensor(tri[:], neg[:], over_rows(M_B1), op=ALU.mult)
                nc.vector.tensor_tensor(triT[:], negT[:], over_rows(M_BT), op=ALU.mult).then_inc(s["tri0a"], 1)
                dve.wait_ge(s["tri0a"], g + 1)
                eye = ident[0:T, 0:T].unsqueeze(1).broadcast_to([T, GB, T])
                nc.vector.tensor_tensor(tri[:], tri[:], eye, op=ALU.add)
                nc.vector.tensor_tensor(triT[:], triT[:], eye, op=ALU.add).then_inc(s["tri0"], 1)
                dve.wait_ge(s["tri0"], g + 1)
                NL = len(LEVELS)
                for n in range(NL):
                    for u in range(2):
                        it = 2 * n + u
                        rows = slice(2 * u, 2 * u + 2)
                        if n < NL - 1:
                            dve.wait_ge(s["tps_t"], 2 * (NL - 1) * g + it + 1)
                            if n > 0:
                                dve.wait_ge(s["tri_up"], 2 * (NL - 1) * g + it - 1)
                            nc.vector.tensor_tensor(tri[:, rows], tri[:, rows], bank[u][0:T, 0:2 * T].rearrange("s (j t) -> s j t", j=2), op=ALU.add).then_inc(s["tri_up"], 1)
                        dve.wait_ge(s["tps_tt"], 2 * NL * g + it + 1)
                        if n > 0:
                            dve.wait_ge(s["triT_up"], 2 * NL * g + it - 1)
                        nc.vector.tensor_tensor(triT[:, rows], triT[:, rows], bank[2 + u][0:T, 0:2 * T].rearrange("s (j t) -> s j t", j=2), op=ALU.add).then_inc(s["triT_up"], 1)
                dve.wait_ge(s["oT_ps"], g + 1)
                nc.vector.tensor_copy(oT[:, 1], bank[7][:, 0:GT]).then_inc(s["oT_d"], 1)
                dve.wait_ge(s["wo_ps"], g + 1)
                dve.wait_ge(s["xn1"], g + 1)
                for u in range(2):
                    last = nc.vector.tensor_tensor(x1[:, 2 * u:2 * u + 2], xn[:, 2 * u:2 * u + 2], bank[u][0:T, 0:2 * D].rearrange("t (j d) -> t j d", j=2), op=ALU.add)
                last.then_inc(s["x1_sb"], 1)
                dve.wait_ge(s["x1_sb"], g + 1)
                dve.wait_ge(s["rms"], g + 1)
                for j in range(GB):
                    last = nc.vector.tensor_scalar(h[:, j], x1[:, j], small[:, 5, j:j + 1], None, ALU.mult)
                last.then_inc(s["h2_sb"], 1)
                dve.wait_ge(s["h2t_ps"], g + 1)
                nc.vector.tensor_copy(hT[:, 1], bank[3][:, 0:GT]).then_inc(s["h2t_d"], 1)
                for m in range(FC):
                    dve.wait_ge(s["silu"], FC * g + m + 1)
                    dve.wait_ge(s["u_ps"], FC * g + m + 1)
                    nc.vector.tensor_tensor(hid[:, m], sg[:, m % 2], bank[6 + m % 2][:, 0:GT], op=ALU.mult).then_inc(s["hid_sb"], 1)
                dve.wait_ge(s["down_ps"], g + 1)
                dve.wait_ge(s["x_plus"], g + 1)
                for u in range(2):
                    rows = x[:, bass.ds(g * GB + 2 * u, 2), :]
                    last = nc.vector.tensor_tensor(rows, rows, bank[u][0:T, 0:2 * D].rearrange("t (j d) -> t j d", j=2), op=ALU.add)
                last.then_inc(s["x_mlp"], 1)
                dve.wait_ge(s["x_mlp"], g + 1)

            def x_row(b):
                return x[:, bass.ds(b, 1), :].rearrange("t a d -> t (a d)")

            def normalise(b):
                nc.vector.bn_stats(out=stats[:, 0], in_=x_row(b)).then_inc(s2["rden"], 1)
                wait_apart(dve, s2["rden"], 4 * b + 1)
                nc.vector.bn_aggr(out=mv[:, 0], in_=stats[:, 0]).then_inc(s2["rden"], 1)
                dve.wait_ge(s2["rden"], 4 * b + 2)
                nc.vector.tensor_scalar(rs[:, 0, 0:1], mv[:, 0, 1:2], LN_EPS, None, ALU.add).then_inc(s2["stat"], 1)
                dve.wait_ge(s2["rs"], b + 1)
                nc.vector.tensor_scalar(h2[:], x_row(b), mv[:, 0, 0:1], rs[:, 0, 0:1], ALU.subtract, ALU.mult).then_inc(s2["h"], 1)

            def split_projections_low(pair, par):
                b = pair * 2 + par
                dve.wait_ge(s2["k_hi"], b + 1)
                for m in range(DC):
                    last = nc.vector.tensor_tensor(klo[:, m], bank[4 + m][:, 0:S2], khi[:, m].bitcast(F32), op=ALU.subtract)
                last.then_inc(s2["k_lo"], 1)
                dve.wait_ge(s2["q_hi"], b + 1)
                nc.vector.tensor_tensor(qlo[:], bank[7][:, 2 * T:4 * T].rearrange("p (m q) -> p m q", m=DC), qhi[:].bitcast(F32), op=ALU.subtract).then_inc(s2["q_lo"], 1)

            def maxima(pair, par):
                b = pair * 2 + par
                dve.wait_ge(s2["flags"], b + 1)
                for hd in range(HEADS):
                    if hd >= 2:
                        dve.wait_ge(s2["smax"], HEADS * b + hd - 1)
                    wait_apart(dve, s2["max_ps"], HEADS * b + hd + 1)
                    nc.vector.tensor_tensor_reduce(out=junk[:, hd % 2, :], in0=bank[4 + hd % 2][0:T, 0:S2], in1=biasq[:, par, :], scale=1.0, scalar=-3e38,
                                                   op0=ALU.add, op1=ALU.max, accum_out=smax[:, hd:hd + 1]).then_inc(s2["smax"], 1)

            def finish_row(b):
                dve.wait_ge(s2["ot_ps"], b + 1)
                o = bank[7][0:T, :].rearrange("q (h d) -> q h d", h=HEADS)
                nc.vector.reciprocal(rden[:], o[:, :, HD:HD + 1]).then_inc(s2["rden"], 1)
                dve.wait_ge(s2["rden"], 4 * b + 3)
                nc.vector.tensor_tensor(on[:], o[:, :, 0:HD], rden[:].broadcast_to([T, HEADS, HD]), op=ALU.mult).then_inc(s2["on"], 1)
                dve.wait_ge(s2["wo_ps"], b + 1)
                nc.vector.tensor_tensor(x_row(b), x_row(b), bank[7][0:T, 0:D], op=ALU.add).then_inc(s2["x_new"], 1)
                nc.vector.memset(junk[:, 0, 0:1], 0.0).then_inc(s2["rden"], 1)
                dve.wait_ge(s2["rden"], 4 * b + 4)

            normalise(0)
            split_projections_low(0, 0)
            with dve.Fori(0, B // 2 - 1) as pair:
                b = pair * 2
                for par in range(2):
                    maxima(pair, par)
                    finish_row(b + par)
                    normalise(b + par + 1)
                    split_projections_low(pair + par, 1 - par)
            maxima(B // 2 - 1, 0)
            finish_row(B - 2)
            normalise(B - 1)
            split_projections_low(B // 2 - 1, 1)
            maxima(B // 2 - 1, 1)
            finish_row(B - 1)

            dve.wait_ge(s2["x_new"], B)
            with dve.Fori(0, G) as g:
                for j in range(GB):
                    nc.vector.bn_stats(out=stats[:, j], in_=x[:, bass.ds(g * GB + j, 1), :].rearrange("t a d -> t (a d)"))
                nc.vector.memset(junk[:, 0, 0:1], 0.0).then_inc(s3["den"], 1)
                wait_apart(dve, s3["den"], 3 * g + 1)
                for j in range(GB):
                    last = nc.vector.bn_aggr(out=mv[:, j], in_=stats[:, j])
                last.then_inc(s3["den"], 1)
                dve.wait_ge(s3["den"], 3 * g + 2)
                nc.vector.tensor_scalar(rs[:, 0, :], mv[:, :, 1], LN_EPS, None, ALU.add).then_inc(s3["stat"], 1)
                dve.wait_ge(s3["rs"], g + 1)
                for j in range(GB):
                    row = x[:, bass.ds(g * GB + j, 1), :].rearrange("t a d -> t (a d)")
                    last = nc.vector.tensor_scalar(h3[:, j], row, mv[:, j, 0:1], rs[:, 0, j:j + 1], ALU.subtract, ALU.mult)
                last.then_inc(s3["h"], 1)
                dve.wait_ge(s3["ht_ps"], g + 1)
                nc.vector.tensor_copy(h3T[:, 1], bank[1][:, 0:GT]).then_inc(s3["ht_d"], 1)
                dve.wait_ge(s3["lg_ps"], g + 1)
                nc.vector.tensor_tensor(logit[:], bank[2][0:T, 0:GB * NE].rearrange("t (j e) -> t j e", j=GB), gateb[:].unsqueeze(1).broadcast_to([T, GB, NE]), op=ALU.add).then_inc(s3["logit"], 1)
                dve.wait_ge(s3["ex"], g + 1)
                nc.vector.tensor_scalar(prob[:], prob[:], 1.0, None, ALU.add).then_inc(s3["prob"], 1)
                dve.wait_ge(s3["prob"], 2 * g + 1)
                nc.vector.reciprocal(prob[:], prob[:]).then_inc(s3["prob"], 1)
                dve.wait_ge(s3["prob"], 2 * g + 2)
                for e in range(NE):
                    mine = prob[:, :, e:e + 1]
                    if e > 0:
                        nc.vector.tensor_tensor(cmp1[:, :, e, 0:e], prob[:, :, 0:e], mine.broadcast_to([T, GB, e]), op=ALU.is_ge)
                    last = nc.vector.tensor_tensor(cmp1[:, :, e, e:NE], prob[:, :, e:NE], mine.broadcast_to([T, GB, NE - e]), op=ALU.is_gt)
                last.then_inc(s3["cmp"], 1)
                dve.wait_ge(s3["cmp"], g + 1)
                nc.vector.tensor_reduce(rank[:], cmp1[:], AX, ALU.add).then_inc(s3["rank"], 1)
                dve.wait_ge(s3["rank"], g + 1)
                nc.vector.scalar_tensor_tensor(out=gate[:], in0=rank[:], scalar=2.0, in1=prob[:], op0=ALU.is_lt, op1=ALU.mult).then_inc(s3["sel"], 1)
                dve.wait_ge(s3["sel"], g + 1)
                nc.vector.tensor_reduce(wsum[:], gate[:], AX, ALU.add).then_inc(s3["wsum"], 1)
                dve.wait_ge(s3["wsum"], 3 * g + 1)
                nc.vector.tensor_scalar(wsum[:], wsum[:], 1e-8, None, ALU.add).then_inc(s3["wsum"], 1)
                dve.wait_ge(s3["wsum"], 3 * g + 2)
                nc.vector.reciprocal(wsum[:], wsum[:]).then_inc(s3["wsum"], 1)
                dve.wait_ge(s3["wsum"], 3 * g + 3)
                nc.vector.tensor_tensor(gate[:], gate[:], wsum[:].broadcast_to([T, GB, NE]), op=ALU.mult).then_inc(s3["gate"], 1)
                dve.wait_ge(s3["gate"], g + 1)

                def hidden(e):
                    for m in range(DC):
                        it = DC * e + m
                        dve.wait_ge(s3["silu"], DC * (NE + 1) * g + it + 1)
                        dve.wait_ge(s3["u_ps"], DC * (NE + 1) * g + it + 1)
                        if e >= 2 and m == 0:
                            dve.wait_ge(s3["d_ps"], (NE + 1) * g + e - 1)
                        nc.vector.tensor_tensor(hid3[:, e % 2, m], sg3[:, it % 2], bank[6 + it % 2][:, 0:GT], op=ALU.mult).then_inc(s3["hid"], 1)

                def accumulate(e):
                    dve.wait_ge(s3["d_ps"], (NE + 1) * g + e + 1)
                    if e > 0:
                        dve.wait_ge(s3["x_new"], (NE + 1) * g + e)
                    for j in range(GB):
                        row = x[:, bass.ds(g * GB + j, 1), :].rearrange("t a d -> t (a d)")
                        part = bank[2 * (e % 2) + j // 2][0:T, cols(j % 2, D)]
                        if e < NE:
                            last = nc.vector.scalar_tensor_tensor(out=row, in0=part, scalar=gate[:, j, e:e + 1], in1=row, op0=ALU.mult, op1=ALU.add)
                        else:
                            last = nc.vector.tensor_tensor(row, row, part, op=ALU.add)
                    last.then_inc(s3["x_new"], 1)

                hidden(0)
                for e in range(1, NE + 1):
                    hidden(e)
                    accumulate(e - 1)
                accumulate(NE)
                nc.vector.memset(junk[:, 0, 0:1], 0.0).then_inc(s3["den"], 1)
                dve.wait_ge(s3["den"], 3 * g + 3)


def kernel(**inputs):
    import concourse.bacc as bacc
    from concourse.bass_utils import run_bass_kernel_spmd

    f = {n: np.ascontiguousarray(a) for n, a in inputs.items()}
    heads_last = (2, 8, HD)

    def split_heads(w):
        return np.ascontiguousarray(w.T.reshape(D, *heads_last).transpose(0, 1, 3, 2).reshape(D, D))

    arrays = {n: f[n] for n in (
        "x", "L0_attn_norm1_w", "L0_attn_Wq", "L0_attn_Wk", "L0_attn_Wv", "L0_attn_beta_w", "L0_attn_beta_b", "L0_attn_Wo",
        "L0_attn_alpha_logit", "L0_attn_norm2_w", "L0_attn_w_gate", "L0_attn_w_up", "L0_attn_w_down", "L0_ffn_gate_b")}
    for n in ("L0_attn_beta_w", "L0_attn_norm1_w", "L0_attn_norm2_w", "L0_attn_alpha_logit"):
        arrays[n] = np.ascontiguousarray(f[n].reshape(DC, P).T)
    arrays["mask"] = f["mask_BxSxS2_ik1"]
    arrays["maskT"] = np.ascontiguousarray(f["mask_BxSxS2_ik1"].transpose(0, 2, 1))
    arrays["ctxT"] = np.ascontiguousarray(f["ctx_1024"].transpose(0, 2, 1))
    arrays["xwq"] = split_heads(f["L0_xattn_wq"])
    arrays["xwk"] = split_heads(f["L0_xattn_wk"])
    arrays["xwv"] = np.ascontiguousarray(f["L0_xattn_wv"].T)
    arrays["xwo"] = np.ascontiguousarray(f["L0_xattn_w_out"].T)
    arrays["router"] = np.ascontiguousarray(f["L0_ffn_gate_w"].T)
    arrays["e1"] = np.ascontiguousarray(np.concatenate([f["L0_ffn_ew1"].transpose(0, 2, 1), f["L0_ffn_fc1"].T[None]]))
    arrays["e3"] = np.ascontiguousarray(np.concatenate([f["L0_ffn_ew3"].transpose(0, 2, 1), f["L0_ffn_fc2"].T[None]]))
    arrays["e2"] = np.ascontiguousarray(np.concatenate([f["L0_ffn_ew2"].transpose(0, 2, 1), f["L0_ffn_fc3"].T[None]]))
    arrays.update(shape_constants())

    nc = bacc.Bacc("TRN2", target_bir_lowering=False, num_devices=1)
    io = {n: nc.dram_tensor(f"in_{n}", a.shape, mybir.dt.from_np(a.dtype), kind="ExternalInput").ap() for n, a in arrays.items()}
    out = nc.dram_tensor("out", (B, T, D), F32, kind="ExternalOutput").ap()
    decoder_layer(nc, io, out)
    r = run_bass_kernel_spmd(nc, [{f"in_{n}": a for n, a in arrays.items()}], core_ids=[0])
    return r.results[0]["out"]
```

```python
from contextlib import ExitStack

import numpy as np

import concourse.bass as bass
from concourse import mybir

ALU = mybir.AluOpType
ACT = mybir.ActivationFunctionType
F32 = mybir.dt.float32
F32R = mybir.dt.float32r
BF16 = mybir.dt.bfloat16
I32 = mybir.dt.int32
AX = mybir.AxisListType.X

P = 128
B, T, D = 32, 112, 256
S2 = 375
HEADS, HD = 16, 16
FF = 512
NE, EW = 6, 256
GB = 4
G = B // GB
GT = GB * T
DC = D // P
FC = FF // P
KC = 3
KP = S2 // KC
S2E = S2 + 1
HPG = DC * (NE + 1)
FRONT = 4
LEVELS = (2, 4, 8, 16, 32, 64)
SLOTS = KC * HEADS // 4
PROBS = 4
BIG = float(2 ** 40)
ROWS = 3 * HD
STAGES = 4
RB = 3
ROUNDS = (B - 3) // RB
DENSE = (3, 7)
HPB = 4
LN_EPS, RMS_EPS = 1e-5, 1e-6

M_SLNEG, M_SUNEG, M_LE, M_B1, M_BT = 0, 1, 2, 3, 4
N_MASKS = 5 + len(LEVELS)


def shape_constants():
    t = np.arange(T)
    row, col = t[:, None], t[None, :]
    masks = np.zeros((T, N_MASKS, T), np.float32)
    masks[:, M_SLNEG] = np.where(col < row, -1.0, 0.0)
    masks[:, M_SUNEG] = np.where(col > row, -1.0, 0.0)
    masks[:, M_LE] = row <= col
    for n, b in enumerate((1,) + LEVELS):
        quarter = (row // (2 * b) == col // (2 * b)) & (row % (2 * b) >= b) & (col % (2 * b) < b)
        if b == 1:
            masks[:, M_B1] = quarter
        masks[:, M_BT + n] = quarter.T
    keep = np.ones((P, GT), np.float32)
    keep[:, ::T] = 0.0
    return {"masks": masks, "ident": np.eye(P, dtype=np.float32), "keep": keep}


def decoder_layer(nc, io, out):
    with ExitStack() as ctx:
        def sb_in(scope):
            return lambda name, shape, dt=F32: scope.enter_context(nc.sbuf_tensor(name, shape, dt))

        def sem(name):
            return ctx.enter_context(nc.semaphore(name))

        sb = sb_in(ctx)
        psum = ctx.enter_context(nc.psum_tensor("psum", [P, 8, 512], F32))
        bank = [psum[:, i, :] for i in range(8)]

        x = sb("x_res", [T, B, D])
        ident = sb("ident_sb", [P, P])
        pcol = sb("pcol", [P, 4, DC])
        alpha = sb("alpha", [P, 2, DC])
        betab = sb("betab", [T, 2])
        gateb = sb("gateb", [T, NE])
        half = sb("neg_half", [T, 2, GB])
        xwq = sb("xwq_sb", [P, DC, D])
        xwk = sb("xwk_sb", [P, DC, D])
        xwv = sb("xwv_sb", [P, DC, D])
        xwo = sb("xwo_sb", [P, DC, D])
        router = sb("router_sb", [P, DC, NE])
        stage = sb("stage", [P, STAGES, DC, EW])
        stats = sb("stats", [T, GB, 6])
        mv = sb("mv", [T, GB, 2])
        rs = sb("rs", [T, 2, GB])
        small = sb("small", [T, 6, GB])

        with ExitStack() as scope:
            w1 = sb_in(scope)
            masks = w1("masks_sb", [T, N_MASKS, T])
            keep = w1("keep_sb", [P, GT])
            decay = w1("decay", [P, DC, GT])
            wparts = {}
            for name, chunks, width in (("q", DC, D), ("k", DC, D), ("v", DC, D), ("o", DC, D), ("gate", DC, FF), ("up", DC, FF), ("down", FC, D)):
                wparts[name] = tuple(w1(f"w{name}_{part}", [P, chunks, width], F32R) for part in ("hi", "lo"))
            wbeta = w1("wbeta", [T, D])
            xn = w1("xn", [T, GB, D])
            h = w1("h", [T, GB, D])
            h2n = w1("h2n", [T, GB, D])
            hThi = w1("hThi", [P, DC, GT], F32R)
            hTlo = w1("hTlo", [P, DC, GT], F32R)
            h2Thi = w1("h2Thi", [P, DC, GT], F32R)
            h2Tlo = w1("h2Tlo", [P, DC, GT], F32R)
            blogit = w1("blogit", [T, GB])
            bjunk = w1("bjunk", [T, 2, D])
            qT = w1("qT", [P, DC, GT])
            va = w1("va", [P, DC, GT])
            vs = w1("vs", [P, DC, GT])
            kt = w1("kt", [T, GB, D])
            kT = w1("kT", [P, DC, GT])
            vt = w1("vt", [T, GB, D])
            neg = w1("neg", [T, GB, T])
            negT = w1("negT", [T, GB, T])
            cT = w1("cT", [T, len(LEVELS), GB, T])
            tri = w1("tri", [T, GB, T])
            triT = w1("triT", [T, GB, T])
            xq = w1("xq", [T, GB, T])
            aT = w1("aT", [T, GB, T])
            y = w1("y", [T, GB, D])
            oThi = w1("oThi", [P, DC, GT], F32R)
            oTlo = w1("oTlo", [P, DC, GT], F32R)
            x1 = w1("x1", [T, GB, D])
            sg = w1("sg", [P, 2, GT])
            hid = w1("hid", [P, 2, GT])
            hidhi = w1("hidhi", [P, FC, GT], F32R)
            hidlo = w1("hidlo", [P, FC, GT], F32R)
        with ExitStack() as scope:
            w2 = sb_in(scope)
            ctxT = w2("ctxT", [P, RB, DC, S2])
            maskq = w2("maskq", [T, RB, S2], I32)
            maskk = w2("maskk", [KP, RB, KC, T], I32)
            biasq = w2("biasq", [T, RB, S2])
            flagk = w2("flagk", [KP, RB, KC, T], BF16)
            negbig = w2("negbig", [KP, KP], BF16)
            h2 = w2("h2", [T, D])
            h2T = w2("h2T", [P, DC, T])
            qhi = w2("qhi", [P, DC, T], F32R)
            qlo = w2("qlo", [P, DC, T], F32R)
            khi = w2("khi", [P, DC, S2E], F32R)
            klo = w2("klo", [P, DC, S2E], F32R)
            qst = [w2(f"qst{i}", [ROWS + 1, HEADS // DC, DC, T], F32R) for i in range(RB)]
            kst = [w2(f"kst{i}", [ROWS + 1, HEADS // DC, DC, S2E], F32R) for i in range(RB)]
            vaug = [w2(f"vaug{i}", [KP, KC, HEADS, 2 * HD]) for i in range(RB)]
            smax = w2("smax", [T, HEADS // DC, DC])
            junk = w2("junk", [T, 2, S2])
            negm = w2("negm", [HEADS, T], F32R)
            pr = [w2(f"pr{i}", [KP, HPB, T]) for i in range(PROBS)]
            pv = w2("pv", [P, HPB * T])
            rden = w2("rden", [T, HEADS, 1])
            on = w2("on", [T, HEADS, HD])
            onT = w2("onT", [P, DC, T])
        with ExitStack() as scope:
            w3 = sb_in(scope)
            h3 = w3("h3", [T, GB, D])
            h3hi = w3("h3hi", [P, DC, GT], F32R)
            h3lo = w3("h3lo", [P, DC, GT], F32R)
            ehi = [w3(f"ehi{i}", [P, NE + 1, DC, EW], F32R) for i in range(3)]
            elo = [w3(f"elo{i}", [P, NE + 1, DC, EW], F32R) for i in range(3)]
            rhi = w3("rhi", [P, DC, NE], F32R)
            rlo = w3("rlo", [P, DC, NE], F32R)
            logit = w3("logit", [T, GB, NE])
            prob = w3("prob", [T, GB, NE])
            cmp1 = w3("cmp1", [T, GB, NE, NE])
            rank = w3("rank", [T, GB, NE])
            wsum = w3("wsum", [T, GB, 1])
            gate = w3("gate", [T, GB, NE])
            sg3 = w3("sg3", [P, 2, GT])
            hid3 = w3("hid3", [P, 2, GT])
            hid3hi = w3("hid3hi", [P, 2, DC, GT], F32R)
            hid3lo = w3("hid3lo", [P, 2, DC, GT], F32R)

        apart = {nc.gpsimd.engine: sem("pool_waited"), nc.vector.engine: sem("dve_waited")}
        names = """x_in0 x_in w_in2 router_in c_in c_in2 setup_pool setup_act setup_dve alpha_t alpha_d w_hi w_lo
            bn1 var1 rs1 xn1 h1 blog ht_ps ht_hi ht_lo q_ps k_ps v_ps q_sb va_sb v_scan tanh_b ksq kscale_a kscale_b kscale_c kscale
            kt_sb kT_ps vt_ps kT_sb vt_sb gram_ps aq_ps negs cmask tri0a tri0 aT_sb
            xps xsb tps_t tps_tt tri_up triT_up y_ps y_sb oT_ps oT_hi oT_lo wo_ps x1_sb x1_sq rms_a rms x_plus h2_sb h2t_ps h2t_hi h2t_lo
            g_ps u_ps silu hid hid_hi hid_lo down_ps x_mlp""".split()
        s = {n: sem(n) for n in names + [f"stage{i}" for i in range(STAGES)]}
        s2 = {n: sem("c_" + n) for n in """ctx0 ctx1 ctx2 ready bn flags stat rs h hT_ps hT_sb q_ps q_hi q_lo k_ps k_hi k_lo v01_ps v_ps v_sb qst0 qst1 qst2 kst0 kst1 kst2
            max_ps smax mt_ps negm negm_in sc_ps exp pv_done pv_ps pv_sb ot_ps rden on onT_ps onT_sb wo_ps x_new""".split()}
        s3 = {n: sem("e_" + n) for n in """bn stat rs h ht_ps ht_hi ht_lo lg_ps logit ex prob cmp rank sel wsum gate g_ps u_ps silu hid hid_hi hid_lo d_ps x_new x_out r_hi r_lo w_hi w_lo""".split()}
        block = ctx.enter_context(nc.Block())

        def cols(j, width=T):
            return slice(j * width, (j + 1) * width)

        def head(stack, hd):
            return stack[:, hd % (HEADS // DC), hd // (HEADS // DC)]

        def down_bank(e):
            return 0 if e < NE else 6

        def over_rows(mask):
            return masks[:, mask, :].unsqueeze(1).broadcast_to([T, GB, T])

        def wait_apart(eng, semaphore, value):
            eng.wait_ge(semaphore, value)
            eng.sem_inc(apart[eng.engine], 1)

        def ahead(t, par, rows):
            return t + (par + rows) // RB, (par + rows) % RB

        def filled(t):
            return t * 48 + 48

        def split_weights():
            pieces = []
            for name, arg, norm in (("q", "L0_attn_Wq", 0), ("k", "L0_attn_Wk", 0), ("v", "L0_attn_Wv", 0), ("o", "L0_attn_Wo", None),
                                    ("gate", "L0_attn_w_gate", 1), ("up", "L0_attn_w_up", 1)):
                src = io[arg].rearrange("(c p) n -> p c n", p=P)
                for n in range(src.shape[2] // D):
                    pieces.append((src[:, :, cols(n, D)], [w[:, :, cols(n, D)] for w in wparts[name]], norm))
            src = io["L0_attn_w_down"].rearrange("(c p) n -> p c n", p=P)
            for n in range(FC // DC):
                pieces.append((src[:, cols(n, DC)], [w[:, cols(n, DC)] for w in wparts["down"]], None))
            return pieces

        pieces = split_weights()
        PIECES = len(pieces)
        READY = {"v": 3, "o": 4, "up": PIECES - FC // DC, "down": PIECES}

        def is_row(b, row):
            return isinstance(b, int) and b == row

        @block.sync
        def _(sp):
            def load_x(g, done):
                sp.dma_start(x[:, g * GB:(g + 1) * GB, :], io["x"][g * GB:(g + 1) * GB].rearrange("b t d -> t b d")).then_inc(s[done], 16)

            def load_piece(k):
                if k >= STAGES:
                    sp.wait_ge(s["w_lo"], k - STAGES + 1)
                sp.dma_start(stage[:, k % STAGES], pieces[k][0]).then_inc(s[f"stage{k % STAGES}"], 16)

            load_x(0, "x_in0")
            for k in range(STAGES):
                load_piece(k)
            for g in range(1, G):
                load_x(g, "x_in")
            for k in range(STAGES, PIECES):
                load_piece(k)
            for tile, name in ((xwq, "xwq"), (xwk, "xwk"), (xwv, "xwv"), (xwo, "xwo")):
                sp.dma_start(tile[:], io[name].rearrange("(c p) n -> p c n", p=P)).then_inc(s["w_in2"], 16)
            sp.dma_start(router[:], io["router"].rearrange("(c p) n -> p c n", p=P)).then_inc(s["router_in"], 16)

            def load_expert(k):
                n = PIECES + k
                sp.dma_start(stage[:, n % STAGES], io[("e1", "e3", "e2")[k % 3]][k // 3].rearrange("(c p) n -> p c n", p=P)).then_inc(s[f"stage{n % STAGES}"], 16)

            sp.wait_ge(s["w_lo"], PIECES)
            for k in range(STAGES):
                load_expert(k)
            sp.wait_ge(s["x_mlp"], G)

            def load_context(t, par):
                b = t * RB + par
                if not isinstance(b, int) or b >= RB:
                    sp.wait_ge(s2["v_ps"], b - RB + 1)
                    sp.wait_ge(s2["flags"], b - RB + 1)
                ready = s2[f"ctx{par}"]
                sp.dma_start(ctxT[:, par], io["ctxT"][bass.ds(b, 1)].rearrange("a (c p) k -> p (a c) k", p=P)).then_inc(ready, 16)
                sp.dma_start(maskq[:, par, :], io["mask"][bass.ds(b, 1)].rearrange("a q k -> (a q) k")).then_inc(ready, 16)
                sp.dma_start(maskk[:, par], io["maskT"][bass.ds(b, 1)].rearrange("a (c p) q -> p (a c) q", p=KP)).then_inc(ready, 16)

            def spread_heads(t, par):
                b = t * RB + par
                for tile, src, r, ready, count, done in ((kst, khi, 0, "k_hi", DC, "kst"), (kst, khi, 2, "k_hi", DC, "kst"), (kst, klo, 1, "k_lo", DC, "kst"),
                                                         (qst, qhi, 0, "q_hi", 1, "qst"), (qst, qhi, 1, "q_hi", 1, "qst"), (qst, qlo, 2, "q_lo", 1, "qst")):
                    sp.wait_ge(s2[ready], count * (b + 1))
                    dst = tile[par][r * HD:(r + 1) * HD]
                    sp.dma_start(dst.bitcast(F32), src[:].bitcast(F32)).then_inc(s2[f"{done}{par}"], 16)

            def spread_max(t, par):
                b = t * RB + par
                sp.wait_ge(s2["negm"], b + 1)
                sp.dma_start(qst[par][ROWS:ROWS + 1].bitcast(F32), negm[:].bitcast(F32)).then_inc(s2["negm_in"], 16)

            def step(t, par, load=True, heads=True):
                if load:
                    load_context(*ahead(t, par, 3))
                if heads:
                    spread_heads(*ahead(t, par, 2))
                spread_max(*ahead(t, par, 1))

            for par in range(RB):
                load_context(0, par)
            sp.wait_ge(s2["ready"], 1)
            spread_heads(0, 0)
            spread_heads(0, 1)
            spread_max(0, 0)
            with sp.Fori(0, ROUNDS) as t:
                for par in range(RB):
                    step(t, par)
            step(ROUNDS, 0, load=ROUNDS * RB + 3 < B)
            step(ROUNDS, 1, load=ROUNDS * RB + 4 < B)
            step(ROUNDS, 2, load=False)
            step(ROUNDS + 1, 0, load=False, heads=False)

            for k in range(STAGES, 3 * (NE + 1)):
                sp.wait_ge(s3["w_lo"], k - STAGES + 1)
                load_expert(k)
            with sp.Fori(0, G) as g:
                sp.wait_ge(s3["x_new"], (g + 1) * (NE + 1))
                sp.dma_start(out[bass.ds(g * GB, GB)].rearrange("b t d -> t b d"), x[:, bass.ds(g * GB, GB), :]).then_inc(s3["x_out"], 16)
            sp.wait_ge(s3["x_out"], 16 * G)

        @block.gpsimd
        def _(pool):
            pool.dma_start(betab[:, 0:1], io["L0_attn_beta_b"].partition_broadcast(T)).then_inc(s["c_in2"], 16)
            pool.dma_start(wbeta[:], io["beta_row"].partition_broadcast(T)).then_inc(s["c_in2"], 16)
            pool.dma_start(bjunk[:, 0], io["norm1_row"].partition_broadcast(T)).then_inc(s["c_in2"], 16)
            pool.dma_start(keep[:], io["keep"]).then_inc(s["c_in2"], 16)
            pool.dma_start(masks[:], io["masks"]).then_inc(s["c_in2"], 16)
            pool.dma_start(gateb[:], io["L0_ffn_gate_b"].partition_broadcast(T)).then_inc(s["c_in2"], 16)
            nc.gpsimd.memset(half[:, 0, :], -0.5)
            nc.gpsimd.memset(half[:, 1, :], 0.5).then_inc(s["setup_pool"], 1)
            pool.wait_ge(s["setup_pool"], 1)

            def powers(g):
                pool.wait_ge(s["var1"], g + 1)
                nc.gpsimd.tensor_tensor(rs[:], rs[:], half[:, 0:1, :].broadcast_to([T, 2, GB]), op=ALU.pow).then_inc(s["rs1"], 1)

            def step(g, ahead=True):
                wait_apart(pool, s["tanh_b"], g + 1)
                nc.gpsimd.tensor_scalar(small[:, 0], small[:, 0], 0.5, 0.5, ALU.mult, ALU.add).then_inc(s["kscale_a"], 1)
                pool.wait_ge(s["kscale_a"], g + 1)
                nc.gpsimd.tensor_tensor(small[:, 1], small[:, 0], half[:, 1, :], op=ALU.pow)
                wait_apart(pool, s["ksq"], g + 1)
                nc.gpsimd.tensor_scalar(small[:, 2], small[:, 2], 1e-24, None, ALU.max).then_inc(s["kscale_b"], 1)
                pool.wait_ge(s["kscale_b"], g + 1)
                nc.gpsimd.tensor_tensor(small[:, 3], small[:, 2], half[:, 0, :], op=ALU.pow).then_inc(s["kscale_c"], 1)
                pool.wait_ge(s["kscale_c"], g + 1)
                nc.gpsimd.tensor_tensor(small[:, 4], small[:, 3], small[:, 1], op=ALU.mult).then_inc(s["kscale"], 1)
                pool.wait_ge(s["negs"], g + 1)
                for n in range(len(LEVELS)):
                    nc.gpsimd.tensor_tensor(cT[:, n], negT[:], over_rows(M_BT + 1 + n), op=ALU.mult).then_inc(s["cmask"], 1)
                    if n == 1 and ahead:
                        powers(g + 1)
                wait_apart(pool, s["x1_sq"], g + 1)
                nc.gpsimd.tensor_scalar(small[:, 5], small[:, 5], 1.0 / D, RMS_EPS, ALU.mult, ALU.add).then_inc(s["rms_a"], 1)
                pool.wait_ge(s["rms_a"], g + 1)
                nc.gpsimd.tensor_tensor(small[:, 5], small[:, 5], half[:, 0, :], op=ALU.pow).then_inc(s["rms"], 1)
                nc.gpsimd.tensor_tensor(x[:, bass.ds(g * GB, GB), :], x[:, bass.ds(g * GB, GB), :], x1[:], op=ALU.add).then_inc(s["x_plus"], 1)

            powers(0)
            step(0)
            with pool.Fori(1, G - 1) as g:
                step(g)
            step(G - 1, ahead=False)

            pool.wait_ge(s["x_mlp"], G)
            for i in range(RB):
                nc.gpsimd.memset(kst[i][:].bitcast(F32), 1.0)
                nc.gpsimd.memset(vaug[i][:], 1.0)
            for part in (khi, klo):
                nc.gpsimd.memset(part[:, :, S2:S2E].bitcast(F32), 0.0)
            nc.gpsimd.tensor_scalar(negbig[:], ident[0:KP, 0:KP], -BIG, None, ALU.mult).then_inc(s2["ready"], 1)

            def mask_bias(t, par):
                b = t * RB + par
                if not isinstance(b, int) or b >= RB:
                    pool.wait_ge(s2["sc_ps"], SLOTS * (b - RB + 1))
                wait_apart(pool, s2[f"ctx{par}"], filled(t))
                nc.gpsimd.tensor_scalar(biasq[:, par, :], maskq[:, par, :], 1.0, -BIG, ALU.is_equal, ALU.mult)
                nc.gpsimd.tensor_scalar(flagk[:, par], maskk[:, par], 1.0, None, ALU.is_equal).then_inc(s2["flags"], 1)

            def rsqrt(t, par):
                pool.wait_ge(s2["stat"], t * RB + par + 1)
                nc.gpsimd.tensor_tensor(rs[:, 0, 0:1], rs[:, 0, 0:1], half[:, 0, 0:1], op=ALU.pow).then_inc(s2["rs"], 1)

            def step(t, par, power=True):
                mask_bias(*ahead(t, par, 2))
                if power:
                    rsqrt(*ahead(t, par, 3))

            for par in range(2):
                rsqrt(0, par)
                mask_bias(0, par)
            rsqrt(0, 2)
            step(0, 0)
            step(0, 1)
            step(0, 2)
            with pool.Fori(1, ROUNDS) as t:
                for par in range(RB):
                    step(t, par)
            for par in range(RB):
                step(ROUNDS, par, power=ROUNDS * RB + par + 3 < B)

            def rsqrt_group(g):
                pool.wait_ge(s3["stat"], g + 1)
                nc.gpsimd.tensor_tensor(rs[:, 0, :], rs[:, 0, :], half[:, 0, :], op=ALU.pow).then_inc(s3["rs"], 1)

            pool.wait_ge(s2["x_new"], B)
            rsqrt_group(0)
            pool.wait_ge(s["router_in"], 16)
            nc.gpsimd.tensor_copy(rhi[:], router[:]).then_inc(s3["r_hi"], 1)
            pool.wait_ge(s3["r_hi"], 1)
            nc.gpsimd.tensor_tensor(rlo[:], router[:], rhi[:].bitcast(F32), op=ALU.subtract).then_inc(s3["r_lo"], 1)
            for k in range(3 * (NE + 1)):
                n = PIECES + k
                pool.wait_ge(s[f"stage{n % STAGES}"], 16 * (n // STAGES + 1))
                nc.gpsimd.tensor_copy(ehi[k % 3][:, k // 3], stage[:, n % STAGES]).then_inc(s3["w_hi"], 1)
                pool.wait_ge(s3["w_hi"], k + 1)
                nc.gpsimd.tensor_tensor(elo[k % 3][:, k // 3], stage[:, n % STAGES], ehi[k % 3][:, k // 3].bitcast(F32), op=ALU.subtract).then_inc(s3["w_lo"], 1)
                if k == 3 * FRONT + 2:
                    rsqrt_group(1)
            with pool.Fori(2, G) as g:
                rsqrt_group(g)

        @block.tensor
        def _(pe):
            def transpose_in(src, b0, b1, done, last=True):
                for c in range(DC):
                    for j in range(GB):
                        mm = pe.transpose(bank[b0 if c == 0 else b1][:, cols(j)], src[:, j, cols(c, P)], ident[0:T, 0:T])
                mm.then_inc(done, 1)

            pe.wait_ge(s["c_in"], 16 * 4)

            def split_products(to, pairs):
                pairs = list(pairs)
                products = [(st[a], mv[b]) for a, b in ((0, 0), (0, 1), (1, 0)) for st, mv in pairs]
                for n, (st, mv) in enumerate(products):
                    mm = pe.matmul(to, st, mv, start=n == 0, stop=n == len(products) - 1)
                return mm

            def weight_cols(name, m):
                return [tuple(w[:, c, cols(m, P)] for w in wparts[name]) for c in range(DC)]

            def token_cols(parts, j, chunks=DC):
                return [tuple(part[:, c, cols(j)] for part in parts) for c in range(chunks)]

            def chunks_of(parts, chunks=DC):
                return [tuple(part[:, c] for part in parts) for c in range(chunks)]

            def transpose_h1(g):
                pe.wait_ge(s["h1"], g + 1)
                if not (isinstance(g, int) and g == 0):
                    pe.wait_ge(s["aT_sb"], g)
                    if not (isinstance(g, int) and g == 1):
                        pe.wait_ge(s["x_mlp"], g - 1)
                transpose_in(h, 4, 5, s["ht_ps"])

            def project_q1(g):
                pe.wait_ge(s["ht_lo"], g + 1)
                for m in range(DC):
                    mm = split_products(bank[2 + m][:, 0:GT], zip(weight_cols("q", m), chunks_of((hThi, hTlo))))
                mm.then_inc(s["q_ps"], 1)

            def project_k1(g):
                for j in range(GB):
                    mm = split_products(bank[4 + j // 2][0:T, cols(j % 2, D)], zip(token_cols((hThi, hTlo), j), chunks_of(wparts["k"])))
                mm.then_inc(s["k_ps"], 1)

            def project_v1(g):
                if not (isinstance(g, int) and g == 0):
                    pe.wait_ge(s["x1_sb"], g)
                for m in range(DC):
                    mm = split_products(bank[m][:, 0:GT], zip(weight_cols("v", m), chunks_of((hThi, hTlo))))
                mm.then_inc(s["v_ps"], 1)

            def transpose_h2(p):
                pe.wait_ge(s["h2_sb"], p + 1)
                transpose_in(h2n, 6, 7, s["h2t_ps"])

            def gate_up(p, m):
                if m == 0:
                    pe.wait_ge(s["h2t_lo"], p + 1)
                elif m == 1:
                    if not (isinstance(p, int) and p == G - 1):
                        pe.wait_ge(s["negs"], p + 2)
                        pe.wait_ge(s["aT_sb"], p + 2)
                else:
                    pe.wait_ge(s["hid"], FC * p + m)
                for name, b0, done in (("gate", 0, "g_ps"), ("up", 1, "u_ps")):
                    split_products(bank[(6 if m == 0 else 4) + b0][:, 0:GT], zip(weight_cols(name, m), chunks_of((h2Thi, h2Tlo)))).then_inc(s[done], 1)

            def mlp_down(p):
                pe.wait_ge(s["hid_lo"], FC * (p + 1))
                for j in range(GB):
                    mm = split_products(bank[4 + j // 2][0:T, cols(j % 2, D)], zip(token_cols((hidhi, hidlo), j, FC), chunks_of(wparts["down"], FC)))
                mm.then_inc(s["down_ps"], 1)

            def keys_values(g):
                pe.wait_ge(s["kt_sb"], g + 1)
                pe.wait_ge(s["q_sb"], g + 1)
                transpose_in(kt, 2, 3, s["kT_ps"])
                pe.wait_ge(s["v_scan"], g + 1)
                for j in range(GB):
                    for c in range(DC):
                        mm = pe.transpose(bank[j // 2][0:T, (j % 2) * D + c * P:(j % 2) * D + (c + 1) * P], vs[:, c, cols(j)], ident[:])
                mm.then_inc(s["vt_ps"], 1)
                pe.wait_ge(s["kT_sb"], g + 1)
                for j in range(GB):
                    for c in range(DC):
                        mm = pe.matmul(bank[4][0:T, cols(j)], kT[:, c, cols(j)], kT[:, c, cols(j)], start=c == 0, stop=c == DC - 1)
                mm.then_inc(s["gram_ps"], 1)
                for j in range(GB):
                    for c in range(DC):
                        mm = pe.matmul(bank[5][0:T, cols(j)], kT[:, c, cols(j)], qT[:, c, cols(j)], start=c == 0, stop=c == DC - 1)
                mm.then_inc(s["aq_ps"], 1)

            def double(g, n, mlp):
                for u in range(2):
                    it = 2 * n + u
                    pe.wait_ge(s["cmask"], len(LEVELS) * g + n + 1)
                    if n == 0:
                        pe.wait_ge(s["tri0"], g + 1)
                        pe.wait_ge(s["vt_sb"], g + 1)
                        if mlp:
                            pe.wait_ge(s["hid"], FC * (g - 1) + 1)
                    else:
                        pe.wait_ge(s["tri_up"], 2 * (len(LEVELS) - 1) * g + it - 1)
                    for j in (2 * u, 2 * u + 1):
                        mm = pe.matmul(bank[6 + u][0:T, cols(j % 2)], cT[:, n, j], tri[:, j], start=True, stop=True)
                    mm.then_inc(s["xps"], 1)
                for u in range(2):
                    it = 2 * n + u
                    pe.wait_ge(s["xsb"], 2 * len(LEVELS) * g + it + 1)
                    if n > 0:
                        pe.wait_ge(s["triT_up"], 2 * len(LEVELS) * g + it - 1)
                    if n < len(LEVELS) - 1:
                        for j in (2 * u, 2 * u + 1):
                            mm = pe.matmul(bank[u][0:T, cols(j % 2)], triT[:, j], xq[:, j], start=True, stop=True)
                        mm.then_inc(s["tps_t"], 1)
                    for j in (2 * u, 2 * u + 1):
                        mm = pe.matmul(bank[2 + u][0:T, cols(j % 2)], xq[:, j], triT[:, j], start=True, stop=True)
                    mm.then_inc(s["tps_tt"], 1)

            def solve_values(g):
                pe.wait_ge(s["triT_up"], 2 * len(LEVELS) * (g + 1))
                for j in range(GB):
                    mm = pe.matmul(bank[j // 2][0:T, cols(j % 2, D)], triT[:, j], vt[:, j], start=True, stop=True)
                mm.then_inc(s["y_ps"], 1)

            def attend(g):
                pe.wait_ge(s["y_sb"], g + 1)
                pe.wait_ge(s["aT_sb"], g + 1)
                for c in range(DC):
                    for j in range(GB):
                        mm = pe.matmul(bank[6 + c][:, cols(j)], y[:, j, cols(c, P)], aT[:, j], start=True, stop=True)
                mm.then_inc(s["oT_ps"], 1)

            def project_o(g):
                pe.wait_ge(s["oT_lo"], g + 1)
                for j in range(GB):
                    mm = split_products(bank[j // 2][0:T, cols(j % 2, D)], zip(token_cols((oThi, oTlo), j), chunks_of(wparts["o"])))
                mm.then_inc(s["wo_ps"], 1)

            def step(g, mlp=True, ahead=True):
                p = g - 1
                project_k1(g)
                project_v1(g)
                if mlp:
                    transpose_h2(p)
                keys_values(g)
                if mlp:
                    gate_up(p, 0)
                for n in range(len(LEVELS)):
                    double(g, n, mlp)
                    if mlp and n < FC - 1:
                        gate_up(p, n + 1)
                    if mlp and n == FC - 1:
                        mlp_down(p)
                solve_values(g)
                if ahead:
                    transpose_h1(g + 1)
                attend(g)
                if ahead:
                    project_q1(g + 1)
                project_o(g)

            pe.wait_ge(s["w_lo"], READY["v"])
            transpose_h1(0)
            project_q1(0)
            pe.wait_ge(s["w_lo"], READY["down"])
            step(0, mlp=False)
            with pe.Fori(1, G - 1) as g:
                step(g)
            step(G - 1, ahead=False)
            transpose_h2(G - 1)
            for m in range(FC):
                gate_up(G - 1, m)
            mlp_down(G - 1)

            pe.wait_ge(s["w_in2"], 16 * 4)
            pe.nop().then_inc(s2["pv_done"], PROBS)

            def project_k(t, par, m):
                f = t * RB + par
                if m == 0:
                    pe.wait_ge(s2[f"ctx{par}"], filled(t))
                    if not is_row(f, 0):
                        pe.wait_ge(s2["v_sb"], 2 * f)
                for c in range(DC):
                    mm = pe.matmul(bank[DENSE[m]][:, 0:S2], xwk[:, c, cols(m, P)], ctxT[:, par, c], start=c == 0, stop=c == DC - 1)
                mm.then_inc(s2["k_ps"], 1)

            def transpose_h(t, par):
                f = t * RB + par
                pe.wait_ge(s2["h"], f + 1)
                pe.wait_ge(s2["k_lo"], DC * (f + 1))
                for c in range(DC):
                    mm = pe.transpose(bank[DENSE[1]][:, cols(c)], h2[:, cols(c, P)], ident[0:T, 0:T])
                mm.then_inc(s2["hT_ps"], 1)

            def project_q(t, par):
                f = t * RB + par
                pe.wait_ge(s2["hT_sb"], f + 1)
                for m in range(DC):
                    for c in range(DC):
                        mm = pe.matmul(bank[DENSE[1]][:, (DC + m) * T:(DC + m + 1) * T], xwq[:, c, cols(m, P)], h2T[:, c], start=c == 0, stop=c == DC - 1)
                mm.then_inc(s2["q_ps"], 1)

            def project_v(t, par, part):
                f = t * RB + par
                if part == 0:
                    pe.wait_ge(s2["q_lo"], f + 1)
                elif isinstance(f, int) and f < 2:
                    pe.wait_ge(s2["k_lo"], DC * f + 1)
                else:
                    pe.wait_ge(s2["x_new"], f - 2)
                for c3 in ((0, 1), (2,))[part]:
                    for c in range(DC):
                        mm = pe.matmul(bank[DENSE[1 - part]][0:KP, cols(c3 % 2, D)], ctxT[:, par, c, cols(c3, KP)], xwv[:, c], start=c == 0, stop=c == DC - 1)
                mm.then_inc(s2[("v01_ps", "v_ps")[part]], 1)

            def row_max(t, par, heads):
                n = t * RB + par
                for hd in heads:
                    if hd == 0:
                        pe.wait_ge(s2[f"qst{par}"], filled(t))
                        pe.wait_ge(s2[f"kst{par}"], filled(t))
                        if not is_row(n, 0):
                            pe.wait_ge(s2["negm"], n)
                    if hd >= 2:
                        pe.wait_ge(s2["smax"], HEADS * n + hd - 1)
                    pe.matmul(bank[4 + hd % 2][0:T, 0:S2E], head(qst[par][0:ROWS], hd), head(kst[par][0:ROWS], hd), start=True, stop=True).then_inc(s2["max_ps"], 1)

            def transpose_max(t, par):
                n = t * RB + par
                pe.wait_ge(s2["smax"], HEADS * (n + 1))
                pe.transpose(bank[5][0:HEADS, 0:T], smax[:].rearrange("q h m -> q (h m)"), ident[0:T, 0:T]).then_inc(s2["mt_ps"], 1)

            def mask_scores(t, par, q):
                b = t * RB + par
                if q == 0:
                    pe.wait_ge(s2["negm_in"], 16 * (b + 1))
                    pe.wait_ge(s2["flags"], b + 1)
                pe.wait_ge(s2["exp"], SLOTS * b + q + 1)
                flags = flagk[:, par, q // HPB, :].unsqueeze(1).broadcast_to([KP, HPB, T])
                pe.matmul(bank[q % 3][0:KP, 0:GT], negbig[:], flags, start=True, stop=False, skip_group_check=True)

            def score(t, par, q, i):
                hd = HPB * (q % HPB) + i
                mm = pe.matmul(bank[q % 3][0:KP, cols(i)], head(kst[par], hd)[:, cols(q // HPB, KP)], head(qst[par], hd), start=False, stop=True, skip_group_check=True)
                if i == HPB - 1:
                    mm.then_inc(s2["sc_ps"], 1)

            def weighted_values(t, par, q):
                b = t * RB + par
                c3 = q // HPB
                if q == 0 and not is_row(b, 0):
                    pe.wait_ge(s2["pv_sb"], b)
                pe.wait_ge(s2["exp"], SLOTS * b + q + 4)
                for i in range(HPB):
                    hd = HPB * (q % HPB) + i
                    row = 2 * HD * i
                    mm = pe.matmul(bank[6][row:row + 2 * HD, cols(hd // HPB)], vaug[par][:, c3, hd], pr[q % PROBS][:, i],
                                   start=q == 0, stop=c3 == KC - 1, skip_group_check=True)
                mm.then_inc(s2["pv_done"], 1)

            def transpose_o(t, par):
                p = t * RB + par
                pe.wait_ge(s2["pv_sb"], p + 1)
                if isinstance(p, int) and p >= B - 3:
                    pe.wait_ge(s2["v_sb"], 2 * B)
                    pe.wait_ge(s2["x_new"], p)
                else:
                    pe.wait_ge(s2["k_lo"], DC * (p + 3) + 1)
                for g4 in range(HPB):
                    mm = pe.transpose(bank[DENSE[0]][0:T, cols(g4, P)], pv[:, cols(g4)], ident[:])
                mm.then_inc(s2["ot_ps"], 1)

            def transpose_on(t, par):
                p = t * RB + par
                pe.wait_ge(s2["on"], p + 1)
                for c in range(DC):
                    mm = pe.transpose(bank[DENSE[0]][:, cols(c)], on[:].rearrange("q h d -> q (h d)")[:, cols(c, P)], ident[0:T, 0:T])
                mm.then_inc(s2["onT_ps"], 1)

            def project_out(t, par):
                p = t * RB + par
                pe.wait_ge(s2["onT_sb"], p + 1)
                for c in range(DC):
                    mm = pe.matmul(bank[DENSE[0]][0:T, 0:D], onT[:, c], xwo[:, c], start=c == 0, stop=c == DC - 1)
                mm.then_inc(s2["wo_ps"], 1)

            def step(t, par, first=False, following=2):
                prev, nxt, far = ahead(t, par, -1), ahead(t, par, 1), ahead(t, par, 2)
                for q in range(SLOTS):
                    mask_scores(t, par, q)
                    score(t, par, q, 0)
                    if following >= 1 and q < HEADS // 2:
                        row_max(*nxt, (2 * q,))
                    score(t, par, q, 1)
                    if following >= 1 and q < HEADS // 2:
                        row_max(*nxt, (2 * q + 1,))
                    if q == 9 and following >= 2:
                        project_v(*far, 1)
                    score(t, par, q, 2)
                    if q >= 2:
                        weighted_values(t, par, q - 2)
                    elif not first:
                        weighted_values(*prev, SLOTS - 2 + q)
                    score(t, par, q, 3)
                    if q == 0 and following >= 2:
                        project_k(*far, 0)
                    if q == 1 and following >= 2:
                        project_k(*far, 1)
                    if q == 3 and not first:
                        transpose_o(*prev)
                    if q == 4 and following >= 2:
                        transpose_h(*far)
                    if q == 5 and not first:
                        transpose_on(*prev)
                    if q == 6 and following >= 2:
                        project_q(*far)
                    if q == 7 and not first:
                        project_out(*prev)
                    if q == 8 and following >= 1:
                        transpose_max(*nxt)
                    if q == 8 and following >= 2:
                        project_v(*far, 0)

            for par in range(2):
                project_k(0, par, 0)
                project_k(0, par, 1)
                transpose_h(0, par)
                project_q(0, par)
                project_v(0, par, 0)
                project_v(0, par, 1)
            row_max(0, 0, range(HEADS))
            transpose_max(0, 0)
            for par in range(RB):
                step(0, par, first=par == 0)
            with pe.Fori(1, ROUNDS) as t:
                for par in range(RB):
                    step(t, par)
            for par in range(RB):
                step(ROUNDS, par)
            step(ROUNDS + 1, 0, following=1)
            step(ROUNDS + 1, 1, following=0)
            for q in (SLOTS - 2, SLOTS - 1):
                weighted_values(ROUNDS + 1, 1, q)
            transpose_o(ROUNDS + 1, 1)
            transpose_on(ROUNDS + 1, 1)
            project_out(ROUNDS + 1, 1)

            def expand(g, e):
                for m in range(DC):
                    it = DC * e + m
                    for w, b0, done, left in ((0, 4, "g_ps", "silu"), (1, 6, "u_ps", "hid")):
                        if m == 0:
                            pe.wait_ge(s3["w_lo"], 3 * e + w + 1)
                        if it >= 2:
                            pe.wait_ge(s3[left], HPG * g + it - 1)
                        elif w == 1 and m == 0 and not (isinstance(g, int) and g == 0):
                            pe.wait_ge(s3["x_new"], (NE + 1) * g)
                        parts = [(wp[w][:, e, c, cols(m, P)], hp[:, c]) for wp, hp in ((ehi, h3hi), (elo, h3hi), (ehi, h3lo)) for c in range(DC)]
                        for n, (wp, hp) in enumerate(parts):
                            mm = pe.matmul(bank[b0 + it % 2][:, 0:GT], wp, hp, start=n == 0, stop=n == len(parts) - 1)
                        mm.then_inc(s3[done], 1)

            def contract(g, e):
                pe.wait_ge(s3["w_lo"], 3 * e + 3)
                pe.wait_ge(s3["hid_lo"], HPG * g + DC * (e + 1))
                if 1 <= e < NE:
                    pe.wait_ge(s3["x_new"], (NE + 1) * g + e)
                for j in range(GB):
                    parts = [(hp[:, e % 2, c, cols(j)], wp[2][:, e, c]) for hp, wp in ((hid3hi, ehi), (hid3hi, elo), (hid3lo, ehi)) for c in range(DC)]
                    for n, (hp, wp) in enumerate(parts):
                        mm = pe.matmul(bank[down_bank(e) + j // 2][0:T, cols(j % 2, D)], hp, wp, start=n == 0, stop=n == len(parts) - 1)
                mm.then_inc(s3["d_ps"], 1)

            def transpose_group(g):
                pe.wait_ge(s3["h"], g + 1)
                if not (isinstance(g, int) and g == 0):
                    pe.wait_ge(s3["logit"], g)
                transpose_in(h3, 2, 3, s3["ht_ps"])

            def route(g):
                pe.wait_ge(s3["ht_lo"], g + 1)
                pe.wait_ge(s3["r_lo"], 1)
                for j in range(GB):
                    parts = [(hp[:, c, cols(j)], rp[:, c]) for hp, rp in ((h3hi, rhi), (h3hi, rlo), (h3lo, rhi)) for c in range(DC)]
                    for n, (hp, rp) in enumerate(parts):
                        mm = pe.matmul(bank[2][0:T, cols(j, NE)], hp, rp, start=n == 0, stop=n == len(parts) - 1)
                mm.then_inc(s3["lg_ps"], 1)

            def experts(g, ahead):
                expand(g, 0)
                for e in range(1, NE + 1):
                    expand(g, e)
                    contract(g, e - 1)
                    if ahead and e == FRONT + 1:
                        transpose_group(g + 1)
                contract(g, NE)
                if ahead:
                    route(g + 1)

            transpose_group(0)
            route(0)
            with pe.Fori(0, G - 1) as g:
                experts(g, True)
            experts(G - 1, False)

        @block.scalar
        def _(act):
            act.dma_start(ident[:], io["ident"]).then_inc(s["c_in"], 16)
            for n, name in enumerate(("L0_attn_norm1_w", "L0_attn_norm2_w", "L0_attn_alpha_logit")):
                act.dma_start(pcol[:, n, :], io[name]).then_inc(s["c_in"], 16)
            act.wait_ge(s["c_in"], 16 * 4)
            nc.scalar.activation(pcol[:, 3, :], pcol[:, 2, :], ACT.Tanh, scale=0.5).then_inc(s["alpha_t"], 1)

            def high_weights(k):
                act.wait_ge(s[f"stage{k % STAGES}"], 16 * (k // STAGES + 1))
                (hi, _), norm = pieces[k][1:]
                if norm is None:
                    last = nc.scalar.copy(hi, stage[:, k % STAGES])
                else:
                    for c in range(DC):
                        last = nc.scalar.activation(hi[:, c], stage[:, k % STAGES, c], ACT.Copy, scale=pcol[:, norm, c:c + 1])
                last.then_inc(s["w_hi"], 1)

            def high_h1(g):
                act.wait_ge(s["ht_ps"], g + 1)
                nc.scalar.copy(hThi[:], psum[:, 4:6, 0:GT]).then_inc(s["ht_hi"], 1)

            def copy_q1(g):
                act.wait_ge(s["q_ps"], g + 1)
                nc.scalar.copy(qT[:], psum[:, 2:4, 0:GT]).then_inc(s["q_sb"], 1)

            def high_h2(p):
                act.wait_ge(s["h2t_ps"], p + 1)
                nc.scalar.copy(h2Thi[:], psum[:, 6:8, 0:GT]).then_inc(s["h2t_hi"], 1)

            def silu1(p, m):
                act.wait_ge(s["g_ps"], FC * p + m + 1)
                if m >= 2:
                    act.wait_ge(s["hid"], FC * p + m - 1)
                nc.scalar.activation(sg[:, m % 2], bank[6 if m == 0 else 4][:, 0:GT], ACT.Silu).then_inc(s["silu"], 1)

            def high_hidden1(p, m):
                act.wait_ge(s["hid"], FC * p + m + 1)
                nc.scalar.copy(hidhi[:, m], hid[:, m % 2]).then_inc(s["hid_hi"], 1)

            def step(g, mlp=True, ahead=True):
                p = g - 1
                act.wait_ge(s["k_ps"], g + 1)
                if not (isinstance(g, int) and g == 0):
                    act.wait_ge(s["x1_sq"], g)
                for j in range(GB):
                    last = nc.scalar.activation(kt[:, j], bank[4 + j // 2][0:T, cols(j % 2, D)], ACT.Square, accum_out=small[:, 2, j:j + 1])
                last.then_inc(s["ksq"], 1)
                act.wait_ge(s["blog"], GB * (g + 1))
                nc.scalar.activation(small[:, 0], blogit[:], ACT.Tanh, bias=betab[:, 1:2], scale=0.5).then_inc(s["tanh_b"], 1)
                act.wait_ge(s["v_ps"], g + 1)
                for m in range(DC):
                    last = nc.scalar.activation(va[:, m], bank[m][:, 0:GT], ACT.Copy, scale=alpha[:, 0, m:m + 1])
                last.then_inc(s["va_sb"], 1)
                act.wait_ge(s["kscale"], g + 1)
                act.wait_ge(s["ksq"], g + 1)
                for j in range(GB):
                    last = nc.scalar.activation(kt[:, j], bank[4 + j // 2][0:T, cols(j % 2, D)], ACT.Copy, scale=small[:, 4, j:j + 1])
                last.then_inc(s["kt_sb"], 1)
                if mlp:
                    high_h2(p)
                act.wait_ge(s["kT_ps"], g + 1)
                nc.scalar.copy(kT[:], psum[:, 2:4, 0:GT]).then_inc(s["kT_sb"], 1)
                act.wait_ge(s["vt_ps"], g + 1)
                for j in range(GB):
                    last = nc.scalar.activation(vt[:, j], bank[j // 2][0:T, cols(j % 2, D)], ACT.Copy, scale=small[:, 1, j:j + 1])
                last.then_inc(s["vt_sb"], 1)
                for n in range(len(LEVELS)):
                    if mlp and n < FC:
                        silu1(p, n)
                    for u in range(2):
                        act.wait_ge(s["xps"], 2 * len(LEVELS) * g + 2 * n + u + 1)
                        nc.scalar.copy(xq[:, 2 * u:2 * u + 2], bank[6 + u][0:T, 0:2 * T]).then_inc(s["xsb"], 1)
                    if mlp and n < FC:
                        high_hidden1(p, n)
                act.wait_ge(s["y_ps"], g + 1)
                nc.scalar.copy(y[:].rearrange("t (u j) d -> t u (j d)", u=2), psum[0:T, 0:2, :]).then_inc(s["y_sb"], 1)
                if ahead:
                    high_h1(g + 1)
                act.wait_ge(s["oT_ps"], g + 1)
                nc.scalar.copy(oThi[:], psum[:, 6:8, 0:GT]).then_inc(s["oT_hi"], 1)
                if ahead:
                    copy_q1(g + 1)
                act.wait_ge(s["x1_sb"], g + 1)
                for j in range(GB):
                    last = nc.scalar.activation(kt[:, j], x1[:, j], ACT.Square, accum_out=small[:, 5, j:j + 1])
                last.then_inc(s["x1_sq"], 1)

            for k in range(READY["o"]):
                high_weights(k)
            high_h1(0)
            for k in range(READY["o"], PIECES):
                high_weights(k)
            act.wait_ge(s["c_in2"], 16 * 6)
            nc.scalar.mul(betab[:, 1:2], betab[:, 0:1], 0.5).then_inc(s["setup_act"], 1)
            act.wait_ge(s["setup_act"], 1)
            act.wait_ge(s["alpha_d"], 2)
            copy_q1(0)
            step(0, mlp=False)
            with act.Fori(1, G - 1) as g:
                step(g)
            step(G - 1, ahead=False)
            high_h2(G - 1)
            for m in range(FC):
                silu1(G - 1, m)
                high_hidden1(G - 1, m)

            def high_k(t, par, m):
                f = t * RB + par
                act.wait_ge(s2["k_ps"], DC * f + m + 1)
                if m == 0 and not is_row(f, 0):
                    before = ahead(t, par, -1)
                    act.wait_ge(s2[f"kst{before[1]}"], filled(before[0]))
                    act.wait_ge(s2[f"qst{before[1]}"], filled(before[0]))
                nc.scalar.copy(khi[:, m, 0:S2], bank[DENSE[m]][:, 0:S2]).then_inc(s2["k_hi"], 1)

            def copy_h(t, par):
                act.wait_ge(s2["hT_ps"], t * RB + par + 1)
                nc.scalar.copy(h2T[:], bank[DENSE[1]][:, 0:2 * T]).then_inc(s2["hT_sb"], 1)

            def high_q(t, par):
                act.wait_ge(s2["q_ps"], t * RB + par + 1)
                nc.scalar.copy(qhi[:], bank[DENSE[1]][:, 2 * T:4 * T]).then_inc(s2["q_hi"], 1)

            def copy_v(t, par, part):
                act.wait_ge(s2[("v01_ps", "v_ps")[part]], t * RB + par + 1)
                if part == 0:
                    nc.scalar.copy(vaug[par][:, 0:2, :, 0:HD], bank[DENSE[1]][0:KP, :].rearrange("k (c h d) -> k c h d", c=2, d=HD)).then_inc(s2["v_sb"], 1)
                else:
                    nc.scalar.copy(vaug[par][:, 2, :, 0:HD], bank[DENSE[0]][0:KP, 0:D].rearrange("k (h d) -> k h d", d=HD)).then_inc(s2["v_sb"], 1)

            def negate_max(t, par):
                act.wait_ge(s2["mt_ps"], t * RB + par + 1)
                nc.scalar.mul(negm[:], bank[5][0:HEADS, 0:T], -1.0).then_inc(s2["negm"], 1)

            def exponentials(t, par, q):
                done = SLOTS * (t * RB + par) + q
                act.wait_ge(s2["sc_ps"], done + 1)
                act.wait_ge(s2["pv_done"], done + 1)
                nc.scalar.activation(pr[q % PROBS][:].rearrange("k i q -> k (i q)"), bank[q % 3][0:KP, 0:GT], ACT.Exp, scale=1.0 / HD ** 0.5).then_inc(s2["exp"], 1)

            def copy_pv(t, par):
                p = t * RB + par
                act.wait_ge(s2["pv_done"], SLOTS * (p + 1) + PROBS)
                nc.scalar.copy(pv[:], bank[6][:, 0:GT]).then_inc(s2["pv_sb"], 1)

            def copy_on(t, par):
                act.wait_ge(s2["onT_ps"], t * RB + par + 1)
                nc.scalar.copy(onT[:], bank[DENSE[0]][:, 0:2 * T]).then_inc(s2["onT_sb"], 1)

            def step(t, par, first=False, following=2):
                prev, nxt, far = ahead(t, par, -1), ahead(t, par, 1), ahead(t, par, 2)
                for q in range(SLOTS):
                    exponentials(t, par, q)
                    if q == 0 and following >= 2:
                        high_k(*far, 0)
                    if q == 1:
                        if not first:
                            copy_pv(*prev)
                        if following >= 2:
                            high_k(*far, 1)
                    if q == 4 and following >= 2:
                        copy_h(*far)
                    if q == 5 and not first:
                        copy_on(*prev)
                    if q == 6 and following >= 2:
                        high_q(*far)
                    if q == 8 and following >= 1:
                        negate_max(*nxt)
                    if q == 8 and following >= 2:
                        copy_v(*far, 0)
                    if q == 9 and following >= 2:
                        copy_v(*far, 1)

            act.wait_ge(s2["ready"], 1)
            act.nop().then_inc(s2["exp"], 3)
            act.wait_ge(s["x_mlp"], G)
            for par in range(2):
                high_k(0, par, 0)
                high_k(0, par, 1)
                copy_h(0, par)
                high_q(0, par)
                copy_v(0, par, 0)
                copy_v(0, par, 1)
            negate_max(0, 0)
            for par in range(RB):
                step(0, par, first=par == 0)
            with act.Fori(1, ROUNDS) as t:
                for par in range(RB):
                    step(t, par)
            for par in range(RB):
                step(ROUNDS, par)
            step(ROUNDS + 1, 0, following=1)
            step(ROUNDS + 1, 1, following=0)
            copy_pv(ROUNDS + 1, 1)
            copy_on(ROUNDS + 1, 1)

            def high_h(g):
                act.wait_ge(s3["ht_ps"], g + 1)
                if not (isinstance(g, int) and g == 0):
                    act.wait_ge(s3["u_ps"], HPG * g)
                nc.scalar.copy(h3hi[:], psum[:, 2:4, 0:GT]).then_inc(s3["ht_hi"], 1)

            def high_hidden(g, it):
                e, m = it // DC, it % DC
                act.wait_ge(s3["hid"], HPG * g + it + 1)
                if e >= 2:
                    act.wait_ge(s3["d_ps"], (NE + 1) * g + e - 1)
                nc.scalar.copy(hid3hi[:, e % 2, m], hid3[:, it % 2]).then_inc(s3["hid_hi"], 1)

            def experts(g, ahead):
                act.wait_ge(s3["logit"], g + 1)
                nc.scalar.activation(prob[:], logit[:], ACT.Exp, scale=-1.0).then_inc(s3["ex"], 1)
                for it in range(HPG):
                    act.wait_ge(s3["g_ps"], HPG * g + it + 1)
                    if it >= 2:
                        act.wait_ge(s3["hid"], HPG * g + it - 1)
                    nc.scalar.activation(sg3[:, it % 2], bank[4 + it % 2][:, 0:GT], ACT.Silu).then_inc(s3["silu"], 1)
                    if it % DC == DC - 1:
                        for m in range(DC):
                            high_hidden(g, it - DC + 1 + m)
                if ahead:
                    high_h(g + 1)

            act.wait_ge(s2["x_new"], B)
            high_h(0)
            with act.Fori(0, G - 1) as g:
                experts(g, True)
            experts(G - 1, False)

        @block.vector
        def _(dve):
            def group_stats(g, done):
                for j in range(GB):
                    nc.vector.bn_stats(out=stats[:, j], in_=x[:, bass.ds(g * GB + j, 1), :].rearrange("t a d -> t (a d)")).then_inc(done, 1)
                wait_apart(dve, done, (GB + 1) * g + GB)
                for j in range(GB):
                    last = nc.vector.bn_aggr(out=mv[:, j], in_=stats[:, j])
                last.then_inc(done, 1)
                dve.wait_ge(done, (GB + 1) * (g + 1))

            def moments1(g):
                if not (isinstance(g, int) and g == 0):
                    dve.wait_ge(s["xn1"], g)
                group_stats(g, s["bn1"])
                nc.vector.tensor_scalar(rs[:, 0, :], mv[:, :, 1], LN_EPS, None, ALU.add)
                nc.vector.tensor_scalar(rs[:, 1, :], mv[:, :, 1], 1.0 + RMS_EPS, LN_EPS * RMS_EPS, ALU.mult, ALU.add).then_inc(s["var1"], 1)

            def normalise1(g, to, scale, done):
                for j in range(GB):
                    row = x[:, bass.ds(g * GB + j, 1), :].rearrange("t a d -> t (a d)")
                    last = nc.vector.tensor_scalar(to[:, j], row, mv[:, j, 0:1], rs[:, scale, j:j + 1], ALU.subtract, ALU.mult)
                last.then_inc(s[done], 1)

            def norm_h1(g):
                dve.wait_ge(s["rs1"], g + 1)
                if not (isinstance(g, int) and g == 0):
                    dve.wait_ge(s["ht_ps"], g)
                normalise1(g, h, 1, "h1")

            def beta_logits(g):
                if not (isinstance(g, int) and g == 0):
                    dve.wait_ge(s["tanh_b"], g)
                for j in range(GB):
                    if j < 2:
                        wait_apart(dve, s["h1"], g + 1)
                    else:
                        wait_apart(dve, s["blog"], GB * g + j - 1)
                    nc.vector.tensor_tensor_reduce(out=bjunk[:, j % 2], in0=h[:, j], in1=wbeta[:], scale=1.0, scalar=0.0,
                                                   op0=ALU.mult, op1=ALU.add, accum_out=blogit[:, j:j + 1]).then_inc(s["blog"], 1)

            def norm_xn(g):
                if not (isinstance(g, int) and g == 0):
                    dve.wait_ge(s["x1_sb"], g)
                normalise1(g, xn, 0, "xn1")

            def low_weights(k):
                dve.wait_ge(s["w_hi"], k + 1)
                (hi, lo), norm = pieces[k][1:]
                raw = stage[:, k % STAGES]
                if norm is None:
                    last = nc.vector.tensor_tensor(lo, raw, hi.bitcast(F32), op=ALU.subtract)
                else:
                    for c in range(DC):
                        last = nc.vector.scalar_tensor_tensor(out=lo[:, c], in0=raw[:, c], scalar=pcol[:, norm, c:c + 1], in1=hi[:, c].bitcast(F32), op0=ALU.mult, op1=ALU.subtract)
                last.then_inc(s["w_lo"], 1)

            def low_h1(g):
                dve.wait_ge(s["ht_hi"], g + 1)
                nc.vector.tensor_tensor(hTlo[:], psum[:, 4:6, 0:GT], hThi[:].bitcast(F32), op=ALU.subtract).then_inc(s["ht_lo"], 1)

            def low_h2(p):
                dve.wait_ge(s["h2t_hi"], p + 1)
                nc.vector.tensor_tensor(h2Tlo[:], psum[:, 6:8, 0:GT], h2Thi[:].bitcast(F32), op=ALU.subtract).then_inc(s["h2t_lo"], 1)

            def hidden1(p, m):
                dve.wait_ge(s["silu"], FC * p + m + 1)
                dve.wait_ge(s["u_ps"], FC * p + m + 1)
                if m >= 2:
                    dve.wait_ge(s["hid_lo"], FC * p + m - 1)
                nc.vector.tensor_tensor(hid[:, m % 2], sg[:, m % 2], bank[7 if m == 0 else 5][:, 0:GT], op=ALU.mult).then_inc(s["hid"], 1)

            def low_hidden1(p, m):
                dve.wait_ge(s["hid_hi"], FC * p + m + 1)
                nc.vector.tensor_tensor(hidlo[:, m], hid[:, m % 2], hidhi[:, m].bitcast(F32), op=ALU.subtract).then_inc(s["hid_lo"], 1)

            def add_mlp(p):
                dve.wait_ge(s["down_ps"], p + 1)
                dve.wait_ge(s["x_plus"], p + 1)
                for u in range(2):
                    rows = x[:, bass.ds(p * GB + 2 * u, 2), :]
                    last = nc.vector.tensor_tensor(rows, rows, bank[4 + u][0:T, 0:2 * D].rearrange("t (j d) -> t j d", j=2), op=ALU.add)
                last.then_inc(s["x_mlp"], 1)

            def step(g, mlp=True, ahead=True):
                p = g - 1
                NL = len(LEVELS)
                dve.wait_ge(s["va_sb"], g + 1)
                for c in range(DC):
                    last = nc.vector.tensor_tensor_scan(vs[:, c], decay[:, c], va[:, c], 0.0, ALU.mult, ALU.add)
                last.then_inc(s["v_scan"], 1)
                if mlp:
                    low_h2(p)
                dve.wait_ge(s["gram_ps"], g + 1)
                gram = bank[4][0:T, 0:GT].rearrange("s (j t) -> s j t", j=GB)
                nc.vector.tensor_tensor(negT[:], gram, over_rows(M_SUNEG), op=ALU.mult)
                nc.vector.tensor_tensor(neg[:], gram, over_rows(M_SLNEG), op=ALU.mult).then_inc(s["negs"], 1)
                dve.wait_ge(s["negs"], g + 1)
                nc.vector.tensor_tensor(tri[:], neg[:], over_rows(M_B1), op=ALU.mult)
                nc.vector.tensor_tensor(triT[:], negT[:], over_rows(M_BT), op=ALU.mult).then_inc(s["tri0a"], 1)
                dve.wait_ge(s["tri0a"], g + 1)
                eye = ident[0:T, 0:T].unsqueeze(1).broadcast_to([T, GB, T])
                nc.vector.tensor_tensor(tri[:], tri[:], eye, op=ALU.add)
                nc.vector.tensor_tensor(triT[:], triT[:], eye, op=ALU.add).then_inc(s["tri0"], 1)
                dve.wait_ge(s["tri0"], g + 1)
                dve.wait_ge(s["aq_ps"], g + 1)
                nc.vector.tensor_tensor(aT[:], bank[5][0:T, 0:GT].rearrange("s (j t) -> s j t", j=GB), over_rows(M_LE), op=ALU.mult).then_inc(s["aT_sb"], 1)
                for n in range(NL):
                    if mlp and n < FC:
                        hidden1(p, n)
                    for u in range(2):
                        it = 2 * n + u
                        rows = slice(2 * u, 2 * u + 2)
                        if n < NL - 1:
                            dve.wait_ge(s["tps_t"], 2 * (NL - 1) * g + it + 1)
                            if n > 0:
                                dve.wait_ge(s["tri_up"], 2 * (NL - 1) * g + it - 1)
                            nc.vector.tensor_tensor(tri[:, rows], tri[:, rows], bank[u][0:T, 0:2 * T].rearrange("s (j t) -> s j t", j=2), op=ALU.add).then_inc(s["tri_up"], 1)
                        dve.wait_ge(s["tps_tt"], 2 * NL * g + it + 1)
                        if n > 0:
                            dve.wait_ge(s["triT_up"], 2 * NL * g + it - 1)
                        nc.vector.tensor_tensor(triT[:, rows], triT[:, rows], bank[2 + u][0:T, 0:2 * T].rearrange("s (j t) -> s j t", j=2), op=ALU.add).then_inc(s["triT_up"], 1)
                    if mlp and n < FC:
                        low_hidden1(p, n)
                    if ahead and n == 0:
                        moments1(g + 1)
                    if ahead and n == 2:
                        norm_h1(g + 1)
                    if ahead and n == 3:
                        beta_logits(g + 1)
                    if mlp and n == FC:
                        add_mlp(p)
                if ahead:
                    low_h1(g + 1)
                dve.wait_ge(s["oT_hi"], g + 1)
                nc.vector.tensor_tensor(oTlo[:], psum[:, 6:8, 0:GT], oThi[:].bitcast(F32), op=ALU.subtract).then_inc(s["oT_lo"], 1)
                dve.wait_ge(s["wo_ps"], g + 1)
                dve.wait_ge(s["xn1"], g + 1)
                for u in range(2):
                    last = nc.vector.tensor_tensor(x1[:, 2 * u:2 * u + 2], xn[:, 2 * u:2 * u + 2], bank[u][0:T, 0:2 * D].rearrange("t (j d) -> t j d", j=2), op=ALU.add)
                last.then_inc(s["x1_sb"], 1)
                if ahead:
                    norm_xn(g + 1)
                dve.wait_ge(s["x1_sb"], g + 1)
                dve.wait_ge(s["rms"], g + 1)
                for j in range(GB):
                    last = nc.vector.tensor_scalar(h2n[:, j], x1[:, j], small[:, 5, j:j + 1], None, ALU.mult)
                last.then_inc(s["h2_sb"], 1)

            dve.wait_ge(s["x_in0"], 16)
            moments1(0)
            for k in range(READY["v"]):
                low_weights(k)
            dve.wait_ge(s["alpha_t"], 1)
            nc.vector.tensor_scalar(alpha[:, 0], pcol[:, 3], 0.5, 0.5, ALU.mult, ALU.add)
            nc.vector.tensor_scalar(alpha[:, 1], pcol[:, 3], -0.5, 0.5, ALU.mult, ALU.add).then_inc(s["alpha_d"], 1)
            norm_h1(0)
            low_weights(READY["v"])
            low_h1(0)
            for k in range(READY["o"], PIECES):
                low_weights(k)
            dve.wait_ge(s["c_in2"], 16 * 6)
            dve.wait_ge(s["alpha_d"], 1)
            for c in range(DC):
                last = nc.vector.tensor_scalar(decay[:, c], keep[:], alpha[:, 1, c:c + 1], None, ALU.mult)
            last.then_inc(s["alpha_d"], 1)
            nc.vector.tensor_tensor(wbeta[:], wbeta[:], bjunk[:, 0], op=ALU.mult).then_inc(s["setup_dve"], 1)
            wait_apart(dve, s["setup_dve"], 1)
            beta_logits(0)
            norm_xn(0)
            dve.wait_ge(s["alpha_d"], 2)
            dve.wait_ge(s["x_in"], 16 * (G - 1))
            step(0, mlp=False)
            with dve.Fori(1, G - 1) as g:
                step(g)
            step(G - 1, ahead=False)
            low_h2(G - 1)
            for m in range(FC):
                hidden1(G - 1, m)
                low_hidden1(G - 1, m)
            add_mlp(G - 1)
            dve.wait_ge(s["x_mlp"], G)

            def x_row(b):
                return x[:, bass.ds(b, 1), :].rearrange("t a d -> t (a d)")

            def normalise(t, par):
                b = t * RB + par
                nc.vector.bn_stats(out=stats[:, 0], in_=x_row(b)).then_inc(s2["bn"], 1)
                wait_apart(dve, s2["bn"], 2 * b + 1)
                nc.vector.bn_aggr(out=mv[:, 0], in_=stats[:, 0]).then_inc(s2["bn"], 1)
                dve.wait_ge(s2["bn"], 2 * b + 2)
                nc.vector.tensor_scalar(rs[:, 0, 0:1], mv[:, 0, 1:2], LN_EPS, None, ALU.add).then_inc(s2["stat"], 1)
                dve.wait_ge(s2["rs"], b + 1)
                if not is_row(b, 0):
                    dve.wait_ge(s2["hT_ps"], b)
                nc.vector.tensor_scalar(h2[:], x_row(b), mv[:, 0, 0:1], rs[:, 0, 0:1], ALU.subtract, ALU.mult).then_inc(s2["h"], 1)

            def low_k(t, par, m):
                dve.wait_ge(s2["k_hi"], DC * (t * RB + par) + m + 1)
                nc.vector.tensor_tensor(klo[:, m, 0:S2], bank[DENSE[m]][:, 0:S2], khi[:, m, 0:S2].bitcast(F32), op=ALU.subtract).then_inc(s2["k_lo"], 1)

            def low_q(t, par):
                dve.wait_ge(s2["q_hi"], t * RB + par + 1)
                nc.vector.tensor_tensor(qlo[:], bank[DENSE[1]][:, 2 * T:4 * T].rearrange("p (m q) -> p m q", m=DC), qhi[:].bitcast(F32), op=ALU.subtract).then_inc(s2["q_lo"], 1)

            def maxima(t, par, heads):
                n = t * RB + par
                for hd in heads:
                    if hd == 0:
                        dve.wait_ge(s2["flags"], n + 1)
                    if hd >= 2:
                        dve.wait_ge(s2["smax"], HEADS * n + hd - 1)
                    wait_apart(dve, s2["max_ps"], HEADS * n + hd + 1)
                    nc.vector.tensor_tensor_reduce(out=junk[:, hd % 2, :], in0=bank[4 + hd % 2][0:T, 0:S2], in1=biasq[:, par, :], scale=1.0, scalar=-3e38,
                                                   op0=ALU.add, op1=ALU.max, accum_out=head(smax, hd).unsqueeze(1)).then_inc(s2["smax"], 1)

            def normalise_heads(t, par):
                p = t * RB + par
                dve.wait_ge(s2["ot_ps"], p + 1)
                o = bank[DENSE[0]][0:T, :].rearrange("q (h d) -> q h d", h=HEADS)
                nc.vector.reciprocal(rden[:], o[:, :, HD:HD + 1]).then_inc(s2["rden"], 1)
                dve.wait_ge(s2["rden"], p + 1)
                nc.vector.tensor_tensor(on[:], o[:, :, 0:HD], rden[:].broadcast_to([T, HEADS, HD]), op=ALU.mult).then_inc(s2["on"], 1)

            def add_row(t, par):
                p = t * RB + par
                dve.wait_ge(s2["wo_ps"], p + 1)
                nc.vector.tensor_tensor(x_row(p), x_row(p), bank[DENSE[0]][0:T, 0:D], op=ALU.add).then_inc(s2["x_new"], 1)

            def step(t, par, first=False, following=2, norm=True):
                prev, nxt, far = ahead(t, par, -1), ahead(t, par, 1), ahead(t, par, 2)
                for q in range(SLOTS):
                    if following >= 1 and q < HEADS // 2:
                        maxima(*nxt, (2 * q, 2 * q + 1))
                    if q == 0 and following >= 2:
                        low_k(*far, 0)
                    if q == 1 and following >= 2:
                        low_k(*far, 1)
                    if q == 3 and not first:
                        normalise_heads(*prev)
                    if q == 6 and following >= 2:
                        low_q(*far)
                    if q == 7 and not first:
                        add_row(*prev)
                if norm:
                    normalise(*ahead(t, par, 3))

            for par in range(2):
                normalise(0, par)
                low_k(0, par, 0)
                low_k(0, par, 1)
                low_q(0, par)
            normalise(0, 2)
            maxima(0, 0, range(HEADS))
            for par in range(RB):
                step(0, par, first=par == 0)
            with dve.Fori(1, ROUNDS) as t:
                for par in range(RB):
                    step(t, par)
            for par in range(RB):
                step(ROUNDS, par, norm=ROUNDS * RB + par + 3 < B)
            step(ROUNDS + 1, 0, following=1, norm=False)
            step(ROUNDS + 1, 1, following=0, norm=False)
            normalise_heads(ROUNDS + 1, 1)
            add_row(ROUNDS + 1, 1)

            def group_moments(g):
                group_stats(g, s3["bn"])
                nc.vector.tensor_scalar(rs[:, 0, :], mv[:, :, 1], LN_EPS, None, ALU.add).then_inc(s3["stat"], 1)

            def normalise_group(g):
                dve.wait_ge(s3["rs"], g + 1)
                if not (isinstance(g, int) and g == 0):
                    dve.wait_ge(s3["ht_ps"], g)
                for j in range(GB):
                    row = x[:, bass.ds(g * GB + j, 1), :].rearrange("t a d -> t (a d)")
                    last = nc.vector.tensor_scalar(h3[:, j], row, mv[:, j, 0:1], rs[:, 0, j:j + 1], ALU.subtract, ALU.mult)
                last.then_inc(s3["h"], 1)

            def low_h(g):
                dve.wait_ge(s3["ht_hi"], g + 1)
                nc.vector.tensor_tensor(h3lo[:], psum[:, 2:4, 0:GT], h3hi[:].bitcast(F32), op=ALU.subtract).then_inc(s3["ht_lo"], 1)

            def add_gate_bias(g):
                dve.wait_ge(s3["lg_ps"], g + 1)
                nc.vector.tensor_tensor(logit[:], bank[2][0:T, 0:GB * NE].rearrange("t (j e) -> t j e", j=GB), gateb[:].unsqueeze(1).broadcast_to([T, GB, NE]), op=ALU.add).then_inc(s3["logit"], 1)

            def gates(g):
                dve.wait_ge(s3["ex"], g + 1)
                nc.vector.tensor_scalar(prob[:], prob[:], 1.0, None, ALU.add).then_inc(s3["prob"], 1)
                dve.wait_ge(s3["prob"], 2 * g + 1)
                nc.vector.reciprocal(prob[:], prob[:]).then_inc(s3["prob"], 1)
                dve.wait_ge(s3["prob"], 2 * g + 2)
                for e in range(NE):
                    mine = prob[:, :, e:e + 1]
                    if e > 0:
                        nc.vector.tensor_tensor(cmp1[:, :, e, 0:e], prob[:, :, 0:e], mine.broadcast_to([T, GB, e]), op=ALU.is_ge)
                    last = nc.vector.tensor_tensor(cmp1[:, :, e, e:NE], prob[:, :, e:NE], mine.broadcast_to([T, GB, NE - e]), op=ALU.is_gt)
                last.then_inc(s3["cmp"], 1)
                dve.wait_ge(s3["cmp"], g + 1)
                nc.vector.tensor_reduce(rank[:], cmp1[:], AX, ALU.add).then_inc(s3["rank"], 1)
                dve.wait_ge(s3["rank"], g + 1)
                nc.vector.scalar_tensor_tensor(out=gate[:], in0=rank[:], scalar=2.0, in1=prob[:], op0=ALU.is_lt, op1=ALU.mult).then_inc(s3["sel"], 1)
                dve.wait_ge(s3["sel"], g + 1)
                nc.vector.tensor_reduce(wsum[:], gate[:], AX, ALU.add).then_inc(s3["wsum"], 1)
                dve.wait_ge(s3["wsum"], 3 * g + 1)
                nc.vector.tensor_scalar(wsum[:], wsum[:], 1e-8, None, ALU.add).then_inc(s3["wsum"], 1)
                dve.wait_ge(s3["wsum"], 3 * g + 2)
                nc.vector.reciprocal(wsum[:], wsum[:]).then_inc(s3["wsum"], 1)
                dve.wait_ge(s3["wsum"], 3 * g + 3)
                nc.vector.tensor_tensor(gate[:], gate[:], wsum[:].broadcast_to([T, GB, NE]), op=ALU.mult).then_inc(s3["gate"], 1)
                dve.wait_ge(s3["gate"], g + 1)

            def hidden(g, it):
                dve.wait_ge(s3["silu"], HPG * g + it + 1)
                dve.wait_ge(s3["u_ps"], HPG * g + it + 1)
                if it >= 2:
                    dve.wait_ge(s3["hid_lo"], HPG * g + it - 1)
                nc.vector.tensor_tensor(hid3[:, it % 2], sg3[:, it % 2], bank[6 + it % 2][:, 0:GT], op=ALU.mult).then_inc(s3["hid"], 1)

            def low_hidden(g, it):
                e, m = it // DC, it % DC
                dve.wait_ge(s3["hid_hi"], HPG * g + it + 1)
                nc.vector.tensor_tensor(hid3lo[:, e % 2, m], hid3[:, it % 2], hid3hi[:, e % 2, m].bitcast(F32), op=ALU.subtract).then_inc(s3["hid_lo"], 1)

            def accumulate(g, e):
                dve.wait_ge(s3["d_ps"], (NE + 1) * g + e + 1)
                if e > 0:
                    dve.wait_ge(s3["x_new"], (NE + 1) * g + e)
                for j in range(GB):
                    row = x[:, bass.ds(g * GB + j, 1), :].rearrange("t a d -> t (a d)")
                    part = bank[down_bank(e) + j // 2][0:T, cols(j % 2, D)]
                    if e < NE:
                        last = nc.vector.scalar_tensor_tensor(out=row, in0=part, scalar=gate[:, j, e:e + 1], in1=row, op0=ALU.mult, op1=ALU.add)
                    else:
                        last = nc.vector.tensor_tensor(row, row, part, op=ALU.add)
                last.then_inc(s3["x_new"], 1)

            def experts(g, ahead):
                add_gate_bias(g)
                for it in range(HPG):
                    e, m = it // DC, it % DC
                    hidden(g, it)
                    if m == DC - 1:
                        for c in range(DC):
                            low_hidden(g, DC * e + c)
                        if e == 1:
                            gates(g)
                        if e >= 1:
                            accumulate(g, e - 1)
                        if ahead and e == FRONT - 1:
                            group_moments(g + 1)
                        if ahead and e == FRONT:
                            normalise_group(g + 1)
                if ahead:
                    low_h(g + 1)
                accumulate(g, NE)
                dve.wait_ge(s3["x_new"], (NE + 1) * (g + 1))

            dve.wait_ge(s2["x_new"], B)
            group_moments(0)
            normalise_group(0)
            low_h(0)
            with dve.Fori(0, G - 1) as g:
                experts(g, True)
            experts(G - 1, False)


def kernel(**inputs):
    import concourse.bacc as bacc
    from concourse.bass_utils import run_bass_kernel_spmd

    f = {n: np.ascontiguousarray(a) for n, a in inputs.items()}
    heads_last = (2, 8, HD)

    def split_heads(w):
        return np.ascontiguousarray(w.T.reshape(D, *heads_last).transpose(0, 1, 3, 2).reshape(D, D))

    arrays = {n: f[n] for n in (
        "x", "L0_attn_norm1_w", "L0_attn_Wq", "L0_attn_Wk", "L0_attn_Wv", "L0_attn_beta_b", "L0_attn_Wo",
        "L0_attn_alpha_logit", "L0_attn_norm2_w", "L0_attn_w_gate", "L0_attn_w_up", "L0_attn_w_down", "L0_ffn_gate_b")}
    arrays["beta_row"] = f["L0_attn_beta_w"].reshape(D)
    arrays["norm1_row"] = f["L0_attn_norm1_w"].reshape(D)
    for n in ("L0_attn_norm1_w", "L0_attn_norm2_w", "L0_attn_alpha_logit"):
        arrays[n] = np.ascontiguousarray(f[n].reshape(DC, P).T)
    arrays["mask"] = f["mask_BxSxS2_ik1"]
    arrays["maskT"] = np.ascontiguousarray(f["mask_BxSxS2_ik1"].transpose(0, 2, 1))
    arrays["ctxT"] = np.ascontiguousarray(f["ctx_1024"].transpose(0, 2, 1))
    arrays["xwq"] = split_heads(f["L0_xattn_wq"])
    arrays["xwk"] = split_heads(f["L0_xattn_wk"])
    arrays["xwv"] = np.ascontiguousarray(f["L0_xattn_wv"].T)
    arrays["xwo"] = np.ascontiguousarray(f["L0_xattn_w_out"].T)
    arrays["router"] = np.ascontiguousarray(f["L0_ffn_gate_w"].T)
    arrays["e1"] = np.ascontiguousarray(np.concatenate([f["L0_ffn_ew1"].transpose(0, 2, 1), f["L0_ffn_fc1"].T[None]]))
    arrays["e3"] = np.ascontiguousarray(np.concatenate([f["L0_ffn_ew3"].transpose(0, 2, 1), f["L0_ffn_fc2"].T[None]]))
    arrays["e2"] = np.ascontiguousarray(np.concatenate([f["L0_ffn_ew2"].transpose(0, 2, 1), f["L0_ffn_fc3"].T[None]]))
    arrays.update(shape_constants())

    nc = bacc.Bacc("TRN2", target_bir_lowering=False, num_devices=1)
    io = {n: nc.dram_tensor(f"in_{n}", a.shape, mybir.dt.from_np(a.dtype), kind="ExternalInput").ap() for n, a in arrays.items()}
    out = nc.dram_tensor("out", (B, T, D), F32, kind="ExternalOutput").ap()
    decoder_layer(nc, io, out)
    r = run_bass_kernel_spmd(nc, [{f"in_{n}": a for n, a in arrays.items()}], core_ids=[0])
    return r.results[0]["out"]
```

```python
from contextlib import ExitStack

import numpy as np

import concourse.bass as bass
from concourse import mybir

ALU = mybir.AluOpType
ACT = mybir.ActivationFunctionType
F32 = mybir.dt.float32
F32R = mybir.dt.float32r
BF16 = mybir.dt.bfloat16
I32 = mybir.dt.int32
AX = mybir.AxisListType.X

P = 128
B, T, D = 32, 112, 256
S2 = 375
HEADS, HD = 16, 16
FF = 512
NE, EW = 6, 256
GB = 4
G = B // GB
GT = GB * T
DC = D // P
FC = FF // P
KC = 3
KP = S2 // KC
S2E = S2 + 1
HPG = DC * (NE + 1)
FRONT = 4
LEVELS = (2, 4, 8, 16, 32, 64)
SLOTS = KC * HEADS // 4
PROBS = 4
BIG = float(2 ** 40)
ROWS = 3 * HD
STAGES = 4
RB = 3
ROUNDS = (B - 3) // RB
DENSE = (3, 7)
HPB = 4
LN_EPS, RMS_EPS = 1e-5, 1e-6

M_SUNEG, M_LE, M_B1, M_BT = 0, 1, 2, 3
N_MASKS = 4 + len(LEVELS)


def shape_constants():
    t = np.arange(T)
    row, col = t[:, None], t[None, :]
    masks = np.zeros((T, N_MASKS, T), np.float32)
    masks[:, M_SUNEG] = np.where(col > row, -1.0, 0.0)
    masks[:, M_LE] = row <= col
    for n, b in enumerate((1,) + LEVELS):
        quarter = (row // (2 * b) == col // (2 * b)) & (row % (2 * b) >= b) & (col % (2 * b) < b)
        if b == 1:
            masks[:, M_B1] = quarter
        masks[:, M_BT + n] = quarter.T
    keep = np.ones((P, GT), np.float32)
    keep[:, ::T] = 0.0
    return {"masks": masks, "ident": np.eye(P, dtype=np.float32), "keep": keep}


def decoder_layer(nc, io, out):
    with ExitStack() as ctx:
        def sb_in(scope):
            return lambda name, shape, dt=F32: scope.enter_context(nc.sbuf_tensor(name, shape, dt))

        def sem(name):
            return ctx.enter_context(nc.semaphore(name))

        sb = sb_in(ctx)
        psum = ctx.enter_context(nc.psum_tensor("psum", [P, 8, 512], F32))
        bank = [psum[:, i, :] for i in range(8)]

        x = sb("x_res", [T, B, D])
        ident = sb("ident_sb", [P, P])
        pcol = sb("pcol", [P, 4, DC])
        alpha = sb("alpha", [P, 2, DC])
        betab = sb("betab", [T, 2])
        gateb = sb("gateb", [T, NE])
        half = sb("neg_half", [T, 2, GB])
        xwq = sb("xwq_sb", [P, DC, D])
        xwo = sb("xwo_sb", [P, DC, D])
        router = sb("router_sb", [P, DC, NE])
        stage = sb("stage", [P, STAGES, DC, EW])
        stats = sb("stats", [T, GB, 6])
        mv = sb("mv", [T, GB, 2])
        rs = sb("rs", [T, 2, GB])
        small = sb("small", [T, 6, GB])

        with ExitStack() as scope:
            w1 = sb_in(scope)
            masks = w1("masks_sb", [T, N_MASKS, T])
            keep = w1("keep_sb", [P, GT])
            decay = w1("decay", [P, DC, GT])
            wparts = {}
            for name, chunks, width in (("q", DC, D), ("k", DC, D), ("v", DC, D), ("o", DC, D)):
                wparts[name] = tuple(w1(f"w{name}_{part}", [P, chunks, width], F32R) for part in ("hi", "lo"))
            wbeta = w1("wbeta", [T, D])
            xn = w1("xn", [T, GB, D])
            h = w1("h", [T, GB, D])
            hThi = w1("hThi", [P, DC, GT], F32R)
            hTlo = w1("hTlo", [P, DC, GT], F32R)
            blogit = w1("blogit", [T, GB])
            bjunk = w1("bjunk", [T, 2, D])
            qT = w1("qT", [P, DC, GT])
            va = w1("va", [P, DC, GT])
            vs = w1("vs", [P, DC, GT])
            kt = w1("kt", [T, GB, D])
            kT = w1("kT", [P, DC, GT])
            vt = w1("vt", [T, GB, D])
            negT = w1("negT", [T, GB, T])
            cT = w1("cT", [T, len(LEVELS), GB, T])
            tri = w1("tri", [T, GB, T])
            triT = w1("triT", [T, GB, T])
            xq = w1("xq", [T, GB, T])
            aT = w1("aT", [T, GB, T])
            y = w1("y", [T, GB, D])
            oThi = w1("oThi", [P, DC, GT], F32R)
            oTlo = w1("oTlo", [P, DC, GT], F32R)
            h2n = w1("h2n", [T, GB, D])
            for name, chunks, width in (("gate", DC, FF), ("up", DC, FF), ("down", FC, D)):
                wparts[name] = tuple(w1(f"w{name}_{part}", [P, chunks, width], F32R) for part in ("hi", "lo"))
            h2Thi = w1("h2Thi", [P, DC, GT], F32R)
            h2Tlo = w1("h2Tlo", [P, DC, GT], F32R)
            x1 = w1("x1", [T, GB, D])
            sg = w1("sg", [P, 2, GT])
            hid = w1("hid", [P, 2, GT])
            hidhi = w1("hidhi", [P, FC, GT], F32R)
            hidlo = w1("hidlo", [P, FC, GT], F32R)
        with ExitStack() as scope:
            w2 = sb_in(scope)
            for name in ("xk", "xv"):
                wparts[name] = tuple(w2(f"w{name}_{part}", [P, DC, D], F32R) for part in ("hi", "lo"))
            ctxT = w2("ctxT", [P, DC, S2])
            chi = w2("chi", [P, DC, S2E], F32R)
            clo = w2("clo", [P, DC, S2E], F32R)
            maskq = w2("maskq", [T, S2], I32)
            maskk = w2("maskk", [KP, KC, T], I32)
            biasq = w2("biasq", [T, RB, S2])
            flagk = w2("flagk", [KP, RB, KC, T], BF16)
            negbig = w2("negbig", [KP, KP], BF16)
            h2 = w2("h2", [T, D])
            h2T = w2("h2T", [P, DC, T])
            qhi = w2("qhi", [P, DC, T], F32R)
            qlo = w2("qlo", [P, DC, T], F32R)
            khi = w2("khi", [P, DC, S2E], F32R)
            klo = w2("klo", [P, DC, S2E], F32R)
            smax = w2("smax", [T, HEADS // DC, DC])
            junk = w2("junk", [T, 2, S2])
            ones = w2("ones", [HEADS, S2E], F32R)
            negm = w2("negm", [HEADS, T], F32R)
            qst, kst, vaug = {}, {}, {}
            for i in (0, 2, 1):
                qst[i] = w2(f"qst{i}", [ROWS + 1, HEADS // DC, DC, T], F32R)
                kst[i] = w2(f"kst{i}", [ROWS + 1, HEADS // DC, DC, S2E], F32R)
                vaug[i] = w2(f"vaug{i}", [KP, KC, HEADS, 2 * HD])
            pr = [w2(f"pr{i}", [KP, HPB, T]) for i in range(PROBS)]
            pv = w2("pv", [P, HPB * T])
            rden = w2("rden", [T, HEADS, 1])
            on = w2("on", [T, HEADS, HD])
            onT = w2("onT", [P, DC, T])
        with ExitStack() as scope:
            w3 = sb_in(scope)
            h3 = w3("h3", [T, GB, D])
            h3hi = w3("h3hi", [P, DC, GT], F32R)
            h3lo = w3("h3lo", [P, DC, GT], F32R)
            ehi = [w3("ehi0", [P, NE + 1, DC, EW], F32R)]
            sg3 = w3("sg3", [P, 2, GT])
            rhi = w3("rhi", [P, DC, NE], F32R)
            rlo = w3("rlo", [P, DC, NE], F32R)
            ehi += [w3(f"ehi{i}", [P, NE + 1, DC, EW], F32R) for i in (1, 2)]
            elo = [w3(f"elo{i}", [P, NE + 1, DC, EW], F32R) for i in range(3)]
            logit = w3("logit", [T, GB, NE])
            prob = w3("prob", [T, GB, NE])
            cmp1 = w3("cmp1", [T, GB, NE, NE])
            rank = w3("rank", [T, GB, NE])
            wsum = w3("wsum", [T, GB, 1])
            gate = w3("gate", [T, GB, NE])
            hid3 = w3("hid3", [P, 2, GT])
            hid3hi = w3("hid3hi", [P, 2, DC, GT], F32R)
            hid3lo = w3("hid3lo", [P, 2, DC, GT], F32R)

        apart = {nc.gpsimd.engine: sem("pool_waited"), nc.vector.engine: sem("dve_waited")}
        names = """x_in0 x_in w_in2 router_in c_in c_in2 masks_in setup_pool setup_act setup_dve alpha_t alpha_d w_hi w_lo
            bn1 var1 rs1 xn1 h1 blog ht_ps ht_hi ht_lo q_ps k_ps v_ps q_sb va_sb v_scan tanh_b ksq kscale_a root_b kscale_b kscale_c kscale
            kt_sb kT_ps vt_ps kT_sb vt_sb gram_ps aq_ps negs cmask tri0a tri0 aT_sb
            xps xsb tps_t tps_tt tri_up triT_up y_ps y_sb oT_ps oT_hi oT_lo wo_ps x1_sb x1_sq rms_a rms x_plus h2_sb h2t_ps h2t_hi h2t_lo
            g_ps u_ps silu hid hid_hi hid_lo down_ps x_mlp""".split()
        s = {n: sem(n) for n in names + [f"stage{i}" for i in range(STAGES)]}
        s2 = {n: sem("c_" + n) for n in """ones_in ctx_in c_hi c_lo mask_in ready bn flags stat rs h hT_ps hT_sb q_ps q_hi q_lo k_ps k_hi k_lo v01_ps v_ps v_sb qst0 qst1 qst2 kst0 kst1 kst2
            max_ps smax mt_ps negm negm_in sc_ps exp pv_done pv_sb ot_ps rden on onT_ps onT_sb wo_ps x_new""".split()}
        s3 = {n: sem("e_" + n) for n in """bn stat rs h ht_ps ht_hi ht_lo lg_ps logit ex prob cmp rank sel wsum gate g_ps u_ps silu hid hid_hi hid_lo d_ps x_new x_out r_hi r_lo w_hi w_lo""".split()}
        block = ctx.enter_context(nc.Block())

        def cols(j, width=T):
            return slice(j * width, (j + 1) * width)

        def head(stack, hd):
            return stack[:, hd % (HEADS // DC), hd // (HEADS // DC)]

        def down_bank(e):
            return 0 if e < NE else 6

        def ht3_banks(g):
            return 4 if isinstance(g, int) and g == 0 else 2

        def max_bank(row, hd):
            return (2, 6)[hd % 2] if is_row(row, 0) else 4 + hd % 2

        def over_rows(mask):
            return masks[:, mask, :].unsqueeze(1).broadcast_to([T, GB, T])

        def wait_apart(eng, semaphore, value):
            eng.wait_ge(semaphore, value)
            eng.sem_inc(apart[eng.engine], 1)

        def ahead(t, par, rows):
            return t + (par + rows) // RB, (par + rows) % RB

        def filled(t):
            return t * 48 + 48

        def split_weights():
            pieces = []
            for name, arg, norm in (("q", "L0_attn_Wq", 0), ("k", "L0_attn_Wk", 0), ("v", "L0_attn_Wv", 0), ("o", "L0_attn_Wo", None),
                                    ("gate", "L0_attn_w_gate", 1), ("up", "L0_attn_w_up", 1)):
                src = io[arg].rearrange("(c p) n -> p c n", p=P)
                for n in range(src.shape[2] // D):
                    pieces.append((src[:, :, cols(n, D)], [w[:, :, cols(n, D)] for w in wparts[name]], norm))
            src = io["L0_attn_w_down"].rearrange("(c p) n -> p c n", p=P)
            for n in range(FC // DC):
                pieces.append((src[:, cols(n, DC)], [w[:, cols(n, DC)] for w in wparts["down"]], None))
            for name, arg in (("xk", "xwk"), ("xv", "xwv")):
                pieces.append((io[arg].rearrange("(c p) n -> p c n", p=P), [w[:] for w in wparts[name]], None))
            return pieces

        pieces = split_weights()
        PIECES = len(pieces)
        READY = {"v": 3, "o": 4, "down": PIECES - 2, "xk": PIECES - 1, "xv": PIECES}

        def mlp_bank(m, alone):
            return 0 if alone and m % 2 == 0 else 4

        def is_row(b, row):
            return isinstance(b, int) and b == row

        @block.sync
        def _(sp):
            def load_x(g, done):
                sp.dma_start(x[:, g * GB:(g + 1) * GB, :], io["x"][g * GB:(g + 1) * GB].rearrange("b t d -> t b d")).then_inc(s[done], 16)

            def load_piece(k):
                if k >= STAGES:
                    sp.wait_ge(s["w_lo"], k - STAGES + 1)
                sp.dma_start(stage[:, k % STAGES], pieces[k][0]).then_inc(s[f"stage{k % STAGES}"], 16)

            load_x(0, "x_in0")
            for k in range(STAGES):
                load_piece(k)
            for tile, name in ((keep, "keep"), (masks, "masks")):
                sp.dma_start(tile[:], io[name]).then_inc(s["masks_in"], 16)
            for g in range(1, G):
                load_x(g, "x_in")
            for k in range(STAGES, PIECES):
                load_piece(k)
            for tile, name in ((xwq, "xwq"), (xwo, "xwo")):
                sp.dma_start(tile[:], io[name].rearrange("(c p) n -> p c n", p=P)).then_inc(s["w_in2"], 16)
            sp.dma_start(router[:], io["router"].rearrange("(c p) n -> p c n", p=P)).then_inc(s["router_in"], 16)

            def load_expert(k):
                n = PIECES + k
                if n - STAGES < PIECES:
                    sp.wait_ge(s["w_lo"], n - STAGES + 1)
                else:
                    sp.wait_ge(s3["w_lo"], k - STAGES + 1)
                sp.dma_start(stage[:, n % STAGES], io[("e1", "e3", "e2")[k % 3]][k // 3].rearrange("(c p) n -> p c n", p=P)).then_inc(s[f"stage{n % STAGES}"], 16)

            sp.wait_ge(s["vt_ps"], G)

            def load_context(t, par):
                b = t * RB + par
                if not is_row(b, 0):
                    sp.wait_ge(s2["c_lo"], b)
                sp.dma_start(ctxT[:], io["ctxT"][bass.ds(b, 1)].rearrange("a (c p) k -> p (a c) k", p=P)).then_inc(s2["ctx_in"], 16)

            def load_masks(t, par):
                b = t * RB + par
                if not is_row(b, 0):
                    sp.wait_ge(s2["flags"], b)
                ready = s2["mask_in"]
                sp.dma_start(maskq[:], io["mask"][bass.ds(b, 1)].rearrange("a q k -> (a q) k")).then_inc(ready, 16)
                sp.dma_start(maskk[:], io["maskT"][bass.ds(b, 1)].rearrange("a (c p) q -> p (a c) q", p=KP)).then_inc(ready, 16)

            def spread_heads(t, par):
                b = t * RB + par
                for tile, src, r, ready, count, done in ((kst, khi, 0, "k_hi", DC, "kst"), (kst, khi, 2, "k_hi", DC, "kst"), (kst, klo, 1, "k_lo", DC, "kst"),
                                                         (qst, qhi, 0, "q_hi", 1, "qst"), (qst, qhi, 1, "q_hi", 1, "qst"), (qst, qlo, 2, "q_lo", 1, "qst")):
                    sp.wait_ge(s2[ready], count * (b + 1))
                    dst = tile[par][r * HD:(r + 1) * HD]
                    sp.dma_start(dst.bitcast(F32), src[:].bitcast(F32)).then_inc(s2[f"{done}{par}"], 16)

            def spread_max(t, par):
                b = t * RB + par
                sp.wait_ge(s2["negm"], b + 1)
                sp.dma_start(qst[par][ROWS:ROWS + 1].bitcast(F32), negm[:].bitcast(F32)).then_inc(s2["negm_in"], 16)

            def step(t, par, load=True, heads=True):
                if load:
                    load_masks(*ahead(t, par, 3))
                    load_context(*ahead(t, par, 3))
                if heads:
                    spread_heads(*ahead(t, par, 2))
                spread_max(*ahead(t, par, 1))

            load_context(0, 0)
            load_masks(0, 0)
            def load_ones(par):
                sp.dma_start(kst[par][ROWS:ROWS + 1].bitcast(F32), ones[:].bitcast(F32)).then_inc(s2["ones_in"], 16)

            sp.wait_ge(s2["ready"], 1)
            load_ones(0)
            load_context(0, 1)
            spread_heads(0, 0)
            load_masks(0, 1)
            sp.wait_ge(s["x_mlp"], G)
            load_ones(1)
            load_ones(2)
            load_context(0, 2)
            load_masks(0, 2)
            spread_max(0, 0)
            spread_heads(0, 1)
            for k in range(STAGES):
                load_expert(k)
            with sp.Fori(0, ROUNDS) as t:
                for par in range(RB):
                    step(t, par)
            step(ROUNDS, 0, load=ROUNDS * RB + 3 < B)
            step(ROUNDS, 1, load=ROUNDS * RB + 4 < B)
            step(ROUNDS, 2, load=False)
            step(ROUNDS + 1, 0, load=False, heads=False)

            for k in range(STAGES, 3 * (NE + 1)):
                load_expert(k)
            with sp.Fori(0, G) as g:
                sp.wait_ge(s3["x_new"], (g + 1) * (NE + 1))
                sp.dma_start(out[bass.ds(g * GB, GB)].rearrange("b t d -> t b d"), x[:, bass.ds(g * GB, GB), :]).then_inc(s3["x_out"], 16)
            sp.wait_ge(s3["x_out"], 16 * G)

        @block.gpsimd
        def _(pool):
            pool.dma_start(betab[:, 0:1], io["L0_attn_beta_b"].partition_broadcast(T)).then_inc(s["c_in2"], 16)
            pool.dma_start(wbeta[:], io["beta_row"].partition_broadcast(T)).then_inc(s["c_in2"], 16)
            pool.dma_start(bjunk[:, 0], io["norm1_row"].partition_broadcast(T)).then_inc(s["c_in2"], 16)
            pool.dma_start(gateb[:], io["L0_ffn_gate_b"].partition_broadcast(T)).then_inc(s["c_in2"], 16)
            nc.gpsimd.memset(half[:, 0, :], -0.5)
            nc.gpsimd.memset(half[:, 1, :], 0.5).then_inc(s["setup_pool"], 1)
            pool.wait_ge(s["setup_pool"], 1)

            def powers(g):
                pool.wait_ge(s["var1"], g + 1)
                nc.gpsimd.tensor_tensor(rs[:], rs[:], half[:, 0:1, :].broadcast_to([T, 2, GB]), op=ALU.pow).then_inc(s["rs1"], 1)

            def key_scale(g):
                wait_apart(pool, s["ksq"], g + 1)
                nc.gpsimd.tensor_scalar(small[:, 2], small[:, 2], 1e-24, None, ALU.max).then_inc(s["kscale_b"], 1)
                pool.wait_ge(s["kscale_b"], g + 1)
                nc.gpsimd.tensor_tensor(small[:, 3], small[:, 2], half[:, 0, :], op=ALU.pow).then_inc(s["kscale_c"], 1)
                pool.wait_ge(s["kscale_c"], g + 1)
                pool.wait_ge(s["root_b"], g + 1)
                nc.gpsimd.tensor_tensor(small[:, 4], small[:, 3], small[:, 1], op=ALU.mult).then_inc(s["kscale"], 1)

            def rsqrt(t, par):
                pool.wait_ge(s2["stat"], t * RB + par + 1)
                nc.gpsimd.tensor_tensor(rs[:, 0, 0:1], rs[:, 0, 0:1], half[:, 0, 0:1], op=ALU.pow).then_inc(s2["rs"], 1)

            def stack_constants():
                pool.wait_ge(s["y_ps"], G)
                nc.gpsimd.memset(vaug[0][:], 1.0)
                nc.gpsimd.memset(ones[:].bitcast(F32), 1.0)
                for part in (chi, clo):
                    nc.gpsimd.memset(part[:, :, S2:S2E].bitcast(F32), 0.0)
                nc.gpsimd.tensor_scalar(negbig[:], ident[0:KP, 0:KP], -BIG, None, ALU.mult).then_inc(s2["ready"], 1)

            def step(g, mlp=True, ahead=True):
                pool.wait_ge(s["negs"], g + 1)
                for n in range(len(LEVELS)):
                    nc.gpsimd.tensor_tensor(cT[:, n], negT[:], over_rows(M_BT + 1 + n), op=ALU.mult).then_inc(s["cmask"], 1)
                    if n == 2 and ahead:
                        powers(g + 1)
                if mlp:
                    add_attention(g - 1)
                if ahead:
                    root_beta(g + 1)
                    key_scale(g + 1)
                else:
                    stack_constants()
                    rsqrt(0, 0)
                wait_apart(pool, s["x1_sq"], g + 1)
                nc.gpsimd.tensor_scalar(small[:, 5], small[:, 5], 1.0 / D, RMS_EPS, ALU.mult, ALU.add).then_inc(s["rms_a"], 1)
                pool.wait_ge(s["rms_a"], g + 1)
                nc.gpsimd.tensor_tensor(small[:, 5], small[:, 5], half[:, 0, :], op=ALU.pow).then_inc(s["rms"], 1)

            def add_attention(g):
                pool.wait_ge(s["x1_sb"], g + 1)
                nc.gpsimd.tensor_tensor(x[:, bass.ds(g * GB, GB), :], x[:, bass.ds(g * GB, GB), :], x1[:], op=ALU.add).then_inc(s["x_plus"], 1)

            def root_beta(g):
                wait_apart(pool, s["tanh_b"], g + 1)
                nc.gpsimd.tensor_scalar(small[:, 0], small[:, 0], 0.5, 0.5, ALU.mult, ALU.add).then_inc(s["kscale_a"], 1)
                pool.wait_ge(s["kscale_a"], g + 1)
                nc.gpsimd.tensor_tensor(small[:, 1], small[:, 0], half[:, 1, :], op=ALU.pow).then_inc(s["root_b"], 1)

            powers(0)
            root_beta(0)
            key_scale(0)
            step(0, mlp=False)
            with pool.Fori(1, G - 1) as g:
                step(g)
            step(G - 1, ahead=False)
            add_attention(G - 1)

            def mask_bias(t, par):
                b = t * RB + par
                if not isinstance(b, int) or b >= RB:
                    pool.wait_ge(s2["sc_ps"], SLOTS * (b - RB + 1))
                wait_apart(pool, s2["mask_in"], 32 * (b + 1))
                nc.gpsimd.tensor_scalar(biasq[:, par, :], maskq[:], 1.0, -BIG, ALU.is_equal, ALU.mult)
                nc.gpsimd.tensor_scalar(flagk[:, par], maskk[:], 1.0, None, ALU.is_equal).then_inc(s2["flags"], 1)

            def step(t, par, power=True):
                mask_bias(*ahead(t, par, 2))
                if power:
                    rsqrt(*ahead(t, par, 3))

            mask_bias(0, 0)
            rsqrt(0, 1)
            mask_bias(0, 1)
            pool.wait_ge(s["x_mlp"], G)
            nc.gpsimd.memset(vaug[1][:], 1.0)
            nc.gpsimd.memset(vaug[2][:], 1.0).then_inc(s2["ready"], 1)
            rsqrt(0, 2)
            step(0, 0)
            step(0, 1)
            step(0, 2)
            with pool.Fori(1, ROUNDS) as t:
                for par in range(RB):
                    step(t, par)
            for par in range(RB):
                step(ROUNDS, par, power=ROUNDS * RB + par + 3 < B)

            def rsqrt_group(g):
                pool.wait_ge(s3["stat"], g + 1)
                nc.gpsimd.tensor_tensor(rs[:, 0, :], rs[:, 0, :], half[:, 0, :], op=ALU.pow).then_inc(s3["rs"], 1)

            rsqrt_group(0)
            for stack in ("qst1", "kst1"):
                pool.wait_ge(s2[stack], filled(ROUNDS + 1))
            pool.wait_ge(s["router_in"], 16)
            nc.gpsimd.tensor_copy(rhi[:], router[:]).then_inc(s3["r_hi"], 1)
            pool.wait_ge(s3["r_hi"], 1)
            nc.gpsimd.tensor_tensor(rlo[:], router[:], rhi[:].bitcast(F32), op=ALU.subtract).then_inc(s3["r_lo"], 1)
            for k in range(3 * (NE + 1)):
                n = PIECES + k
                if k == 0:
                    pool.wait_ge(s2["pv_done"], SLOTS * (B - 1) + PROBS)
                if k == 6:
                    pool.wait_ge(s2["x_new"], B)
                pool.wait_ge(s3["w_hi"], k + 1)
                nc.gpsimd.tensor_tensor(elo[k % 3][:, k // 3], stage[:, n % STAGES], ehi[k % 3][:, k // 3].bitcast(F32), op=ALU.subtract).then_inc(s3["w_lo"], 1)
                if k == 3 * FRONT + 2:
                    rsqrt_group(1)
            with pool.Fori(2, G) as g:
                rsqrt_group(g)

        @block.tensor
        def _(pe):
            def transpose_in(src, b0, b1, done):
                for c in range(DC):
                    for j in range(GB):
                        mm = pe.transpose(bank[b0 if c == 0 else b1][:, cols(j)], src[:, j, cols(c, P)], ident[0:T, 0:T])
                mm.then_inc(done, 1)

            pe.wait_ge(s["c_in"], 16 * 4)

            def split_products(to, pairs):
                pairs = list(pairs)
                products = [(st[a], mv[b]) for a, b in ((0, 0), (0, 1), (1, 0)) for st, mv in pairs]
                for n, (st, mv) in enumerate(products):
                    mm = pe.matmul(to, st, mv, start=n == 0, stop=n == len(products) - 1)
                return mm

            def weight_cols(name, m):
                return [tuple(w[:, c, cols(m, P)] for w in wparts[name]) for c in range(DC)]

            def token_cols(parts, j, chunks=DC):
                return [tuple(part[:, c, cols(j)] for part in parts) for c in range(chunks)]

            def chunks_of(parts, chunks=DC):
                return [tuple(part[:, c] for part in parts) for c in range(chunks)]

            def transpose_h1(g):
                pe.wait_ge(s["h1"], g + 1)
                transpose_in(h, 2, 3, s["ht_ps"])

            def project_k1(g):
                pe.wait_ge(s["ht_lo"], g + 1)
                if not (isinstance(g, int) and g < 2):
                    pe.wait_ge(s["x_mlp"], g - 1)
                for j in range(GB):
                    mm = split_products(bank[4 + j // 2][0:T, cols(j % 2, D)], zip(token_cols((hThi, hTlo), j), chunks_of(wparts["k"])))
                mm.then_inc(s["k_ps"], 1)

            def project_q1(g):
                for m in range(DC):
                    mm = split_products(bank[2 + m][:, 0:GT], zip(weight_cols("q", m), chunks_of((hThi, hTlo))))
                mm.then_inc(s["q_ps"], 1)

            def project_v1(g, m):
                split_products(bank[m][:, 0:GT], zip(weight_cols("v", m), chunks_of((hThi, hTlo)))).then_inc(s["v_ps"], 1)

            def transpose_h2(p):
                pe.wait_ge(s["h2_sb"], p + 1)
                if not (isinstance(p, int) and p == G - 1):
                    pe.wait_ge(s["vt_sb"], p + 2)
                else:
                    pe.wait_ge(s["x_mlp"], p)
                transpose_in(h2n, 4, 5, s["h2t_ps"])

            def gate(p, m, alone=False):
                if m == 0:
                    pe.wait_ge(s["h2t_lo"], p + 1)
                elif not alone:
                    pe.wait_ge(s["silu"], FC * p + m)
                elif m >= 2:
                    pe.wait_ge(s["hid"], FC * p + m - 1)
                split_products(bank[mlp_bank(m, alone)][:, 0:GT], zip(weight_cols("gate", m), chunks_of((h2Thi, h2Tlo)))).then_inc(s["g_ps"], 1)

            def up(p, m, alone=False):
                if not alone and m > 0:
                    pe.wait_ge(s["hid"], FC * p + m)
                split_products(bank[mlp_bank(m, alone) + 1][:, 0:GT], zip(weight_cols("up", m), chunks_of((h2Thi, h2Tlo)))).then_inc(s["u_ps"], 1)

            def gate_up(p, m):
                gate(p, m, alone=True)
                up(p, m, alone=True)

            def mlp_down(p, rows=range(GB)):
                pe.wait_ge(s["hid_lo"], FC * (p + 1))
                for j in rows:
                    mm = split_products(bank[4 + j // 2][0:T, cols(j % 2, D)], zip(token_cols((hidhi, hidlo), j, FC), chunks_of(wparts["down"], FC)))
                if GB - 1 in rows:
                    mm.then_inc(s["down_ps"], 1)

            def transpose_v(g):
                pe.wait_ge(s["v_scan"], g + 1)
                pe.wait_ge(s["tri0a"], g + 1)
                pe.wait_ge(s["aT_sb"], g + 1)
                for j in range(GB):
                    for c in range(DC):
                        mm = pe.transpose(bank[4 + j // 2][0:T, (j % 2) * D + c * P:(j % 2) * D + (c + 1) * P], vs[:, c, cols(j)], ident[:])
                mm.then_inc(s["vt_ps"], 1)

            def transpose_k(g):
                pe.wait_ge(s["kt_sb"], g + 1)
                pe.wait_ge(s["q_sb"], g + 1)
                transpose_in(kt, 2, 3, s["kT_ps"])

            def products_of_keys(g):
                pe.wait_ge(s["kT_sb"], g + 1)
                for j in range(GB):
                    for c in range(DC):
                        mm = pe.matmul(bank[4][0:T, cols(j)], kT[:, c, cols(j)], kT[:, c, cols(j)], start=c == 0, stop=c == DC - 1)
                mm.then_inc(s["gram_ps"], 1)
                project_v1(g, 1)
                for j in range(GB):
                    for c in range(DC):
                        mm = pe.matmul(bank[5][0:T, cols(j)], kT[:, c, cols(j)], qT[:, c, cols(j)], start=c == 0, stop=c == DC - 1)
                mm.then_inc(s["aq_ps"], 1)

            def double(g, n, mlp):
                for u in range(2):
                    it = 2 * n + u
                    pe.wait_ge(s["cmask"], len(LEVELS) * g + n + 1)
                    if n == 0:
                        pe.wait_ge(s["tri0"], g + 1)
                        pe.wait_ge(s["va_sb"], g + 1)
                        if mlp:
                            pe.wait_ge(s["x1_sb"], g)
                    else:
                        pe.wait_ge(s["tri_up"], 2 * (len(LEVELS) - 1) * g + it - 1)
                    for j in (2 * u, 2 * u + 1):
                        mm = pe.matmul(bank[6 + u][0:T, cols(j % 2)], cT[:, n, j], tri[:, j], start=True, stop=True)
                    mm.then_inc(s["xps"], 1)
                if mlp and n >= 3:
                    up(g - 1, n - 3)
                for u in range(2):
                    it = 2 * n + u
                    pe.wait_ge(s["xsb"], 2 * len(LEVELS) * g + it + 1)
                    if n > 0:
                        pe.wait_ge(s["triT_up"], 2 * len(LEVELS) * g + it - 1)
                    if n < len(LEVELS) - 1:
                        for j in (2 * u, 2 * u + 1):
                            mm = pe.matmul(bank[u][0:T, cols(j % 2)], triT[:, j], xq[:, j], start=True, stop=True)
                        mm.then_inc(s["tps_t"], 1)
                    for j in (2 * u, 2 * u + 1):
                        mm = pe.matmul(bank[2 + u][0:T, cols(j % 2)], xq[:, j], triT[:, j], start=True, stop=True)
                    mm.then_inc(s["tps_tt"], 1)

            def solve_values(g):
                pe.wait_ge(s["triT_up"], 2 * len(LEVELS) * (g + 1))
                for j in range(GB):
                    mm = pe.matmul(bank[j // 2][0:T, cols(j % 2, D)], triT[:, j], vt[:, j], start=True, stop=True)
                mm.then_inc(s["y_ps"], 1)

            def attend(g):
                pe.wait_ge(s["y_sb"], g + 1)
                pe.wait_ge(s["aT_sb"], g + 1)
                for c in range(DC):
                    for j in range(GB):
                        mm = pe.matmul(bank[6 + c][:, cols(j)], y[:, j, cols(c, P)], aT[:, j], start=True, stop=True)
                mm.then_inc(s["oT_ps"], 1)

            def project_o(g):
                pe.wait_ge(s["oT_lo"], g + 1)
                for j in range(GB):
                    mm = split_products(bank[6 + j // 2][0:T, cols(j % 2, D)], zip(token_cols((oThi, oTlo), j), chunks_of(wparts["o"])))
                mm.then_inc(s["wo_ps"], 1)

            def step(g, mlp=True, ahead=True):
                p = g - 1
                transpose_k(g)
                project_v1(g, 0)
                products_of_keys(g)
                for n in range(len(LEVELS)):
                    double(g, n, mlp)
                    if n == 0:
                        transpose_v(g)
                    if mlp and n == 1:
                        transpose_h2(p)
                    if mlp and n >= 2:
                        gate(p, n - 2)
                if mlp:
                    up(p, FC - 1)
                solve_values(g)
                if ahead:
                    transpose_h1(g + 1)
                if mlp:
                    mlp_down(p, range(GB if ahead else GB // 2))
                attend(g)
                if ahead:
                    project_k1(g + 1)
                    project_q1(g + 1)
                else:
                    mlp_down(p, range(GB // 2, GB))
                project_o(g)

            transpose_h1(0)
            pe.wait_ge(s["w_lo"], READY["v"])
            project_k1(0)
            project_q1(0)
            pe.wait_ge(s["w_lo"], READY["o"])
            step(0, mlp=False)
            pe.wait_ge(s["w_lo"], READY["down"])
            with pe.Fori(1, G - 1) as g:
                step(g)
            step(G - 1, ahead=False)
            pe.wait_ge(s["w_in2"], 16 * 2)
            pe.nop().then_inc(s2["pv_done"], PROBS)

            def project_k(t, par, m):
                f = t * RB + par
                if m == 0:
                    pe.wait_ge(s2["c_lo"], f + 1)
                    if not is_row(f, 0):
                        pe.wait_ge(s2["v_sb"], 2 * f)
                split_products(bank[DENSE[m]][:, 0:S2E], zip(weight_cols("xk", m), chunks_of((chi, clo)))).then_inc(s2["k_ps"], 1)

            def transpose_h(t, par):
                f = t * RB + par
                pe.wait_ge(s2["h"], f + 1)
                pe.wait_ge(s2["k_lo"], DC * (f + 1))
                for c in range(DC):
                    mm = pe.transpose(bank[DENSE[1]][:, cols(c)], h2[:, cols(c, P)], ident[0:T, 0:T])
                mm.then_inc(s2["hT_ps"], 1)

            def project_q(t, par):
                f = t * RB + par
                pe.wait_ge(s2["hT_sb"], f + 1)
                for m in range(DC):
                    for c in range(DC):
                        mm = pe.matmul(bank[DENSE[1]][:, (DC + m) * T:(DC + m + 1) * T], xwq[:, c, cols(m, P)], h2T[:, c], start=c == 0, stop=c == DC - 1)
                mm.then_inc(s2["q_ps"], 1)

            def project_v(t, par, part):
                f = t * RB + par
                if part == 0:
                    pe.wait_ge(s2["q_lo"], f + 1)
                elif isinstance(f, int) and f < 2:
                    pe.wait_ge(s2["k_lo"], DC * f + 1)
                else:
                    pe.wait_ge(s2["x_new"], f - 2)
                for c3 in ((0, 1), (2,))[part]:
                    keys = [(chi[:, c, cols(c3, KP)], clo[:, c, cols(c3, KP)]) for c in range(DC)]
                    mm = split_products(bank[DENSE[1 - part]][0:KP, cols(c3 % 2, D)], zip(keys, chunks_of(wparts["xv"])))
                mm.then_inc(s2[("v01_ps", "v_ps")[part]], 1)

            def row_max(t, par, heads):
                n = t * RB + par
                for hd in heads:
                    if hd == 0:
                        pe.wait_ge(s2[f"qst{par}"], filled(t))
                        pe.wait_ge(s2[f"kst{par}"], filled(t))
                        if not is_row(n, 0):
                            pe.wait_ge(s2["negm"], n)
                    if hd >= 2:
                        pe.wait_ge(s2["smax"], HEADS * n + hd - 1)
                    pe.matmul(bank[max_bank(n, hd)][0:T, 0:S2E], head(qst[par][0:ROWS], hd), head(kst[par][0:ROWS], hd), start=True, stop=True).then_inc(s2["max_ps"], 1)

            def transpose_max(t, par):
                n = t * RB + par
                pe.wait_ge(s2["smax"], HEADS * (n + 1))
                pe.transpose(bank[5][0:HEADS, 0:T], smax[:].rearrange("q h m -> q (h m)"), ident[0:T, 0:T]).then_inc(s2["mt_ps"], 1)

            def mask_scores(t, par, q):
                b = t * RB + par
                if q == 0:
                    pe.wait_ge(s2["negm_in"], 16 * (b + 1))
                    pe.wait_ge(s2["flags"], b + 1)
                pe.wait_ge(s2["exp"], SLOTS * b + q + 1)
                flags = flagk[:, par, q // HPB, :].unsqueeze(1).broadcast_to([KP, HPB, T])
                pe.matmul(bank[q % 3][0:KP, 0:GT], negbig[:], flags, start=True, stop=False, skip_group_check=True)

            def score(t, par, q, i):
                hd = HPB * (q % HPB) + i
                mm = pe.matmul(bank[q % 3][0:KP, cols(i)], head(kst[par], hd)[:, cols(q // HPB, KP)], head(qst[par], hd), start=False, stop=True, skip_group_check=True)
                if i == HPB - 1:
                    mm.then_inc(s2["sc_ps"], 1)

            def weighted_values(t, par, q):
                b = t * RB + par
                c3 = q // HPB
                if q == 0 and not is_row(b, 0):
                    pe.wait_ge(s2["pv_sb"], b)
                pe.wait_ge(s2["exp"], SLOTS * b + q + 4)
                for i in range(HPB):
                    hd = HPB * (q % HPB) + i
                    row = 2 * HD * i
                    mm = pe.matmul(bank[6][row:row + 2 * HD, cols(hd // HPB)], vaug[par][:, c3, hd], pr[q % PROBS][:, i],
                                   start=q == 0, stop=c3 == KC - 1, skip_group_check=True)
                mm.then_inc(s2["pv_done"], 1)

            def transpose_o(t, par):
                p = t * RB + par
                pe.wait_ge(s2["pv_sb"], p + 1)
                if isinstance(p, int) and p >= B - 3:
                    pe.wait_ge(s2["v_sb"], 2 * B)
                    pe.wait_ge(s2["x_new"], p)
                else:
                    pe.wait_ge(s2["k_lo"], DC * (p + 3) + 1)
                for g4 in range(HPB):
                    mm = pe.transpose(bank[DENSE[0]][0:T, cols(g4, P)], pv[:, cols(g4)], ident[:])
                mm.then_inc(s2["ot_ps"], 1)

            def transpose_on(t, par):
                p = t * RB + par
                pe.wait_ge(s2["on"], p + 1)
                for c in range(DC):
                    mm = pe.transpose(bank[DENSE[0]][:, cols(c)], on[:].rearrange("q h d -> q (h d)")[:, cols(c, P)], ident[0:T, 0:T])
                mm.then_inc(s2["onT_ps"], 1)

            def project_out(t, par):
                p = t * RB + par
                pe.wait_ge(s2["onT_sb"], p + 1)
                for c in range(DC):
                    mm = pe.matmul(bank[DENSE[0]][0:T, 0:D], onT[:, c], xwo[:, c], start=c == 0, stop=c == DC - 1)
                mm.then_inc(s2["wo_ps"], 1)

            def step(t, par, first=False, following=2):
                prev, nxt, far = ahead(t, par, -1), ahead(t, par, 1), ahead(t, par, 2)
                for q in range(SLOTS):
                    mask_scores(t, par, q)
                    score(t, par, q, 0)
                    if following >= 1 and q < HEADS // 2:
                        row_max(*nxt, (2 * q,))
                    score(t, par, q, 1)
                    if following >= 1 and q < HEADS // 2:
                        row_max(*nxt, (2 * q + 1,))
                    score(t, par, q, 2)
                    if q >= 2:
                        weighted_values(t, par, q - 2)
                    elif not first:
                        weighted_values(*prev, SLOTS - 2 + q)
                    score(t, par, q, 3)
                    if q in (1, 2) and following >= 2 and not first:
                        project_k(*far, q - 1)
                    if q == 3 and not first:
                        transpose_o(*prev)
                    if q == 4 and following >= 2:
                        transpose_h(*far)
                    if q == 5 and not first:
                        transpose_on(*prev)
                    if q == 6 and following >= 2:
                        project_q(*far)
                    if q == 7 and not first:
                        project_out(*prev)
                    if q == 8 and following >= 1:
                        transpose_max(*nxt)
                    if q == 8 and following == 0:
                        transpose_group(0)
                    if q == 8 and following >= 2:
                        project_v(*far, 0)
                        project_v(*far, 1)

            def route(g, n):
                j, (hp, rp), c = n // (3 * DC), ((h3hi, rhi), (h3hi, rlo), (h3lo, rhi))[n // DC % 3], n % DC
                mm = pe.matmul(bank[2][0:T, cols(j, NE)], hp[:, c, cols(j)], rp[:, c], start=n % (3 * DC) == 0, stop=n % (3 * DC) == 3 * DC - 1)
                if n == GB * 3 * DC - 1:
                    mm.then_inc(s3["lg_ps"], 1)

            def half_expert(g, e, m, w):
                it = DC * e + m
                b0, done, left = ((4, "g_ps", "silu"), (6, "u_ps", "hid"))[w]
                if e == 0 and m == 0 and w == 0:
                    pe.wait_ge(s3["ht_lo"], g + 1)
                    pe.wait_ge(s3["r_lo"], 1)
                if m == 0:
                    pe.wait_ge(s3["w_lo"], 3 * e + w + 1)
                if it >= 2:
                    pe.wait_ge(s3[left], HPG * g + it - 1)
                elif w == 1 and m == 0 and not (isinstance(g, int) and g == 0):
                    pe.wait_ge(s3["x_new"], (NE + 1) * g)
                parts = [(wp[w][:, e, c, cols(m, P)], hp[:, c]) for wp, hp in ((ehi, h3hi), (elo, h3hi), (ehi, h3lo)) for c in range(DC)]
                for n, (wp, hp) in enumerate(parts):
                    mm = pe.matmul(bank[b0 + it % 2][:, 0:GT], wp, hp, start=n == 0, stop=n == len(parts) - 1)
                    if n == len(parts) - 1:
                        mm.then_inc(s3[done], 1)
                    if e == 0:
                        route(g, (2 * m + w) * len(parts) + n)

            def expand(g, e):
                for m in range(DC):
                    for w in range(2):
                        half_expert(g, e, m, w)

            def contract(g, e):
                pe.wait_ge(s3["w_lo"], 3 * e + 3)
                pe.wait_ge(s3["hid_lo"], HPG * g + DC * (e + 1))
                if 1 <= e < NE:
                    pe.wait_ge(s3["x_new"], (NE + 1) * g + e)
                for j in range(GB):
                    parts = [(hp[:, e % 2, c, cols(j)], wp[2][:, e, c]) for hp, wp in ((hid3hi, ehi), (hid3hi, elo), (hid3lo, ehi)) for c in range(DC)]
                    for n, (hp, wp) in enumerate(parts):
                        mm = pe.matmul(bank[down_bank(e) + j // 2][0:T, cols(j % 2, D)], hp, wp, start=n == 0, stop=n == len(parts) - 1)
                mm.then_inc(s3["d_ps"], 1)

            def transpose_group(g):
                pe.wait_ge(s3["h"], g + 1)
                if not (isinstance(g, int) and g == 0):
                    pe.wait_ge(s3["logit"], g)
                transpose_in(h3, ht3_banks(g), ht3_banks(g) + 1, s3["ht_ps"])

            def experts(g, ahead):
                if not (isinstance(g, int) and g == 0):
                    expand(g, 0)
                for e in range(1, NE + 1):
                    expand(g, e)
                    contract(g, e - 1)
                    if ahead and e == FRONT + 1:
                        transpose_group(g + 1)
                contract(g, NE)

            pe.wait_ge(s["w_lo"], READY["xv"])
            project_k(0, 0, 0)
            pe.wait_ge(s["x1_sb"], G)
            project_k(0, 0, 1)
            transpose_h(0, 0)
            transpose_h2(G - 1)
            project_q(0, 0)
            gate_up(G - 1, 0)
            project_v(0, 0, 0)
            project_v(0, 0, 1)
            gate_up(G - 1, 1)
            gate(G - 1, 2, alone=True)
            row_max(0, 0, range(0, 2))
            up(G - 1, 2, alone=True)
            row_max(0, 0, range(2, 4))
            gate(G - 1, 3, alone=True)
            row_max(0, 0, range(4, 6))
            up(G - 1, 3, alone=True)
            row_max(0, 0, range(6, 8))
            project_k(0, 1, 0)
            row_max(0, 0, range(8, 10))
            project_k(0, 1, 1)
            row_max(0, 0, range(10, 12))
            mlp_down(G - 1, range(0, GB // 2))
            row_max(0, 0, range(12, 14))
            mlp_down(G - 1, range(GB // 2, GB))
            row_max(0, 0, range(14, HEADS))
            transpose_h(0, 1)
            project_q(0, 1)
            pe.wait_ge(s["x_mlp"], G)
            transpose_max(0, 0)
            project_v(0, 1, 0)
            project_v(0, 1, 1)
            project_k(0, 2, 0)
            project_k(0, 2, 1)
            pe.wait_ge(s2["ones_in"], 16 * RB)
            for par in range(RB):
                step(0, par, first=par == 0)
            with pe.Fori(1, ROUNDS) as t:
                for par in range(RB):
                    step(t, par)
            for par in range(RB):
                step(ROUNDS, par)
            step(ROUNDS + 1, 0, following=1)
            step(ROUNDS + 1, 1, following=0)
            for q in (SLOTS - 2, SLOTS - 1):
                weighted_values(ROUNDS + 1, 1, q)
            half_expert(0, 0, 0, 0)
            transpose_o(ROUNDS + 1, 1)
            half_expert(0, 0, 1, 0)
            transpose_on(ROUNDS + 1, 1)
            half_expert(0, 0, 0, 1)
            project_out(ROUNDS + 1, 1)
            half_expert(0, 0, 1, 1)

            experts(0, True)
            with pe.Fori(1, G - 1) as g:
                experts(g, True)
            experts(G - 1, False)

        @block.scalar
        def _(act):
            act.dma_start(ident[:], io["ident"]).then_inc(s["c_in"], 16)
            for n, name in enumerate(("L0_attn_norm1_w", "L0_attn_norm2_w", "L0_attn_alpha_logit")):
                act.dma_start(pcol[:, n, :], io[name]).then_inc(s["c_in"], 16)
            act.wait_ge(s["c_in"], 16 * 4)
            nc.scalar.activation(pcol[:, 3, :], pcol[:, 2, :], ACT.Tanh, scale=0.5).then_inc(s["alpha_t"], 1)

            def high_weights(k):
                act.wait_ge(s[f"stage{k % STAGES}"], 16 * (k // STAGES + 1))
                (hi, _), norm = pieces[k][1:]
                if norm is None:
                    last = nc.scalar.copy(hi, stage[:, k % STAGES])
                else:
                    for c in range(DC):
                        last = nc.scalar.activation(hi[:, c], stage[:, k % STAGES, c], ACT.Copy, scale=pcol[:, norm, c:c + 1])
                last.then_inc(s["w_hi"], 1)

            def high_h1(g):
                act.wait_ge(s["ht_ps"], g + 1)
                nc.scalar.copy(hThi[:], psum[:, 2:4, 0:GT]).then_inc(s["ht_hi"], 1)

            def copy_q1(g):
                act.wait_ge(s["q_ps"], g + 1)
                nc.scalar.copy(qT[:], psum[:, 2:4, 0:GT]).then_inc(s["q_sb"], 1)

            def high_h2(p):
                act.wait_ge(s["h2t_ps"], p + 1)
                nc.scalar.copy(h2Thi[:], psum[:, 4:6, 0:GT]).then_inc(s["h2t_hi"], 1)

            def silu1(p, m, alone=False):
                act.wait_ge(s["g_ps"], FC * p + m + 1)
                if m >= 2:
                    act.wait_ge(s["hid"], FC * p + m - 1)
                nc.scalar.activation(sg[:, m % 2], bank[mlp_bank(m, alone)][:, 0:GT], ACT.Silu).then_inc(s["silu"], 1)

            def high_hidden1(p, m):
                act.wait_ge(s["hid"], FC * p + m + 1)
                nc.scalar.copy(hidhi[:, m], hid[:, m % 2]).then_inc(s["hid_hi"], 1)

            def scale_values(g):
                act.wait_ge(s["vt_ps"], g + 1)
                for j in range(GB):
                    last = nc.scalar.activation(vt[:, j], bank[4 + j // 2][0:T, cols(j % 2, D)], ACT.Copy, scale=small[:, 1, j:j + 1])
                last.then_inc(s["vt_sb"], 1)

            def squares(g):
                act.wait_ge(s["x1_sb"], g + 1)
                for j in range(GB):
                    last = nc.scalar.activation(h2n[:, j], x1[:, j], ACT.Square, accum_out=small[:, 5, j:j + 1])
                last.then_inc(s["x1_sq"], 1)

            def scale_keys(g):
                act.wait_ge(s["k_ps"], g + 1)
                for j in range(GB):
                    last = nc.scalar.activation(kt[:, j], bank[4 + j // 2][0:T, cols(j % 2, D)], ACT.Square, accum_out=small[:, 2, j:j + 1])
                last.then_inc(s["ksq"], 1)
                copy_q1(g)
                act.wait_ge(s["kscale"], g + 1)
                act.wait_ge(s["ksq"], g + 1)
                for j in range(GB):
                    last = nc.scalar.activation(kt[:, j], bank[4 + j // 2][0:T, cols(j % 2, D)], ACT.Copy, scale=small[:, 4, j:j + 1])
                last.then_inc(s["kt_sb"], 1)

            def high_context(t, par):
                f = t * RB + par
                act.wait_ge(s2["ctx_in"], 16 * (f + 1))
                if not is_row(f, 0):
                    act.wait_ge(s2["v_ps"], f)
                nc.scalar.copy(chi[:, :, 0:S2], ctxT[:]).then_inc(s2["c_hi"], 1)

            def beta_tanh(g):
                act.wait_ge(s["blog"], GB * (g + 1))
                nc.scalar.activation(small[:, 0], blogit[:], ACT.Tanh, bias=betab[:, 1:2], scale=0.5).then_inc(s["tanh_b"], 1)

            def step(g, mlp=True, ahead=True):
                p = g - 1
                act.wait_ge(s["kT_ps"], g + 1)
                nc.scalar.copy(kT[:], psum[:, 2:4, 0:GT]).then_inc(s["kT_sb"], 1)
                if mlp:
                    squares(p)
                act.wait_ge(s["v_ps"], DC * (g + 1))
                for m in range(DC):
                    last = nc.scalar.activation(va[:, m], bank[m][:, 0:GT], ACT.Copy, scale=alpha[:, 0, m:m + 1])
                last.then_inc(s["va_sb"], 1)
                for n in range(len(LEVELS)):
                    for u in range(2):
                        act.wait_ge(s["xps"], 2 * len(LEVELS) * g + 2 * n + u + 1)
                        nc.scalar.copy(xq[:, 2 * u:2 * u + 2], bank[6 + u][0:T, 0:2 * T]).then_inc(s["xsb"], 1)
                    if n == 1:
                        scale_values(g)
                    if mlp and n == 1:
                        high_h2(p)
                    if mlp and n >= 3:
                        silu1(p, n - 3)
                        high_hidden1(p, n - 3)
                    if not mlp:
                        high_weights(READY["o"] + n)
                    if ahead and n == FC:
                        beta_tanh(g + 1)
                if mlp:
                    silu1(p, FC - 1)
                    high_hidden1(p, FC - 1)
                if not ahead:
                    for k in range(READY["down"], PIECES):
                        high_weights(k)
                act.wait_ge(s["y_ps"], g + 1)
                nc.scalar.copy(y[:].rearrange("t (u j) d -> t u (j d)", u=2), psum[0:T, 0:2, :]).then_inc(s["y_sb"], 1)
                if ahead:
                    high_h1(g + 1)
                else:
                    act.wait_ge(s2["ready"], 1)
                    high_context(0, 0)
                act.wait_ge(s["oT_ps"], g + 1)
                nc.scalar.copy(oThi[:], psum[:, 6:8, 0:GT]).then_inc(s["oT_hi"], 1)
                if ahead:
                    scale_keys(g + 1)

            for k in range(READY["v"]):
                high_weights(k)
            high_h1(0)
            high_weights(READY["v"])
            act.wait_ge(s["c_in2"], 16 * 4)
            nc.scalar.mul(betab[:, 1:2], betab[:, 0:1], 0.5).then_inc(s["setup_act"], 1)
            act.wait_ge(s["setup_act"], 1)
            beta_tanh(0)
            scale_keys(0)
            act.wait_ge(s["alpha_d"], 1)
            step(0, mlp=False)
            step(1)
            with act.Fori(2, G - 1) as g:
                step(g)
            step(G - 1, ahead=False)

            def high_k(t, par, m):
                f = t * RB + par
                act.wait_ge(s2["k_ps"], DC * f + m + 1)
                if m == 0 and not is_row(f, 0):
                    before = ahead(t, par, -1)
                    act.wait_ge(s2[f"kst{before[1]}"], filled(before[0]))
                    act.wait_ge(s2[f"qst{before[1]}"], filled(before[0]))
                nc.scalar.copy(khi[:, m], bank[DENSE[m]][:, 0:S2E]).then_inc(s2["k_hi"], 1)

            def copy_h(t, par):
                act.wait_ge(s2["hT_ps"], t * RB + par + 1)
                nc.scalar.copy(h2T[:], bank[DENSE[1]][:, 0:2 * T]).then_inc(s2["hT_sb"], 1)

            def high_q(t, par):
                act.wait_ge(s2["q_ps"], t * RB + par + 1)
                nc.scalar.copy(qhi[:], bank[DENSE[1]][:, 2 * T:4 * T]).then_inc(s2["q_hi"], 1)

            def copy_v(t, par, part):
                act.wait_ge(s2[("v01_ps", "v_ps")[part]], t * RB + par + 1)
                if part == 0:
                    nc.scalar.copy(vaug[par][:, 0:2, :, 0:HD], bank[DENSE[1]][0:KP, :].rearrange("k (c h d) -> k c h d", c=2, d=HD)).then_inc(s2["v_sb"], 1)
                else:
                    nc.scalar.copy(vaug[par][:, 2, :, 0:HD], bank[DENSE[0]][0:KP, 0:D].rearrange("k (h d) -> k h d", d=HD)).then_inc(s2["v_sb"], 1)

            def negate_max(t, par):
                act.wait_ge(s2["mt_ps"], t * RB + par + 1)
                nc.scalar.mul(negm[:], bank[5][0:HEADS, 0:T], -1.0).then_inc(s2["negm"], 1)

            def exponentials(t, par, q):
                done = SLOTS * (t * RB + par) + q
                act.wait_ge(s2["sc_ps"], done + 1)
                act.wait_ge(s2["pv_done"], done + 1)
                nc.scalar.activation(pr[q % PROBS][:].rearrange("k i q -> k (i q)"), bank[q % 3][0:KP, 0:GT], ACT.Exp, scale=1.0 / HD ** 0.5).then_inc(s2["exp"], 1)

            def copy_pv(t, par):
                p = t * RB + par
                act.wait_ge(s2["pv_done"], SLOTS * (p + 1) + PROBS)
                nc.scalar.copy(pv[:], bank[6][:, 0:GT]).then_inc(s2["pv_sb"], 1)

            def copy_on(t, par):
                act.wait_ge(s2["onT_ps"], t * RB + par + 1)
                nc.scalar.copy(onT[:], bank[DENSE[0]][:, 0:2 * T]).then_inc(s2["onT_sb"], 1)

            def high_h(g):
                act.wait_ge(s3["ht_ps"], g + 1)
                if not (isinstance(g, int) and g == 0):
                    act.wait_ge(s3["u_ps"], HPG * g)
                nc.scalar.copy(h3hi[:], psum[:, ht3_banks(g):ht3_banks(g) + 2, 0:GT]).then_inc(s3["ht_hi"], 1)

            def high_expert(k):
                n = PIECES + k
                act.wait_ge(s[f"stage{n % STAGES}"], 16 * (n // STAGES + 1))
                nc.scalar.copy(ehi[k % 3][:, k // 3], stage[:, n % STAGES]).then_inc(s3["w_hi"], 1)

            def step(t, par, first=False, following=2, context=True):
                prev, nxt, far = ahead(t, par, -1), ahead(t, par, 1), ahead(t, par, 2)
                for q in range(SLOTS):
                    exponentials(t, par, q)
                    if q == 1 and not first:
                        copy_pv(*prev)
                    if q in (1, 2) and following >= 2:
                        high_k(*far, q - 1)
                    if q == 4 and following >= 2:
                        copy_h(*far)
                    if q == 5 and not first:
                        copy_on(*prev)
                    if q == 6 and following >= 2:
                        high_q(*far)
                    if q == 8 and following >= 1:
                        negate_max(*nxt)
                    if q == 8 and following >= 2:
                        copy_v(*far, 0)
                    if q == 9 and following >= 2:
                        copy_v(*far, 1)
                    if q == 9 and context:
                        high_context(*ahead(t, par, 3))
                    if q in (3, 5, 7) and following == 0:
                        high_expert((q + 3) // 2)
                    if q == 9 and following == 0:
                        high_h(0)

            def last_mlp(m):
                silu1(G - 1, m, alone=True)
                high_hidden1(G - 1, m)

            act.nop().then_inc(s2["exp"], 3)
            squares(G - 1)
            high_k(0, 0, 0)
            high_k(0, 0, 1)
            copy_h(0, 0)
            high_h2(G - 1)
            high_q(0, 0)
            last_mlp(0)
            copy_v(0, 0, 0)
            copy_v(0, 0, 1)
            high_context(0, 1)
            for m in range(1, FC):
                last_mlp(m)
            high_k(0, 1, 0)
            high_k(0, 1, 1)
            copy_h(0, 1)
            high_q(0, 1)
            negate_max(0, 0)
            act.wait_ge(s2["ready"], 2)
            copy_v(0, 1, 0)
            copy_v(0, 1, 1)
            high_context(0, 2)
            for par in range(RB):
                step(0, par, first=par == 0)
            with act.Fori(1, ROUNDS) as t:
                for par in range(RB):
                    step(t, par)
            for par in range(RB):
                step(ROUNDS, par, context=ROUNDS * RB + par + 3 < B)
            step(ROUNDS + 1, 0, following=1, context=False)
            act.wait_ge(s2["v_ps"], B)
            high_expert(0)
            for stack in ("qst1", "kst1"):
                act.wait_ge(s2[stack], filled(ROUNDS + 1))
            high_expert(1)
            act.wait_ge(s2["sc_ps"], SLOTS * (B - 1))
            high_expert(2)
            step(ROUNDS + 1, 1, following=0, context=False)
            copy_pv(ROUNDS + 1, 1)
            copy_on(ROUNDS + 1, 1)

            def high_hidden(g, it):
                e, m = it // DC, it % DC
                act.wait_ge(s3["hid"], HPG * g + it + 1)
                if e >= 2:
                    act.wait_ge(s3["d_ps"], (NE + 1) * g + e - 1)
                nc.scalar.copy(hid3hi[:, e % 2, m], hid3[:, it % 2]).then_inc(s3["hid_hi"], 1)

            def experts(g, ahead, split=False):
                for it in range(HPG):
                    act.wait_ge(s3["g_ps"], HPG * g + it + 1)
                    if it >= 2:
                        act.wait_ge(s3["hid"], HPG * g + it - 1)
                    nc.scalar.activation(sg3[:, it % 2], bank[4 + it % 2][:, 0:GT], ACT.Silu).then_inc(s3["silu"], 1)
                    if it == 1:
                        act.wait_ge(s3["logit"], g + 1)
                        nc.scalar.activation(prob[:], logit[:], ACT.Exp, scale=-1.0).then_inc(s3["ex"], 1)
                    if it % DC == DC - 1:
                        for m in range(DC):
                            high_hidden(g, it - DC + 1 + m)
                        if split and it // DC + 2 <= NE:
                            for k in range(3):
                                high_expert(3 * (it // DC + 2) + k)
                if ahead:
                    high_h(g + 1)

            act.wait_ge(s2["x_new"], B)
            experts(0, True, split=True)
            with act.Fori(1, G - 1) as g:
                experts(g, True)
            experts(G - 1, False)

        @block.vector
        def _(dve):
            def group_stats(g, done):
                for j in range(GB):
                    nc.vector.bn_stats(out=stats[:, j], in_=x[:, bass.ds(g * GB + j, 1), :].rearrange("t a d -> t (a d)")).then_inc(done, 1)
                wait_apart(dve, done, (GB + 1) * g + GB)
                for j in range(GB):
                    last = nc.vector.bn_aggr(out=mv[:, j], in_=stats[:, j])
                last.then_inc(done, 1)
                dve.wait_ge(done, (GB + 1) * (g + 1))

            def moments1(g):
                if not (isinstance(g, int) and g == 0):
                    dve.wait_ge(s["xn1"], g)
                group_stats(g, s["bn1"])
                nc.vector.tensor_scalar(rs[:, 0, :], mv[:, :, 1], LN_EPS, None, ALU.add)
                nc.vector.tensor_scalar(rs[:, 1, :], mv[:, :, 1], 1.0 + RMS_EPS, LN_EPS * RMS_EPS, ALU.mult, ALU.add).then_inc(s["var1"], 1)

            def normalise1(g, to, scale, done):
                for j in range(GB):
                    row = x[:, bass.ds(g * GB + j, 1), :].rearrange("t a d -> t (a d)")
                    last = nc.vector.tensor_scalar(to[:, j], row, mv[:, j, 0:1], rs[:, scale, j:j + 1], ALU.subtract, ALU.mult)
                last.then_inc(s[done], 1)

            def norm_h1(g):
                dve.wait_ge(s["rs1"], g + 1)
                if not (isinstance(g, int) and g == 0):
                    dve.wait_ge(s["ht_ps"], g)
                normalise1(g, h, 1, "h1")

            def beta_logits(g):
                if not (isinstance(g, int) and g == 0):
                    dve.wait_ge(s["tanh_b"], g)
                for j in range(GB):
                    if j < 2:
                        wait_apart(dve, s["h1"], g + 1)
                    else:
                        wait_apart(dve, s["blog"], GB * g + j - 1)
                    nc.vector.tensor_tensor_reduce(out=bjunk[:, j % 2], in0=h[:, j], in1=wbeta[:], scale=1.0, scalar=0.0,
                                                   op0=ALU.mult, op1=ALU.add, accum_out=blogit[:, j:j + 1]).then_inc(s["blog"], 1)

            def norm_xn(g):
                if not (isinstance(g, int) and g == 0):
                    dve.wait_ge(s["x1_sb"], g)
                normalise1(g, xn, 0, "xn1")

            def low_weights(k):
                dve.wait_ge(s["w_hi"], k + 1)
                (hi, lo), norm = pieces[k][1:]
                raw = stage[:, k % STAGES]
                if norm is None:
                    last = nc.vector.tensor_tensor(lo, raw, hi.bitcast(F32), op=ALU.subtract)
                else:
                    for c in range(DC):
                        last = nc.vector.scalar_tensor_tensor(out=lo[:, c], in0=raw[:, c], scalar=pcol[:, norm, c:c + 1], in1=hi[:, c].bitcast(F32), op0=ALU.mult, op1=ALU.subtract)
                last.then_inc(s["w_lo"], 1)

            def low_h1(g):
                dve.wait_ge(s["ht_hi"], g + 1)
                nc.vector.tensor_tensor(hTlo[:], psum[:, 2:4, 0:GT], hThi[:].bitcast(F32), op=ALU.subtract).then_inc(s["ht_lo"], 1)

            def norm_h2(g):
                dve.wait_ge(s["x1_sb"], g + 1)
                dve.wait_ge(s["rms"], g + 1)
                for j in range(GB):
                    last = nc.vector.tensor_scalar(h2n[:, j], x1[:, j], small[:, 5, j:j + 1], None, ALU.mult)
                last.then_inc(s["h2_sb"], 1)

            def low_h2(p):
                dve.wait_ge(s["h2t_hi"], p + 1)
                nc.vector.tensor_tensor(h2Tlo[:], psum[:, 4:6, 0:GT], h2Thi[:].bitcast(F32), op=ALU.subtract).then_inc(s["h2t_lo"], 1)

            def hidden1(p, m, alone=False):
                dve.wait_ge(s["silu"], FC * p + m + 1)
                dve.wait_ge(s["u_ps"], FC * p + m + 1)
                if m >= 2:
                    dve.wait_ge(s["hid_lo"], FC * p + m - 1)
                nc.vector.tensor_tensor(hid[:, m % 2], sg[:, m % 2], bank[mlp_bank(m, alone) + 1][:, 0:GT], op=ALU.mult).then_inc(s["hid"], 1)

            def low_hidden1(p, m):
                dve.wait_ge(s["hid_hi"], FC * p + m + 1)
                nc.vector.tensor_tensor(hidlo[:, m], hid[:, m % 2], hidhi[:, m].bitcast(F32), op=ALU.subtract).then_inc(s["hid_lo"], 1)

            def add_mlp(p):
                dve.wait_ge(s["down_ps"], p + 1)
                dve.wait_ge(s["x_plus"], p + 1)
                for u in range(2):
                    rows = x[:, bass.ds(p * GB + 2 * u, 2), :]
                    last = nc.vector.tensor_tensor(rows, rows, bank[4 + u][0:T, 0:2 * D].rearrange("t (j d) -> t j d", j=2), op=ALU.add)
                last.then_inc(s["x_mlp"], 1)

            def low_context(t, par):
                dve.wait_ge(s2["c_hi"], t * RB + par + 1)
                nc.vector.tensor_tensor(clo[:, :, 0:S2], ctxT[:], chi[:, :, 0:S2].bitcast(F32), op=ALU.subtract).then_inc(s2["c_lo"], 1)

            def step(g, mlp=True, ahead=True):
                p = g - 1
                NL = len(LEVELS)
                dve.wait_ge(s["gram_ps"], g + 1)
                gram = bank[4][0:T, 0:GT].rearrange("s (j t) -> s j t", j=GB)
                eye = ident[0:T, 0:T].unsqueeze(1).broadcast_to([T, GB, T])
                nc.vector.tensor_tensor(negT[:], gram, over_rows(M_SUNEG), op=ALU.mult).then_inc(s["negs"], 1)
                nc.vector.tensor_tensor(tri[:], gram, over_rows(M_B1), op=ALU.mult)
                nc.vector.tensor_tensor(triT[:], gram, over_rows(M_BT), op=ALU.mult).then_inc(s["tri0a"], 1)
                dve.wait_ge(s["tri0a"], g + 1)
                nc.vector.tensor_tensor(tri[:], eye, tri[:], op=ALU.subtract)
                nc.vector.tensor_tensor(triT[:], eye, triT[:], op=ALU.subtract).then_inc(s["tri0"], 1)
                dve.wait_ge(s["tri0"], g + 1)
                dve.wait_ge(s["aq_ps"], g + 1)
                nc.vector.tensor_tensor(aT[:], bank[5][0:T, 0:GT].rearrange("s (j t) -> s j t", j=GB), over_rows(M_LE), op=ALU.mult).then_inc(s["aT_sb"], 1)
                dve.wait_ge(s["va_sb"], g + 1)
                for c in range(DC):
                    last = nc.vector.tensor_tensor_scan(vs[:, c], decay[:, c], va[:, c], 0.0, ALU.mult, ALU.add)
                last.then_inc(s["v_scan"], 1)
                if mlp:
                    norm_h2(p)
                for n in range(NL):
                    for u in range(2):
                        it = 2 * n + u
                        rows = slice(2 * u, 2 * u + 2)
                        if n < NL - 1:
                            dve.wait_ge(s["tps_t"], 2 * (NL - 1) * g + it + 1)
                            if n > 0:
                                dve.wait_ge(s["tri_up"], 2 * (NL - 1) * g + it - 1)
                            nc.vector.tensor_tensor(tri[:, rows], tri[:, rows], bank[u][0:T, 0:2 * T].rearrange("s (j t) -> s j t", j=2), op=ALU.add).then_inc(s["tri_up"], 1)
                        dve.wait_ge(s["tps_tt"], 2 * NL * g + it + 1)
                        if n > 0:
                            dve.wait_ge(s["triT_up"], 2 * NL * g + it - 1)
                        nc.vector.tensor_tensor(triT[:, rows], triT[:, rows], bank[2 + u][0:T, 0:2 * T].rearrange("s (j t) -> s j t", j=2), op=ALU.add).then_inc(s["triT_up"], 1)
                    if mlp and n == 1:
                        low_h2(p)
                    if mlp and n >= 3:
                        hidden1(p, n - 3)
                        low_hidden1(p, n - 3)
                    if not mlp:
                        low_weights(READY["o"] + n)
                    if ahead and n == 0:
                        moments1(g + 1)
                    if ahead and n == 2:
                        norm_h1(g + 1)
                    if ahead and n == 3:
                        beta_logits(g + 1)
                if mlp:
                    hidden1(p, FC - 1)
                    low_hidden1(p, FC - 1)
                if ahead:
                    low_h1(g + 1)
                    if mlp:
                        add_mlp(p)
                else:
                    for k in range(READY["down"], PIECES):
                        low_weights(k)
                    low_context(0, 0)
                dve.wait_ge(s["oT_hi"], g + 1)
                nc.vector.tensor_tensor(oTlo[:], psum[:, 6:8, 0:GT], oThi[:].bitcast(F32), op=ALU.subtract).then_inc(s["oT_lo"], 1)
                if not ahead:
                    add_mlp(p)
                dve.wait_ge(s["wo_ps"], g + 1)
                dve.wait_ge(s["xn1"], g + 1)
                for u in range(2):
                    last = nc.vector.tensor_tensor(x1[:, 2 * u:2 * u + 2], xn[:, 2 * u:2 * u + 2], bank[6 + u][0:T, 0:2 * D].rearrange("t (j d) -> t j d", j=2), op=ALU.add)
                last.then_inc(s["x1_sb"], 1)
                if ahead:
                    norm_xn(g + 1)

            assert READY["o"] + len(LEVELS) == READY["down"]
            dve.wait_ge(s["x_in0"], 16)
            moments1(0)
            norm_h1(0)
            for k in range(READY["v"]):
                low_weights(k)
            low_h1(0)
            dve.wait_ge(s["c_in2"], 16 * 4)
            nc.vector.tensor_tensor(wbeta[:], wbeta[:], bjunk[:, 0], op=ALU.mult).then_inc(s["setup_dve"], 1)
            wait_apart(dve, s["setup_dve"], 1)
            beta_logits(0)
            dve.wait_ge(s["alpha_t"], 1)
            nc.vector.tensor_scalar(alpha[:, 0], pcol[:, 3], 0.5, 0.5, ALU.mult, ALU.add)
            nc.vector.tensor_scalar(alpha[:, 1], pcol[:, 3], -0.5, 0.5, ALU.mult, ALU.add).then_inc(s["alpha_d"], 1)
            norm_xn(0)
            low_weights(READY["v"])
            dve.wait_ge(s["masks_in"], 16 * 2)
            dve.wait_ge(s["alpha_d"], 1)
            for c in range(DC):
                last = nc.vector.tensor_scalar(decay[:, c], keep[:], alpha[:, 1, c:c + 1], None, ALU.mult)
            last.then_inc(s["alpha_d"], 1)
            dve.wait_ge(s["alpha_d"], 2)
            dve.wait_ge(s["x_in"], 16 * (G - 1))
            step(0, mlp=False)
            with dve.Fori(1, G - 1) as g:
                step(g)
            step(G - 1, ahead=False)

            def x_row(b):
                return x[:, bass.ds(b, 1), :].rearrange("t a d -> t (a d)")

            def normalise(t, par):
                b = t * RB + par
                nc.vector.bn_stats(out=stats[:, 0], in_=x_row(b)).then_inc(s2["bn"], 1)
                wait_apart(dve, s2["bn"], 2 * b + 1)
                nc.vector.bn_aggr(out=mv[:, 0], in_=stats[:, 0]).then_inc(s2["bn"], 1)
                dve.wait_ge(s2["bn"], 2 * b + 2)
                nc.vector.tensor_scalar(rs[:, 0, 0:1], mv[:, 0, 1:2], LN_EPS, None, ALU.add).then_inc(s2["stat"], 1)
                dve.wait_ge(s2["rs"], b + 1)
                if not is_row(b, 0):
                    dve.wait_ge(s2["hT_ps"], b)
                nc.vector.tensor_scalar(h2[:], x_row(b), mv[:, 0, 0:1], rs[:, 0, 0:1], ALU.subtract, ALU.mult).then_inc(s2["h"], 1)

            def low_k(t, par, m):
                dve.wait_ge(s2["k_hi"], DC * (t * RB + par) + m + 1)
                nc.vector.tensor_tensor(klo[:, m], bank[DENSE[m]][:, 0:S2E], khi[:, m].bitcast(F32), op=ALU.subtract).then_inc(s2["k_lo"], 1)

            def low_q(t, par):
                dve.wait_ge(s2["q_hi"], t * RB + par + 1)
                nc.vector.tensor_tensor(qlo[:], bank[DENSE[1]][:, 2 * T:4 * T].rearrange("p (m q) -> p m q", m=DC), qhi[:].bitcast(F32), op=ALU.subtract).then_inc(s2["q_lo"], 1)

            def maxima(t, par, heads):
                n = t * RB + par
                for hd in heads:
                    if hd == 0:
                        dve.wait_ge(s2["flags"], n + 1)
                    if hd >= 2:
                        dve.wait_ge(s2["smax"], HEADS * n + hd - 1)
                    wait_apart(dve, s2["max_ps"], HEADS * n + hd + 1)
                    nc.vector.tensor_tensor_reduce(out=junk[:, hd % 2, :], in0=bank[max_bank(n, hd)][0:T, 0:S2], in1=biasq[:, par, :], scale=1.0, scalar=-3e38,
                                                   op0=ALU.add, op1=ALU.max, accum_out=head(smax, hd).unsqueeze(1)).then_inc(s2["smax"], 1)

            def normalise_heads(t, par):
                p = t * RB + par
                dve.wait_ge(s2["ot_ps"], p + 1)
                o = bank[DENSE[0]][0:T, :].rearrange("q (h d) -> q h d", h=HEADS)
                nc.vector.reciprocal(rden[:], o[:, :, HD:HD + 1]).then_inc(s2["rden"], 1)
                dve.wait_ge(s2["rden"], p + 1)
                nc.vector.tensor_tensor(on[:], o[:, :, 0:HD], rden[:].broadcast_to([T, HEADS, HD]), op=ALU.mult).then_inc(s2["on"], 1)

            def add_row(t, par):
                p = t * RB + par
                dve.wait_ge(s2["wo_ps"], p + 1)
                nc.vector.tensor_tensor(x_row(p), x_row(p), bank[DENSE[0]][0:T, 0:D], op=ALU.add).then_inc(s2["x_new"], 1)

            def group_moments(g):
                group_stats(g, s3["bn"])
                nc.vector.tensor_scalar(rs[:, 0, :], mv[:, :, 1], LN_EPS, None, ALU.add).then_inc(s3["stat"], 1)

            def normalise_group(g):
                dve.wait_ge(s3["rs"], g + 1)
                if not (isinstance(g, int) and g == 0):
                    dve.wait_ge(s3["ht_ps"], g)
                for j in range(GB):
                    row = x[:, bass.ds(g * GB + j, 1), :].rearrange("t a d -> t (a d)")
                    last = nc.vector.tensor_scalar(h3[:, j], row, mv[:, j, 0:1], rs[:, 0, j:j + 1], ALU.subtract, ALU.mult)
                last.then_inc(s3["h"], 1)

            def low_h(g):
                dve.wait_ge(s3["ht_hi"], g + 1)
                nc.vector.tensor_tensor(h3lo[:], psum[:, ht3_banks(g):ht3_banks(g) + 2, 0:GT], h3hi[:].bitcast(F32), op=ALU.subtract).then_inc(s3["ht_lo"], 1)

            def step(t, par, first=False, following=2, norm=True):
                prev, nxt, far = ahead(t, par, -1), ahead(t, par, 1), ahead(t, par, 2)
                for q in range(SLOTS):
                    if following >= 1 and q < HEADS // 2:
                        maxima(*nxt, (2 * q, 2 * q + 1))
                    if q in (2, 3) and following >= 2:
                        low_k(*far, q - 2)
                    if q == 4 and not first:
                        normalise_heads(*prev)
                    if q == 7 and following >= 2:
                        low_q(*far)
                    if q == 7 and not first:
                        add_row(*prev)
                if norm:
                    normalise(*ahead(t, par, 3))
                    low_context(*ahead(t, par, 3))

            def last_mlp(m):
                hidden1(G - 1, m, alone=True)
                low_hidden1(G - 1, m)

            normalise(0, 0)
            low_k(0, 0, 0)
            low_k(0, 0, 1)
            norm_h2(G - 1)
            low_h2(G - 1)
            low_q(0, 0)
            last_mlp(0)
            low_context(0, 1)
            normalise(0, 1)
            last_mlp(1)
            maxima(0, 0, range(0, 4))
            last_mlp(2)
            maxima(0, 0, range(4, 8))
            last_mlp(3)
            low_k(0, 1, 0)
            maxima(0, 0, range(8, 10))
            low_k(0, 1, 1)
            maxima(0, 0, range(10, HEADS))
            add_mlp(G - 1)
            low_q(0, 1)
            low_context(0, 2)
            dve.wait_ge(s["x_mlp"], G)
            normalise(0, 2)
            for par in range(RB):
                step(0, par, first=par == 0)
            with dve.Fori(1, ROUNDS) as t:
                for par in range(RB):
                    step(t, par)
            for par in range(RB):
                step(ROUNDS, par, norm=ROUNDS * RB + par + 3 < B)
            step(ROUNDS + 1, 0, following=1, norm=False)
            dve.wait_ge(s2["v_ps"], B)
            group_moments(0)
            normalise_group(0)
            step(ROUNDS + 1, 1, following=0, norm=False)
            low_h(0)
            normalise_heads(ROUNDS + 1, 1)
            add_row(ROUNDS + 1, 1)

            def add_gate_bias(g):
                dve.wait_ge(s3["lg_ps"], g + 1)
                nc.vector.tensor_tensor(logit[:], bank[2][0:T, 0:GB * NE].rearrange("t (j e) -> t j e", j=GB), gateb[:].unsqueeze(1).broadcast_to([T, GB, NE]), op=ALU.add).then_inc(s3["logit"], 1)

            def gates(g):
                dve.wait_ge(s3["ex"], g + 1)
                nc.vector.tensor_scalar(prob[:], prob[:], 1.0, None, ALU.add).then_inc(s3["prob"], 1)
                dve.wait_ge(s3["prob"], 2 * g + 1)
                nc.vector.reciprocal(prob[:], prob[:]).then_inc(s3["prob"], 1)
                dve.wait_ge(s3["prob"], 2 * g + 2)
                for e in range(NE):
                    mine = prob[:, :, e:e + 1]
                    if e > 0:
                        nc.vector.tensor_tensor(cmp1[:, :, e, 0:e], prob[:, :, 0:e], mine.broadcast_to([T, GB, e]), op=ALU.is_ge)
                    last = nc.vector.tensor_tensor(cmp1[:, :, e, e:NE], prob[:, :, e:NE], mine.broadcast_to([T, GB, NE - e]), op=ALU.is_gt)
                last.then_inc(s3["cmp"], 1)
                dve.wait_ge(s3["cmp"], g + 1)
                nc.vector.tensor_reduce(rank[:], cmp1[:], AX, ALU.add).then_inc(s3["rank"], 1)
                dve.wait_ge(s3["rank"], g + 1)
                nc.vector.scalar_tensor_tensor(out=gate[:], in0=rank[:], scalar=2.0, in1=prob[:], op0=ALU.is_lt, op1=ALU.mult).then_inc(s3["sel"], 1)
                dve.wait_ge(s3["sel"], g + 1)
                nc.vector.tensor_reduce(wsum[:], gate[:], AX, ALU.add).then_inc(s3["wsum"], 1)
                dve.wait_ge(s3["wsum"], 3 * g + 1)
                nc.vector.tensor_scalar(wsum[:], wsum[:], 1e-8, None, ALU.add).then_inc(s3["wsum"], 1)
                dve.wait_ge(s3["wsum"], 3 * g + 2)
                nc.vector.reciprocal(wsum[:], wsum[:]).then_inc(s3["wsum"], 1)
                dve.wait_ge(s3["wsum"], 3 * g + 3)
                nc.vector.tensor_tensor(gate[:], gate[:], wsum[:].broadcast_to([T, GB, NE]), op=ALU.mult).then_inc(s3["gate"], 1)
                dve.wait_ge(s3["gate"], g + 1)

            def hidden(g, it):
                dve.wait_ge(s3["silu"], HPG * g + it + 1)
                dve.wait_ge(s3["u_ps"], HPG * g + it + 1)
                if it >= 2:
                    dve.wait_ge(s3["hid_lo"], HPG * g + it - 1)
                nc.vector.tensor_tensor(hid3[:, it % 2], sg3[:, it % 2], bank[6 + it % 2][:, 0:GT], op=ALU.mult).then_inc(s3["hid"], 1)

            def low_hidden(g, it):
                e, m = it // DC, it % DC
                dve.wait_ge(s3["hid_hi"], HPG * g + it + 1)
                nc.vector.tensor_tensor(hid3lo[:, e % 2, m], hid3[:, it % 2], hid3hi[:, e % 2, m].bitcast(F32), op=ALU.subtract).then_inc(s3["hid_lo"], 1)

            def accumulate(g, e):
                dve.wait_ge(s3["d_ps"], (NE + 1) * g + e + 1)
                if e > 0:
                    dve.wait_ge(s3["x_new"], (NE + 1) * g + e)
                for j in range(GB):
                    row = x[:, bass.ds(g * GB + j, 1), :].rearrange("t a d -> t (a d)")
                    part = bank[down_bank(e) + j // 2][0:T, cols(j % 2, D)]
                    if e < NE:
                        last = nc.vector.scalar_tensor_tensor(out=row, in0=part, scalar=gate[:, j, e:e + 1], in1=row, op0=ALU.mult, op1=ALU.add)
                    else:
                        last = nc.vector.tensor_tensor(row, row, part, op=ALU.add)
                last.then_inc(s3["x_new"], 1)

            def experts(g, ahead):
                for it in range(HPG):
                    e, m = it // DC, it % DC
                    hidden(g, it)
                    if it == 0:
                        add_gate_bias(g)
                    if m == DC - 1:
                        for c in range(DC):
                            low_hidden(g, DC * e + c)
                        if e == 1:
                            gates(g)
                        if e >= 1:
                            accumulate(g, e - 1)
                        if ahead and e == FRONT - 1:
                            group_moments(g + 1)
                        if ahead and e == FRONT:
                            normalise_group(g + 1)
                if ahead:
                    low_h(g + 1)
                accumulate(g, NE)
                dve.wait_ge(s3["x_new"], (NE + 1) * (g + 1))

            dve.wait_ge(s2["x_new"], B)
            with dve.Fori(0, G - 1) as g:
                experts(g, True)
            experts(G - 1, False)


def kernel(**inputs):
    import concourse.bacc as bacc
    from concourse.bass_utils import run_bass_kernel_spmd

    f = {n: np.ascontiguousarray(a) for n, a in inputs.items()}
    heads_last = (2, 8, HD)

    def split_heads(w):
        return np.ascontiguousarray(w.T.reshape(D, *heads_last).transpose(0, 1, 3, 2).reshape(D, D))

    arrays = {n: f[n] for n in (
        "x", "L0_attn_norm1_w", "L0_attn_Wq", "L0_attn_Wk", "L0_attn_Wv", "L0_attn_beta_b", "L0_attn_Wo",
        "L0_attn_alpha_logit", "L0_attn_norm2_w", "L0_attn_w_gate", "L0_attn_w_up", "L0_attn_w_down", "L0_ffn_gate_b")}
    arrays["beta_row"] = f["L0_attn_beta_w"].reshape(D)
    arrays["norm1_row"] = f["L0_attn_norm1_w"].reshape(D)
    for n in ("L0_attn_norm1_w", "L0_attn_norm2_w", "L0_attn_alpha_logit"):
        arrays[n] = np.ascontiguousarray(f[n].reshape(DC, P).T)
    arrays["mask"] = f["mask_BxSxS2_ik1"]
    arrays["maskT"] = np.ascontiguousarray(f["mask_BxSxS2_ik1"].transpose(0, 2, 1))
    arrays["ctxT"] = np.ascontiguousarray(f["ctx_1024"].transpose(0, 2, 1))
    arrays["xwq"] = split_heads(f["L0_xattn_wq"])
    arrays["xwk"] = split_heads(f["L0_xattn_wk"])
    arrays["xwv"] = np.ascontiguousarray(f["L0_xattn_wv"].T)
    arrays["xwo"] = np.ascontiguousarray(f["L0_xattn_w_out"].T)
    arrays["router"] = np.ascontiguousarray(f["L0_ffn_gate_w"].T)
    arrays["e1"] = np.ascontiguousarray(np.concatenate([f["L0_ffn_ew1"].transpose(0, 2, 1), f["L0_ffn_fc1"].T[None]]))
    arrays["e3"] = np.ascontiguousarray(np.concatenate([f["L0_ffn_ew3"].transpose(0, 2, 1), f["L0_ffn_fc2"].T[None]]))
    arrays["e2"] = np.ascontiguousarray(np.concatenate([f["L0_ffn_ew2"].transpose(0, 2, 1), f["L0_ffn_fc3"].T[None]]))
    arrays.update(shape_constants())

    nc = bacc.Bacc("TRN2", target_bir_lowering=False, num_devices=1)
    io = {n: nc.dram_tensor(f"in_{n}", a.shape, mybir.dt.from_np(a.dtype), kind="ExternalInput").ap() for n, a in arrays.items()}
    out = nc.dram_tensor("out", (B, T, D), F32, kind="ExternalOutput").ap()
    decoder_layer(nc, io, out)
    r = run_bass_kernel_spmd(nc, [{f"in_{n}": a for n, a in arrays.items()}], core_ids=[0])
    return r.results[0]["out"]
```
